# Optimizing a Trainium2 kernel written in Bass

```python
import numpy as np
import jax
import jax.numpy as jnp

def _softmax(x, axis=-1):
    return jax.nn.softmax(x, axis=axis)

def _gelu(x):
    return jax.nn.gelu(x, approximate=True)

def _silu(x):
    return jax.nn.silu(x)

def _sigmoid(x):
    return jax.nn.sigmoid(x)

def _layernorm(x, axis=-1, eps=1e-05):
    m = jnp.mean(x, axis=axis, keepdims=True)
    v = jnp.var(x, axis=axis, keepdims=True)
    return (x - m) / jnp.sqrt(v + eps)

def _scatter_add(tgt, idx, src, axis=0):
    return tgt.at[idx].add(src)

def _segment_sum(src, seg, n):
    return jax.ops.segment_sum(src, seg, n)
kernel_name = 'mk_perceiver_d1_seqx_r4_da9029'

def setup_inputs(seed: int=0):
    np.random.seed(seed)
    _w = jnp.asarray

    def _rec_inputs():
        import jax
        import jax.numpy as jnp
        _rk = jax.random.key(seed)
        x = 7.22e-05 + 1 * jax.random.normal(jax.random.fold_in(_rk, 1), (64, 32, 256), jnp.float32)
        _lenS = 32 - jax.random.randint(jax.random.fold_in(_rk, 7), (64,), 0, max(1, 32 // 4) + 1, jnp.int32)
        _lenS2 = 257 - jax.random.randint(jax.random.fold_in(_rk, 8), (64,), 0, max(1, 257 // 4) + 1, jnp.int32)
        _ctx_1024P = jax.random.normal(jax.random.fold_in(_rk, 11), (64, 16, 256), jnp.float32)
        _ctx_1024c = jax.random.dirichlet(jax.random.fold_in(_rk, 511), 0.3 * jnp.ones((16,), jnp.float32), (64, 257))
        _ctx_1024t = jnp.einsum('bsk,bkd->bsd', _ctx_1024c, _ctx_1024P)
        _ctx_1024t = _ctx_1024t * jax.lax.rsqrt(jnp.mean(jnp.square(_ctx_1024t)) + 1e-12) * 0.953939
        ctx_1024 = 4.13588e-05 + 0.999923 * (_ctx_1024t + 0.3 * jax.random.normal(jax.random.fold_in(_rk, 611), (64, 257, 256), jnp.float32))
        return (x, ctx_1024)
    x, ctx_1024 = _rec_inputs()

    def _L0_xattn_setup():
        import jax, jax.numpy as jnp
        import numpy as np
        B, S, D, H, DK = (4, 512, 256, 16, 64)

        def _proj(x, W, b):
            y = jnp.einsum('bsd,ed->bse', x, W) + b
            return y.reshape(x.shape[0], x.shape[1], H, DK).transpose(0, 2, 1, 3)
        key = jax.random.key(seed)
        ks = jax.random.split(key, 10)
        scale = 1.0 / np.sqrt(D)
        return {'input_Q': jax.random.normal(ks[0], (B, S, D), jnp.float32), 'input_K': jax.random.normal(ks[1], (B, S, D), jnp.float32), 'input_V': jax.random.normal(ks[2], (B, S, D), jnp.float32), 'Wq': jax.random.normal(ks[3], (H * DK, D), jnp.float32) * scale, 'bq': jax.random.normal(ks[4], (H * DK,), jnp.float32) * scale, 'Wk': jax.random.normal(ks[5], (H * DK, D), jnp.float32) * scale, 'bk': jax.random.normal(ks[6], (H * DK,), jnp.float32) * scale, 'Wv': jax.random.normal(ks[7], (H * DK, D), jnp.float32) * scale, 'bv': jax.random.normal(ks[8], (H * DK,), jnp.float32) * scale, 'Wo': jax.random.normal(ks[9], (D, H * DK), jnp.float32) * scale}
    _L0_xattn_all = _L0_xattn_setup()
    _L0_xattn_in = {k: v for k, v in _L0_xattn_all.items() if k in ('Wq', 'bq', 'Wk', 'bk', 'Wv', 'bv', 'Wo')}
    del _L0_xattn_all

    def _L0_attn_setup():
        import jax, jax.numpy as jnp
        import numpy as np
        B, T, C = (8, 256, 256)
        EPS = 1e-05
        NEG_INF = -1e+38

        def layernorm(x, w, b):
            mu = jnp.mean(x, axis=-1, keepdims=True)
            var = jnp.var(x, axis=-1, keepdims=True)
            return (x - mu) * jax.lax.rsqrt(var + EPS) * w + b

        def wkv_scan(w, u, k, v):
            kt = jnp.swapaxes(k, 0, 1)
            vt = jnp.swapaxes(v, 0, 1)
            bsz = k.shape[0]
            a0 = jnp.zeros((bsz, C), k.dtype)
            b0 = jnp.zeros((bsz, C), k.dtype)
            p0 = jnp.full((bsz, C), NEG_INF, k.dtype)

            def step(carry, inp):
                a, b, p = carry
                kk, vv = inp
                q = jnp.maximum(p, u + kk)
                e1 = jnp.exp(p - q)
                e2 = jnp.exp(u + kk - q)
                out = (e1 * a + e2 * vv) / (e1 * b + e2)
                q2 = jnp.maximum(p + w, kk)
                f1 = jnp.exp(p + w - q2)
                f2 = jnp.exp(kk - q2)
                return ((f1 * a + f2 * vv, f1 * b + f2, q2), out)
            _, outs = jax.lax.scan(step, (a0, b0, p0), (kt, vt))
            return jnp.swapaxes(outs, 0, 1)
        key = jax.random.key(seed)
        ks = jax.random.split(key, 12)
        s = 0.02
        d = {}
        d['x'] = jax.random.normal(ks[0], (B, T, C), jnp.float32)
        d['ln1_w'] = jnp.ones((C,), jnp.float32)
        d['ln1_b'] = jnp.zeros((C,), jnp.float32)
        d['ln2_w'] = jnp.ones((C,), jnp.float32)
        d['ln2_b'] = jnp.zeros((C,), jnp.float32)
        d['Wr'] = jax.random.normal(ks[1], (C, C), jnp.float32) * s
        d['Wk'] = jax.random.normal(ks[2], (C, C), jnp.float32) * s
        d['Wv'] = jax.random.normal(ks[3], (C, C), jnp.float32) * s
        d['Wo'] = jax.random.normal(ks[4], (C, C), jnp.float32) * s
        d['decay'] = jax.random.normal(ks[5], (C,), jnp.float32) * 0.1
        d['u'] = jax.random.normal(ks[6], (C,), jnp.float32) * 0.1
        d['Wfk'] = jax.random.normal(ks[7], (4 * C, C), jnp.float32) * s
        d['Wfv'] = jax.random.normal(ks[8], (C, 4 * C), jnp.float32) * s
        d['Wfr'] = jax.random.normal(ks[9], (C, C), jnp.float32) * s
        return d
    _L0_attn_all = _L0_attn_setup()
    _L0_attn_in = {k: v for k, v in _L0_attn_all.items() if k in ('ln1_w', 'ln1_b', 'ln2_w', 'ln2_b', 'Wr', 'Wk', 'Wv', 'Wo', 'decay', 'u', 'Wfk', 'Wfv', 'Wfr')}
    del _L0_attn_all

    def _L0_ffn_setup():
        import math
        import jax, jax.numpy as jnp
        import numpy as np
        B, L, D, F_FF, E = (4, 512, 256, 1024, 8)
        TOP_K = 1
        CAPACITY_FACTOR = 1.25
        key = jax.random.key(seed)
        ks = jax.random.split(key, 4)
        h = jax.random.normal(ks[0], (B, L, D), dtype=jnp.float32)
        gate_w = jax.random.normal(ks[1], (E, D), dtype=jnp.float32) * 0.02
        gate_b = jnp.zeros((E,), dtype=jnp.float32)
        w1 = jax.random.normal(ks[2], (E, D, F_FF), dtype=jnp.float32) * 0.02
        b1 = jnp.zeros((E, F_FF), dtype=jnp.float32)
        w2 = jax.random.normal(ks[3], (E, F_FF, D), dtype=jnp.float32) * 0.02
        b2 = jnp.zeros((E, D), dtype=jnp.float32)
        return {'h': h, 'gate_w': gate_w, 'gate_b': gate_b, 'w1': w1, 'b1': b1, 'w2': w2, 'b2': b2}
    _L0_ffn_all = _L0_ffn_setup()
    _L0_ffn_in = {k: v for k, v in _L0_ffn_all.items() if k in ('gate_w', 'gate_b', 'w1', 'b1', 'w2', 'b2')}
    del _L0_ffn_all
    return {'x': x, 'ctx_1024': ctx_1024, 'L0_xattn_Wq': _L0_xattn_in['Wq'], 'L0_xattn_bq': _L0_xattn_in['bq'], 'L0_xattn_Wk': _L0_xattn_in['Wk'], 'L0_xattn_bk': _L0_xattn_in['bk'], 'L0_xattn_Wv': _L0_xattn_in['Wv'], 'L0_xattn_bv': _L0_xattn_in['bv'], 'L0_xattn_Wo': _L0_xattn_in['Wo'], 'L0_attn_ln1_w': _L0_attn_in['ln1_w'], 'L0_attn_ln1_b': _L0_attn_in['ln1_b'], 'L0_attn_ln2_w': _L0_attn_in['ln2_w'], 'L0_attn_ln2_b': _L0_attn_in['ln2_b'], 'L0_attn_Wr': _L0_attn_in['Wr'], 'L0_attn_Wk': _L0_attn_in['Wk'], 'L0_attn_Wv': _L0_attn_in['Wv'], 'L0_attn_Wo': _L0_attn_in['Wo'], 'L0_attn_decay': _L0_attn_in['decay'], 'L0_attn_u': _L0_attn_in['u'], 'L0_attn_Wfk': _L0_attn_in['Wfk'], 'L0_attn_Wfv': _L0_attn_in['Wfv'], 'L0_attn_Wfr': _L0_attn_in['Wfr'], 'L0_ffn_gate_w': _L0_ffn_in['gate_w'], 'L0_ffn_gate_b': _L0_ffn_in['gate_b'], 'L0_ffn_w1': _L0_ffn_in['w1'], 'L0_ffn_b1': _L0_ffn_in['b1'], 'L0_ffn_w2': _L0_ffn_in['w2'], 'L0_ffn_b2': _L0_ffn_in['b2']}

def reference(x, ctx_1024, L0_xattn_Wq, L0_xattn_bq, L0_xattn_Wk, L0_xattn_bk, L0_xattn_Wv, L0_xattn_bv, L0_xattn_Wo, L0_attn_ln1_w, L0_attn_ln1_b, L0_attn_ln2_w, L0_attn_ln2_b, L0_attn_Wr, L0_attn_Wk, L0_attn_Wv, L0_attn_Wo, L0_attn_decay, L0_attn_u, L0_attn_Wfk, L0_attn_Wfv, L0_attn_Wfr, L0_ffn_gate_w, L0_ffn_gate_b, L0_ffn_w1, L0_ffn_b1, L0_ffn_w2, L0_ffn_b2):
    import jax
    import jax.numpy as jnp

    def _L0_xattn_ref(input_Q, input_K, input_V, Wq, bq, Wk, bk, Wv, bv, Wo):
        import jax, jax.numpy as jnp
        import numpy as np
        B, S, D, H, DK = (4, 512, 256, 16, 64)

        def _proj(x, W, b):
            y = jnp.einsum('bsd,ed->bse', x, W) + b
            return y.reshape(x.shape[0], x.shape[1], H, DK).transpose(0, 2, 1, 3)
        Q = _proj(input_Q, Wq, bq)
        K = _proj(input_K, Wk, bk)
        V = _proj(input_V, Wv, bv)
        scores = jnp.einsum('bhqd,bhkd->bhqk', Q, K) / np.sqrt(DK).astype(np.float32)
        attn = jax.nn.softmax(scores, axis=-1)
        context = jnp.einsum('bhqk,bhkd->bhqd', attn, V)
        context = context.transpose(0, 2, 1, 3).reshape(input_Q.shape[0], -1, H * DK)
        return jnp.einsum('bse,de->bsd', context, Wo)

    def _L0_attn_ref(x, ln1_w, ln1_b, ln2_w, ln2_b, Wr, Wk, Wv, Wo, decay, u, Wfk, Wfv, Wfr):
        import jax, jax.numpy as jnp
        import numpy as np
        B, T, C = (8, 256, 256)
        EPS = 1e-05
        NEG_INF = -1e+38

        def layernorm(x, w, b):
            mu = jnp.mean(x, axis=-1, keepdims=True)
            var = jnp.var(x, axis=-1, keepdims=True)
            return (x - mu) * jax.lax.rsqrt(var + EPS) * w + b

        def wkv_scan(w, u, k, v):
            kt = jnp.swapaxes(k, 0, 1)
            vt = jnp.swapaxes(v, 0, 1)
            bsz = k.shape[0]
            a0 = jnp.zeros((bsz, C), k.dtype)
            b0 = jnp.zeros((bsz, C), k.dtype)
            p0 = jnp.full((bsz, C), NEG_INF, k.dtype)

            def step(carry, inp):
                a, b, p = carry
                kk, vv = inp
                q = jnp.maximum(p, u + kk)
                e1 = jnp.exp(p - q)
                e2 = jnp.exp(u + kk - q)
                out = (e1 * a + e2 * vv) / (e1 * b + e2)
                q2 = jnp.maximum(p + w, kk)
                f1 = jnp.exp(p + w - q2)
                f2 = jnp.exp(kk - q2)
                return ((f1 * a + f2 * vv, f1 * b + f2, q2), out)
            _, outs = jax.lax.scan(step, (a0, b0, p0), (kt, vt))
            return jnp.swapaxes(outs, 0, 1)
        xn = layernorm(x, ln1_w, ln1_b)
        r = jax.nn.sigmoid(xn @ Wr.T)
        k = xn @ Wk.T
        v = xn @ Wv.T
        w = -jnp.exp(decay)
        wkv_f = wkv_scan(w, u, k, v)
        wkv_b = jnp.flip(wkv_scan(w, u, jnp.flip(k, axis=1), jnp.flip(v, axis=1)), axis=1)
        wkv = 0.5 * (wkv_f + wkv_b)
        x = x + r * wkv @ Wo.T
        xn2 = layernorm(x, ln2_w, ln2_b)
        kk = jnp.square(jax.nn.relu(xn2 @ Wfk.T))
        x = x + jax.nn.sigmoid(xn2 @ Wfr.T) * (kk @ Wfv.T)
        return x

    def _L0_ffn_ref(h, gate_w, gate_b, w1, b1, w2, b2):
        import math
        import jax, jax.numpy as jnp
        import numpy as np
        B, L, D, F_FF, E = (4, 512, 256, 1024, 8)
        TOP_K = 1
        CAPACITY_FACTOR = 1.25
        Bh, Lh, Dh = h.shape
        T = Bh * Lh
        capacity = max(1, math.ceil(CAPACITY_FACTOR * (T * TOP_K / E)))
        x = h.reshape(T, Dh)
        logits = x @ gate_w.T + gate_b
        probs = jax.nn.softmax(logits, axis=-1)
        idx = jnp.argmax(probs, axis=-1)
        top_prob = jnp.max(probs, axis=-1)
        one_hot = jax.nn.one_hot(idx, E, dtype=jnp.int32)
        pos = jnp.take_along_axis(jnp.cumsum(one_hot, axis=0), idx[:, None], axis=1)[:, 0] - 1
        keep = pos < capacity
        safe_pos = jnp.where(keep, pos, 0)
        buf = jnp.zeros((E, capacity, Dh), dtype=x.dtype)
        buf = buf.at[idx, safe_pos].add(x * keep[:, None].astype(x.dtype))
        hdn = jax.nn.relu(jnp.einsum('ecd,edf->ecf', buf, w1) + b1[:, None, :])
        eout = jnp.einsum('ecf,efd->ecd', hdn, w2) + b2[:, None, :]
        gathered = eout[idx, safe_pos]
        out = gathered * (top_prob * keep.astype(x.dtype))[:, None]
        return out.reshape(Bh, Lh, Dh)
    x = x + _L0_xattn_ref(_layernorm(x, axis=-1), ctx_1024, ctx_1024, L0_xattn_Wq, L0_xattn_bq, L0_xattn_Wk, L0_xattn_bk, L0_xattn_Wv, L0_xattn_bv, L0_xattn_Wo)
    x = x + _L0_attn_ref(_layernorm(x, axis=-1), L0_attn_ln1_w, L0_attn_ln1_b, L0_attn_ln2_w, L0_attn_ln2_b, L0_attn_Wr, L0_attn_Wk, L0_attn_Wv, L0_attn_Wo, L0_attn_decay, L0_attn_u, L0_attn_Wfk, L0_attn_Wfv, L0_attn_Wfr)
    x = x + _L0_ffn_ref(_layernorm(x, axis=-1), L0_ffn_gate_w, L0_ffn_gate_b, L0_ffn_w1, L0_ffn_b1, L0_ffn_w2, L0_ffn_b2)
    return x

_drawn_inputs = setup_inputs


def setup_inputs(seed=0):
    import zlib

    import numpy as np

    out = dict(_drawn_inputs(seed))
    spreads = {'L0_attn_ln1_w': (1.0, 0.6),
     'L0_attn_ln1_b': (0.0, 0.8),
     'L0_attn_ln2_w': (1.0, 0.6),
     'L0_attn_ln2_b': (0.0, 0.8),
     'L0_ffn_gate_b': (0.0, 0.8),
     'L0_ffn_b1': (0.0, 0.8),
     'L0_ffn_b2': (0.0, 0.8)}
    factors = {'L0_xattn_bq': 3.06,
     'L0_xattn_bk': 8.0,
     'L0_attn_Wr': 8.0,
     'L0_attn_Wk': 8.0,
     'L0_attn_Wv': 3.262,
     'L0_attn_Wo': 3.265,
     'L0_attn_decay': 8.0,
     'L0_attn_u': 8.0,
     'L0_attn_Wfk': 3.292,
     'L0_attn_Wfv': 3.021,
     'L0_attn_Wfr': 8.0,
     'L0_ffn_gate_w': 4.319,
     'L0_ffn_w1': 6.037,
     'L0_ffn_w2': 4.863}
    for name, (base, spread) in spreads.items():
        noise = np.random.default_rng([zlib.crc32(name.encode()), seed]).standard_normal(out[name].shape)
        drawn = base * np.exp(spread * noise) if base else spread * noise
        out[name] = jnp.asarray(drawn.astype(out[name].dtype))
    for name, factor in factors.items():
        out[name] = (out[name] * factor).astype(out[name].dtype)
    return out
```

```python
from contextlib import ExitStack

import concourse.bass as bass
from concourse import mybir

F32 = mybir.dt.float32
F32R = mybir.dt.float32r
U32 = mybir.dt.uint32
ALU = mybir.AluOpType
ACT = mybir.ActivationFunctionType
AX_X = mybir.AxisListType.X

P = 128
BATCH, QLEN, D = 64, 32, 256
KEYS = 257
HEADS, DK = 16, 64
E = HEADS * DK
TOKENS = BATCH * QLEN
DT = D // P
ET = E // P
TT = TOKENS // P
NB = 8
GROUPS = BATCH // NB
GTOK = NB * QLEN
HT = HEADS * QLEN // P
TILES = NB * HT
KC = KEYS // P
KPAD = KEYS + 1
EPS = 1e-5
SCALE = DK ** -0.5



def wait(eng, sem, loop, per, count):
    value = loop * per + count
    if isinstance(value, int) and value <= 0:
        return
    eng.wait_ge(sem, value)


def turns(eng, n, body):
    body(0)
    with eng.Fori(1, n) as i:
        body(i)


def wait_alone(eng, sem, loop, per, count, passed):
    wait(eng, sem, loop, per, count)
    if not isinstance(loop, int):
        eng.sem_inc(passed, 1)


def three_pass(pe, out, w_hi, w_lo, m_hi, m_lo, first, last, **kw):
    pe.matmul(out, w_hi, m_hi, start=first, stop=False, **kw)
    pe.matmul(out, w_hi, m_lo, start=False, stop=False, **kw)
    return pe.matmul(out, w_lo, m_hi, start=False, stop=last, **kw)


def f(ap):
    return ap.bitcast(F32)


def identity(pool, ident, made):
    pool.memset(ident[:, :], 0.0).then_inc(made, 1)
    pool.wait_ge(made, 1)
    pool.affine_select(out=ident[:, :], in_=ident[:, :], compare_op=ALU.not_equal, fill=1.0, base=0,
                       pattern=[[-1, P]], channel_multiplier=1).then_inc(made, 1)


def three_zero(view):
    return view.rearrange("p d t (c k) -> p (d t) c k", k=DK)[:, :, 0:3:2, :]


def prepare(nc, A, W, dram):
    with ExitStack() as ctx:
        def sb(name, shape, dt=F32):
            return ctx.enter_context(nc.sbuf_tensor(name, shape, dt))

        def sem(name):
            return ctx.enter_context(nc.semaphore(name))

        x = sb("x_in", [P, TT, D])
        raw_wq = sb("raw_wq", [P, DT, E])
        raw_wk = sb("raw_wk", [P, ET, D])
        raw_wv = sb("raw_wv", [P, DT * ET, 2, DK])
        raw_wo = sb("raw_wo", [P, ET, D])
        wq_nat = sb("wq_nat", [P, ET, D])
        bk_col = sb("bk_col", [P, ET])
        bk_diag = sb("bk_diag", [P, ET, HEADS])
        stats = sb("ln_stats", [P, TT, 6])
        mv = sb("ln_mv", [P, TT, 2])
        veps = sb("ln_veps", [P, TT])
        power = sb("ln_power", [P, TT])
        rstd = sb("ln_rstd", [P, TT])
        xT_hi = sb("p_xT_hi", [P, 2, DT, GTOK], F32R)
        xT_lo = sb("p_xT_lo", [P, 2, DT, GTOK], F32R)
        g_hi = sb("g_hi", [P, DT, HEADS], F32R)
        g_lo = sb("g_lo", [P, DT, HEADS], F32R)
        g_raw = sb("g_raw", [P, DT, HEADS])
        c0 = sb("c0", [P, HEADS])
        c_tok = sb("c_tok", [P, TT, HEADS])
        ps_t = [ctx.enter_context(nc.psum_tensor(f"ps_t{i}", [P, DT, GTOK], F32)) for i in range(2)]
        ps_g = ctx.enter_context(nc.psum_tensor("ps_g", [P, DT, HEADS], F32))
        ps_c0 = ctx.enter_context(nc.psum_tensor("ps_c0", [P, HEADS], F32))
        ps_c = ctx.enter_context(nc.psum_tensor("ps_c", [P, TT, HEADS], F32))

        x_loaded = sem("x_loaded")
        b_loaded = sem("b_loaded")
        wq_loaded, wk_loaded, wv_loaded, wo_loaded = (sem(n + "_loaded") for n in ("wq", "wk", "wv", "wo"))
        w_hi_done = sem("w_hi_done")
        w_lo_dve = sem("w_lo_dve")
        w_lo_pool = sem("w_lo_pool")
        ident_made = sem("ident_made")
        diag_zero = sem("diag_zero")
        diag_made = sem("diag_made")
        stats_done = sem("stats_done")
        mv_done = sem("mv_done")
        power_set = sem("power_set")
        veps_done = sem("veps_done")
        rstd_done = sem("rstd_done")
        xn_done = sem("xn_done")
        xT_done = sem("xT_done")
        hi_done = sem("hi_done")
        lo_done = sem("lo_done")
        stored = [sem("stored_even"), sem("stored_odd")]
        g_done = sem("g_done")
        g_split = sem("g_split")
        c_done = sem("c_done")
        c_copied = sem("c_copied")

        with nc.Block() as block:
            @block.sync
            def _(sp):
                sp.dma_start(x[:, :, :], A["x"].rearrange("(t p) d -> p t d", p=P)).then_inc(x_loaded, 16)
                sp.dma_start(wq_nat[:, :, :], A["wq_nat"].rearrange("(t p) d -> p t d", p=P)).then_inc(b_loaded, 16)
                sp.dma_start(bk_col[:, :], A["bk"]).then_inc(b_loaded, 16)
                sp.dma_start(W["bq"][:, :], A["bq"]).then_inc(b_loaded, 16)
                sp.dma_start(W["bv"][:, :], A["bv"]).then_inc(b_loaded, 16)
                sp.dma_start(raw_wq[:, :, :], A["wqT"].rearrange("(t p) e -> p t e", p=P)).then_inc(wq_loaded, 16)
                sp.dma_start(raw_wk[:, :, :], A["wk"].rearrange("(t p) d -> p t d", p=P)).then_inc(wk_loaded, 16)
                sp.dma_start(raw_wv[:, :, :, :].rearrange("p a b c -> p (a b c)").rearrange("p (t e) -> p t e", t=DT),
                             A["wvT"].rearrange("(t p) e -> p t e", p=P)).then_inc(wv_loaded, 16)
                sp.dma_start(raw_wo[:, :, :], A["woT"].rearrange("(t p) d -> p t d", p=P)).then_inc(wo_loaded, 16)
                for g in range(GROUPS):
                    sp.wait_ge(lo_done, g + 1)
                    for name, part in (("xT_hi", xT_hi), ("xT_lo", xT_lo)):
                        sp.dma_start(dram[name][g], f(part[:, g % 2].rearrange("p a b -> p (a b)")))\
                          .then_inc(stored[g % 2], 16)
                for parity in range(2):
                    sp.wait_ge(stored[parity], 16 * GROUPS)

            @block.gpsimd
            def _(pool):
                identity(pool, W["ident"], ident_made)
                pool.memset(bk_diag[:, :, :], 0.0).then_inc(diag_zero, 1)
                pool.memset(power[:, :], -0.5).then_inc(power_set, 1)
                pool.wait_ge(power_set, 1)
                pool.wait_ge(veps_done, 1)
                pool.tensor_tensor(rstd[:, :], veps[:, :], power[:, :], ALU.pow).then_inc(rstd_done, 1)
                for part in ("wv_hi", "wv_lo"):
                    pool.memset(f(W[part][:, :, :, DK:2 * DK]), 0.0).then_inc(w_lo_pool, 1)
                pool.wait_ge(w_hi_done, 3)
                pool.tensor_tensor(three_zero(W["wv_lo"][:, :, :, :]), raw_wv[:, :, :, :],
                                   f(three_zero(W["wv_hi"][:, :, :, :])), ALU.subtract).then_inc(w_lo_pool, 1)
                pool.wait_ge(w_hi_done, 4)
                pool.tensor_tensor(W["wo_lo"][:, :, :], raw_wo[:, :, :], f(W["wo_hi"][:, :, :]),
                                   ALU.subtract).then_inc(w_lo_pool, 1)

            @block.vector
            def _(dve):
                dve.wait_ge(b_loaded, 64)
                dve.wait_ge(diag_zero, 1)
                flat = bk_diag[:, :, :].rearrange("p t h -> p (t h)")
                step = HEADS + 2
                dve.tensor_copy(flat[0:DK, 0:(ET - 1) * step + 1:step], bk_col[0:DK, :]).then_inc(diag_made, 1)
                dve.tensor_copy(flat[DK:P, 1:(ET - 1) * step + 2:step], bk_col[DK:P, :]).then_inc(diag_made, 1)
                dve.wait_ge(x_loaded, 16)
                for t in range(TT):
                    dve.bn_stats(stats[:, t, :], x[:, t, :]).then_inc(stats_done, 1)
                for t in range(TT):
                    dve.wait_ge(stats_done, t + 1)
                    dve.bn_aggr(mv[:, t, :], stats[:, t, :]).then_inc(mv_done, 1)
                dve.wait_ge(mv_done, TT)
                dve.tensor_scalar(veps[:, :], mv[:, :, 1], EPS, None, ALU.add).then_inc(veps_done, 1)
                dve.wait_ge(rstd_done, 1)
                for t in range(TT):
                    dve.tensor_scalar(x[:, t, :], x[:, t, :], mv[:, t, 0:1], rstd[:, t:t + 1],
                                      ALU.subtract, ALU.mult).then_inc(xn_done, 1)
                dve.wait_ge(g_done, 1)
                dve.tensor_copy(g_raw[:, :, :], ps_g[:, :, :]).then_inc(g_split, 1)
                dve.tensor_copy(c0[:, :], ps_c0[:, :]).then_inc(g_split, 1)
                dve.wait_ge(g_split, 2)
                dve.tensor_copy(g_hi[:, :, :], g_raw[:, :, :]).then_inc(g_split, 1)
                dve.wait_ge(g_split, 3)
                dve.tensor_tensor(g_lo[:, :, :], g_raw[:, :, :], f(g_hi[:, :, :]), ALU.subtract).then_inc(g_split, 1)
                for g in range(GROUPS):
                    dve.wait_ge(hi_done, g + 1)
                    if g >= 2:
                        dve.wait_ge(stored[g % 2], 32 * (g // 2))
                        dve.wait_ge(c_done, g - 1)
                    dve.tensor_tensor(xT_lo[:, g % 2], ps_t[g % 2][:, :, :], f(xT_hi[:, g % 2]),
                                      ALU.subtract).then_inc(lo_done, 1)
                dve.wait_ge(c_done, GROUPS)
                for t in range(TT):
                    dve.tensor_tensor(c_tok[:, t, :], ps_c[:, t, :], c0[:, :], ALU.add).then_inc(c_copied, 1)
                dve.wait_ge(c_copied, TT)
                dve.tensor_scalar(c_tok[:, :, :], c_tok[:, :, :], SCALE, None, ALU.mult).then_inc(c_copied, 1)
                dve.wait_ge(c_copied, TT + 1)
                for b in range(4):
                    for h in range(4):
                        src = c_tok[32 * b:32 * b + 32, :, :].rearrange("q t (a h) -> q t a h", h=4)[:, :, :, h]
                        dst = W["cmap"][32 * h:32 * h + 32, :].rearrange("q (t b a) -> q t b a", b=4, a=HT)[:, :, b, :]
                        dve.tensor_copy(dst, src).then_inc(c_copied, 1)
                dve.wait_ge(w_hi_done, 1)
                dve.tensor_tensor(W["wq_lo"][:, :, :], raw_wq[:, :, :], f(W["wq_hi"][:, :, :]),
                                  ALU.subtract).then_inc(w_lo_dve, 1)
                dve.wait_ge(w_hi_done, 2)
                dve.tensor_tensor(W["wk_lo"][:, :, :], raw_wk[:, :, :], f(W["wk_hi"][:, :, :]),
                                  ALU.subtract).then_inc(w_lo_dve, 1)

            @block.scalar
            def _(act):
                for g in range(GROUPS):
                    act.wait_ge(xT_done, g + 1)
                    if g >= 2:
                        act.wait_ge(stored[g % 2], 32 * (g // 2))
                        act.wait_ge(c_done, g - 1)
                    act.activation(xT_hi[:, g % 2], ps_t[g % 2][:, :, :], ACT.Copy).then_inc(hi_done, 1)
                act.wait_ge(wq_loaded, 16)
                act.activation(W["wq_hi"][:, :, :], raw_wq[:, :, :], ACT.Copy).then_inc(w_hi_done, 1)
                act.wait_ge(wk_loaded, 16)
                act.activation(W["wk_hi"][:, :, :], raw_wk[:, :, :], ACT.Copy).then_inc(w_hi_done, 1)
                act.wait_ge(wv_loaded, 16)
                act.activation(three_zero(W["wv_hi"][:, :, :, :]), raw_wv[:, :, :, :], ACT.Copy).then_inc(w_hi_done, 1)
                act.wait_ge(wo_loaded, 16)
                act.activation(W["wo_hi"][:, :, :], raw_wo[:, :, :], ACT.Copy).then_inc(w_hi_done, 1)

            @block.tensor
            def _(pe):
                pe.wait_ge(b_loaded, 64)
                pe.wait_ge(diag_made, 2)
                for d in range(DT):
                    for i in range(ET):
                        pe.matmul(ps_g[:, d, :], wq_nat[:, i, d * P:(d + 1) * P], bk_diag[:, i, :],
                                  start=(i == 0), stop=(i == ET - 1))
                for i in range(ET):
                    mm = pe.matmul(ps_c0[:, :], W["bq"][:, i:i + 1].to_broadcast([P, P]), bk_diag[:, i, :],
                                   start=(i == 0), stop=(i == ET - 1))
                mm.then_inc(g_done, 1)

                def q_dot_bk(g):
                    pe.wait_ge(lo_done, g + 1)
                    if g == 0:
                        pe.wait_ge(g_split, 4)
                    for half in range(2):
                        cols = slice(half * P, (half + 1) * P)
                        for d in range(DT):
                            mm = three_pass(pe, ps_c[:, 2 * g + half, :], xT_hi[:, g % 2, d, cols],
                                            xT_lo[:, g % 2, d, cols], g_hi[:, d, :], g_lo[:, d, :],
                                            d == 0, d == DT - 1)
                    mm.then_inc(c_done, 1)

                pe.wait_ge(ident_made, 2)
                for g in range(GROUPS):
                    pe.wait_ge(xn_done, 2 * g + 2)
                    for half in range(2):
                        for d in range(DT):
                            mm = pe.transpose(ps_t[g % 2][:, d, half * P:(half + 1) * P],
                                              x[:, 2 * g + half, d * P:(d + 1) * P], W["ident"][:, :])
                    mm.then_inc(xT_done, 1)
                    if g >= 1:
                        q_dot_bk(g - 1)
                q_dot_bk(GROUPS - 1)


T_LAG = 3
PV_PARTS = 4
PV_LAG = 9
ROUND_T, REST_T = 0, 1
ROUND_N, REST_N = 6, 7
P_HI, P_LO = (5, 7), (6, 8)
Z_HI, Z_LO = (10, 12), (11, 13)
STEPS = TILES - HT + Z_LO[1] + 1
RING = 8


def due(s, lag):
    b, t = divmod(s - lag, HT)
    return [b] if t == 0 and 0 <= b < NB else []


def both_due(s, lags):
    return [(b, part) for part in range(2) for b in due(s, lags[part])]


def attention(nc, A, W, dram):
    with ExitStack() as ctx:
        def sb(name, shape, dt=F32):
            return ctx.enter_context(nc.sbuf_tensor(name, shape, dt))

        def sem(name):
            return ctx.enter_context(nc.semaphore(name))

        xT_hi = sb("xT_hi", [P, DT, GTOK], F32R)
        xT_lo = sb("xT_lo", [P, DT, GTOK], F32R)
        cg = sb("cg", [P, TILES])
        e_hi = [sb(f"e_hi{i}", [P, GTOK], F32R) for i in range(3)]
        e_lo = [sb(f"e_lo{i}", [P, GTOK], F32R) for i in range(3)]
        qk_hi = sb("qk_hi", [P, DT, NB, HEADS * QLEN], F32R)
        qk_lo = sb("qk_lo", [P, DT, NB, HEADS * QLEN], F32R)
        raw_T = [sb(f"raw_T{i}", [P, DT, KPAD]) for i in range(2)]
        raw_N = [sb(f"raw_N{i}", [P, KC, D]) for i in range(2)]
        raw_L = [sb(f"raw_L{i}", [96, D]) for i in range(2)]
        ctxT_hi = [sb(f"ctxT_hi{i}", [P, DT, KPAD], F32R) for i in range(2)]
        ctxT_lo = [sb(f"ctxT_lo{i}", [P, DT, KPAD], F32R) for i in range(2)]
        ctxN_hi = [sb(f"ctxN_hi{i}", [P, KC, D], F32R) for i in range(2)]
        ctxN_lo = [sb(f"ctxN_lo{i}", [P, KC, D], F32R) for i in range(2)]
        ctxL = [sb(f"ctxL{i}", [96, D], F32R) for i in range(2)]
        probs = sb("probs", [P, RING, KEYS])
        pT_hi = [sb(f"pT_hi{i}", [P, KC, HEADS * QLEN], F32R) for i in range(2)]
        pT_lo = [sb(f"pT_lo{i}", [P, KC, HEADS * QLEN], F32R) for i in range(2)]
        pL = [sb(f"pL{i}", [96, HEADS * QLEN], F32R) for i in range(2)]
        mx = sb("mx", [P, TILES])
        mc = sb("mc", [P, TILES])
        neg = sb("neg", [P, TILES])
        total = sb("total", [P, TILES])
        rec = sb("rec", [P, TILES])
        y = sb("y", [P, 2, D])

        ps_s = [ctx.enter_context(nc.psum_tensor(f"ps_s{i}", [P, 512], F32)) for i in range(2)]
        ps_p = [ctx.enter_context(nc.psum_tensor(f"ps_p{i}", [P, KC, 2 * P], F32)) for i in range(2)]
        ps_l = ctx.enter_context(nc.psum_tensor("ps_l", [P, HEADS * QLEN], F32))
        ps_z = [ctx.enter_context(nc.psum_tensor(f"ps_z{i}", [P, 512], F32)) for i in range(2)]
        ps_x = ctx.enter_context(nc.psum_tensor("ps_x", [P, 2, D], F32))
        ps_x_flat = ps_x[:, :, :].rearrange("p a b -> p (a b)")
        qk_banks = [ps_z[0][:, :], ps_z[1][:, :], ps_x_flat]
        score_banks = [ps_s[0][:, :], ps_s[1][:, :], ps_x_flat]

        pads_zero = sem("pads_zero")
        passed = {n: sem("passed_" + n) for n in ("sp", "pool")}
        xT_in = sem("xT_in")
        rawT_in = [sem("rawT_in_even"), sem("rawT_in_odd")]
        rawN_in = [sem("rawN_in_even"), sem("rawN_in_odd")]
        ctxT_hi_done, ctxN_hi_done, ctxL_hi_done = (sem(f"ctx{n}_hi_done") for n in "TNL")
        ctxT_split, ctxN_split, ctxL_split = (sem(f"ctx{n}_split") for n in "TNL")
        cg_ready = sem("cg_ready")
        q_done, q_hi, q_lo = sem("q_done"), sem("q_hi"), sem("q_lo")
        qk_done, qk_hi_done, qk_lo_done = sem("qk_done"), sem("qk_hi_done"), sem("qk_lo_done")
        sc_done = sem("sc_done")
        max_done = sem("max_done")
        mc_done = sem("mc_done")
        neg_done = sem("neg_done")
        exp_done = sem("exp_done")
        rec_done = sem("rec_done")
        norm_done = sem("norm_done")
        tp_done = sem("tp_done")
        tpL_done = sem("tpL_done")
        pT_hi_done, pT_lo_done = sem("pT_hi_done"), sem("pT_lo_done")
        z_done, z_hi, z_lo = sem("z_done"), sem("z_hi"), sem("z_lo")
        o_done, o_hi, o_lo = sem("o_done"), sem("o_hi"), sem("o_lo")
        wo_done = sem("wo_done")
        y_copied = sem("y_copied")
        y_stored = sem("y_stored")

        ctxT_dram, ctxN_dram, ctxL_dram = A["ctxT"], A["ctxN"], A["ctxL"]

        def groups(eng, body):
            body(0)
            with eng.Fori(1, GROUPS - 1) as g:
                body(g)
            body(GROUPS - 1)

        with nc.Block() as block:
            @block.sync
            def _(sp):
                def load_T(b, i):
                    sp.dma_start(raw_T[i][:, :, 0:KEYS], ctxT_dram[b]).then_inc(rawT_in[i], 16)

                def load_N(b, i):
                    sp.dma_start(raw_N[i][:, :, :], ctxN_dram[b]).then_inc(rawN_in[i], 16)
                    sp.dma_start(raw_L[i][0:65:32, :], ctxL_dram[b].to_broadcast([3, D])).then_inc(rawN_in[i], 16)

                def load_x(g):
                    sp.dma_start(f(xT_hi[:, :, :].rearrange("p a b -> p (a b)")), dram["xT_hi"][g]).then_inc(xT_in, 16)
                    sp.dma_start(f(xT_lo[:, :, :].rearrange("p a b -> p (a b)")), dram["xT_lo"][g]).then_inc(xT_in, 16)

                def body(g):
                    last = isinstance(g, int) and g == GROUPS - 1
                    for b in range(NB):
                        if not (last and b == NB - 1):
                            wait(sp, ctxT_split, g, NB, b)
                            load_T(g * NB + b + 1, (b + 1) % 2)
                        wait_alone(sp, ctxN_split, g, NB, b - 1, passed["sp"])
                        wait_alone(sp, ctxL_split, g, NB, b - 1, passed["sp"])
                        load_N(g * NB + b, b % 2)
                    if not last:
                        wait(sp, q_done, g, ET, ET)
                        load_x(g + 1)
                    wait(sp, y_copied, g, 1, 1)
                    sp.dma_start(dram["y"][g], y[:, :, :].rearrange("p a b -> p (a b)")).then_inc(y_stored, 16)

                sp.wait_ge(pads_zero, 4)
                load_T(0, 0)
                load_x(0)
                groups(sp, body)
                sp.wait_ge(y_stored, 16 * GROUPS)

            @block.gpsimd
            def _(pool):
                def rest_T(g, b):
                    wait(pool, ctxT_hi_done, g, NB, b + 1)
                    pool.tensor_tensor(ctxT_lo[b % 2][:, :, :], raw_T[b % 2][:, :, :], f(ctxT_hi[b % 2][:, :, :]),
                                       ALU.subtract).then_inc(ctxT_split, 1)

                def body(g):
                    last = isinstance(g, int) and g == GROUPS - 1
                    for s in range(STEPS):
                        if s < TILES:
                            wait_alone(pool, rec_done, g, TILES, s + 1, passed["pool"])
                            pool.tensor_scalar(probs[:, s % RING, :], probs[:, s % RING, :], rec[:, s:s + 1], 1.0,
                                               ALU.mult, ALU.mult).then_inc(norm_done, 1)
                        for b in due(s, REST_T):
                            if not (last and b == NB - 1):
                                rest_T(g, b + 1)
                        for b in due(s, ROUND_N):
                            wait(pool, rawN_in[b % 2], g, 32 * NB // 2, 32 * (b // 2 + 1))
                            wait_alone(pool, z_done, g, DT * NB, DT * (b - 1), passed["pool"])
                            pool.tensor_copy(ctxL[b % 2][:, :], raw_L[b % 2][:, :]).then_inc(ctxL_hi_done, 1)
                        for b in due(s, REST_N):
                            wait(pool, ctxN_hi_done, g, NB, b + 1)
                            pool.tensor_tensor(ctxN_lo[b % 2][:, :, :], raw_N[b % 2][:, :, :],
                                               f(ctxN_hi[b % 2][:, :, :]), ALU.subtract).then_inc(ctxN_split, 1)

                for i in range(2):
                    pool.memset(raw_T[i][:, :, KEYS:KPAD], 0.0).then_inc(pads_zero, 1)
                    pool.memset(raw_L[i][:, :], 0.0).then_inc(pads_zero, 1)
                rest_T(0, 0)
                groups(pool, body)

            @block.vector
            def _(dve):
                def body(g):
                    wait(dve, exp_done, g, TILES, 0)
                    dve.tensor_copy(cg[:, :], W["cmap"][:, bass.ts(g, TILES)]).then_inc(cg_ready, 1)
                    def q_part(i):
                        wait(dve, q_hi, g, ET, i + 1)
                        dve.scalar_tensor_tensor(e_lo[i % 3][:, :], ps_s[i % 2][:, 0:GTOK], W["bq"][:, i:i + 1],
                                                 f(e_hi[i % 3][:, :]), ALU.add, ALU.subtract).then_inc(q_lo, 1)

                    q_part(0)
                    for i in range(ET):
                        if i + 1 < ET:
                            q_part(i + 1)
                        for h in (2 * i, 2 * i + 1):
                            wait(dve, qk_hi_done, g, HEADS, h + 1)
                            rows = (slice(None), slice(None), slice(None), slice(h * QLEN, (h + 1) * QLEN))
                            src = qk_banks[h % 3].rearrange("p (d b q) -> p d b q", d=DT, b=NB)
                            dve.tensor_tensor(qk_lo[rows], src, f(qk_hi[rows]), ALU.subtract).then_inc(qk_lo_done, 1)
                    wait(dve, cg_ready, g, 1, 1)
                    for s in range(STEPS):
                        if s < TILES:
                            wait(dve, sc_done, g, TILES, s + 1)
                            dve.tensor_reduce(mx[:, s:s + 1], score_banks[s % 3][:, 0:KEYS], AX_X, ALU.max).then_inc(max_done, 1)
                            wait(dve, max_done, g, TILES, s + 1)
                            dve.tensor_scalar(mc[:, s:s + 1], mx[:, s:s + 1], SCALE, cg[:, s:s + 1],
                                              ALU.mult, ALU.add).then_inc(mc_done, 1)
                            wait(dve, mc_done, g, TILES, s + 1)
                            dve.tensor_scalar(neg[:, s:s + 1], mc[:, s:s + 1], -1.0, cg[:, s:s + 1],
                                              ALU.mult, ALU.add).then_inc(neg_done, 1)
                        for b, dt in both_due(s, Z_LO):
                            wait(dve, z_hi, g, DT * NB, DT * b + dt + 1)
                            dve.tensor_tensor(qk_lo[:, dt, b, :], ps_z[dt][:, :], f(qk_hi[:, dt, b, :]),
                                              ALU.subtract).then_inc(z_lo, 1)
                        for b, half in both_due(s, P_LO):
                            wait(dve, pT_hi_done, g, 3 * NB, 3 * b + half + 1)
                            cols = slice(half * 2 * P, (half + 1) * 2 * P)
                            dve.tensor_tensor(pT_lo[b % 2][:, :, cols], ps_p[half][:, :, :],
                                              f(pT_hi[b % 2][:, :, cols]), ALU.subtract).then_inc(pT_lo_done, 1)
                        if s < TILES:
                            wait(dve, exp_done, g, TILES, s + 1)
                            dve.reciprocal(rec[:, s:s + 1], total[:, s:s + 1]).then_inc(rec_done, 1)
                        for b in due(s, P_LO[1]):
                            wait(dve, pT_hi_done, g, 3 * NB, 3 * b + 3)
                            dve.tensor_tensor(pL[b % 2][32:64, :], ps_l[32:64, :], f(pL[b % 2][32:64, :]),
                                              ALU.subtract).then_inc(pT_lo_done, 1)
                        for b in due(s, REST_N):
                            wait(dve, ctxL_hi_done, g, NB, b + 1)
                            dve.tensor_tensor(ctxL[b % 2][64:96, :], raw_L[b % 2][64:96, :],
                                              f(ctxL[b % 2][64:96, :]), ALU.subtract).then_inc(ctxL_split, 1)
                    for i in range(ET):
                        wait(dve, o_hi, g, ET, i + 1)
                        dve.scalar_tensor_tensor(e_lo[i % 3][:, :], ps_s[i % 2][:, 0:GTOK], W["bv"][:, i:i + 1],
                                                 f(e_hi[i % 3][:, :]), ALU.add, ALU.subtract).then_inc(o_lo, 1)

                groups(dve, body)

            @block.scalar
            def _(act):
                def round_T(g, b):
                    i = b % 2
                    wait(act, rawT_in[i], g, 16 * NB // 2, 16 * (b // 2 + 1))
                    wait(act, sc_done, g, TILES, HT * (b - 1))
                    act.activation(ctxT_hi[i][:, :, :], raw_T[i][:, :, :], ACT.Copy).then_inc(ctxT_hi_done, 1)

                def round_N(g, b):
                    i = b % 2
                    wait(act, rawN_in[i], g, 32 * NB // 2, 32 * (b // 2 + 1))
                    wait(act, z_done, g, DT * NB, DT * (b - 1))
                    act.activation(ctxN_hi[i][:, :, :], raw_N[i][:, :, :], ACT.Copy).then_inc(ctxN_hi_done, 1)

                def body(g):
                    last = isinstance(g, int) and g == GROUPS - 1

                    def q_part(i):
                        wait(act, q_done, g, ET, i + 1)
                        if i >= 3:
                            wait(act, qk_done, g, HEADS, 2 * (i - 3) + 2)
                        act.activation(e_hi[i % 3][:, :], ps_s[i % 2][:, 0:GTOK], ACT.Identity,
                                       bias=W["bq"][:, i:i + 1]).then_inc(q_hi, 1)

                    q_part(0)
                    for i in range(ET):
                        if i + 1 < ET:
                            q_part(i + 1)
                        for h in (2 * i, 2 * i + 1):
                            wait(act, qk_done, g, HEADS, h + 1)
                            rows = (slice(None), slice(None), slice(None), slice(h * QLEN, (h + 1) * QLEN))
                            src = qk_banks[h % 3].rearrange("p (d b q) -> p d b q", d=DT, b=NB)
                            act.activation(qk_hi[rows], src, ACT.Copy).then_inc(qk_hi_done, 1)
                    for s in range(STEPS):
                        if s < TILES:
                            if s >= RING and s % HT == 0:
                                wait(act, tpL_done, g, NB, s // HT - 1)
                            wait(act, neg_done, g, TILES, s + 1)
                            act.activation(probs[:, s % RING, :], score_banks[s % 3][:, 0:KEYS], ACT.Exp, bias=neg[:, s:s + 1],
                                           scale=SCALE, accum_out=total[:, s:s + 1]).then_inc(exp_done, 1)
                        for b, dt in both_due(s, Z_HI):
                            wait(act, z_done, g, DT * NB, DT * b + dt + 1)
                            act.activation(qk_hi[:, dt, b, :], ps_z[dt][:, :], ACT.Copy).then_inc(z_hi, 1)
                        for b, half in both_due(s, P_HI):
                            wait(act, tp_done, g, TILES, HT * b + 2 * half + 2)
                            if half == 0:
                                wait(act, z_done, g, DT * NB, DT * (b - 1))
                            act.activation(pT_hi[b % 2][:, :, half * 2 * P:(half + 1) * 2 * P], ps_p[half][:, :, :],
                                           ACT.Copy).then_inc(pT_hi_done, 1)
                        for b in due(s, P_HI[1]):
                            wait(act, tpL_done, g, NB, b + 1)
                            act.activation(pL[b % 2][:, :], ps_l[0:96, :], ACT.Copy).then_inc(pT_hi_done, 1)
                        for b in due(s, ROUND_T):
                            if not (last and b == NB - 1):
                                round_T(g, b + 1)
                        for b in due(s, ROUND_N):
                            round_N(g, b)
                    for i in range(ET):
                        wait(act, o_done, g, ET, i + 1)
                        if i >= 3:
                            wait(act, wo_done, g, ET, i - 2)
                        act.activation(e_hi[i % 3][:, :], ps_s[i % 2][:, 0:GTOK], ACT.Identity,
                                       bias=W["bv"][:, i:i + 1]).then_inc(o_hi, 1)
                    wait(act, wo_done, g, ET, ET)
                    wait(act, y_stored, g, 16, 0)
                    act.activation(y[:, :, :], ps_x[:, :, :], ACT.Copy).then_inc(y_copied, 1)

                act.wait_ge(pads_zero, 4)
                round_T(0, 0)
                groups(act, body)

            @block.tensor
            def _(pe):
                def body(g):
                    wait(pe, xT_in, g, 32, 32)

                    def q_part(i):
                        if i >= 2:
                            wait(pe, q_lo, g, ET, i - 1)
                        else:
                            wait(pe, o_lo, g, ET, 0)
                        for d in range(DT):
                            mm = three_pass(pe, ps_s[i % 2][:, 0:GTOK], W["wq_hi"][:, d, i * P:(i + 1) * P],
                                            W["wq_lo"][:, d, i * P:(i + 1) * P], xT_hi[:, d, :], xT_lo[:, d, :],
                                            d == 0, d == DT - 1)
                        mm.then_inc(q_done, 1)

                    def qk_part(h):
                        i, rows = h // 2, slice(DK * (h % 2), DK * (h % 2) + DK)
                        if h >= 3:
                            wait(pe, qk_lo_done, g, HEADS, h - 2)
                        elif h == 2:
                            wait(pe, y_copied, g, 1, 0)
                        wait(pe, q_lo, g, ET, i + 1)
                        for d in range(DT):
                            cols = slice(d * P, (d + 1) * P)
                            mm = three_pass(pe, qk_banks[h % 3][:, d * GTOK:(d + 1) * GTOK],
                                            W["wk_hi"][rows, i, cols], W["wk_lo"][rows, i, cols],
                                            e_hi[i % 3][rows, :], e_lo[i % 3][rows, :], True, True)
                        mm.then_inc(qk_done, 1)

                    q_part(0)
                    for i in range(ET):
                        if i + 1 < ET:
                            q_part(i + 1)
                        qk_part(2 * i)
                        qk_part(2 * i + 1)

                    def scores(s):
                        b, t = divmod(s, HT)
                        i, cols = b % 2, slice(t * P, (t + 1) * P)
                        if t == 0:
                            wait(pe, ctxT_split, g, NB, b + 1)
                        if b == 0:
                            wait(pe, qk_lo_done, g, HEADS, 4 * (t + 1) if t != 2 else HEADS - 1)
                        if s >= 3:
                            wait(pe, exp_done, g, TILES, s - 2)
                        for d in range(DT):
                            mm = three_pass(pe, score_banks[s % 3][:, 0:KPAD], qk_hi[:, d, b, cols], qk_lo[:, d, b, cols],
                                            ctxT_hi[i][:, d, :], ctxT_lo[i][:, d, :], d == 0, d == DT - 1)
                        mm.then_inc(sc_done, 1)

                    def transposes(s):
                        b, t = divmod(s, HT)
                        half, cols = t // 2, slice((t % 2) * P, (t % 2 + 1) * P)
                        wait(pe, norm_done, g, TILES, s + 1)
                        if t % 2 == 0:
                            wait(pe, pT_lo_done, g, 3 * NB, 3 * (b - 1) + half + 1)
                        for c in range(KC):
                            mm = pe.transpose(ps_p[half][:, c, cols], probs[:, s % RING, c * P:(c + 1) * P], W["ident"][:, :])
                        mm.then_inc(tp_done, 1)

                    def last_key(b):
                        wait(pe, pT_lo_done, g, 3 * NB, 3 * b)
                        for t in range(HT):
                            mm = pe.transpose(ps_l[0:96, t * P:(t + 1) * P],
                                              probs[:, (HT * b + t) % RING, KC * P:KEYS].to_broadcast([P, 96]), W["ident"][:, :])
                        mm.then_inc(tpL_done, 1)

                    def values(b, part):
                        dt, cols = part // 2, slice((part // 2) * P, (part // 2 + 1) * P)
                        i, out = b % 2, ps_z[part // 2][:, :]
                        if part == 0:
                            wait(pe, pT_lo_done, g, 3 * NB, 3 * (b + 1))
                            wait(pe, ctxN_split, g, NB, b + 1)
                            wait(pe, ctxL_split, g, NB, b + 1)
                        if part % 2 == 0:
                            if b >= 1:
                                wait(pe, z_lo, g, DT * NB, DT * (b - 1) + dt + 1)
                            three_pass(pe, out, ctxN_hi[i][:, 0, cols], ctxN_lo[i][:, 0, cols],
                                       pT_hi[i][:, 0, :], pT_lo[i][:, 0, :], True, False)
                            return
                        three_pass(pe, out, ctxN_hi[i][:, 1, cols], ctxN_lo[i][:, 1, cols],
                                   pT_hi[i][:, 1, :], pT_lo[i][:, 1, :], False, False)
                        pe.matmul(out, ctxL[i][:, cols], pL[i][:, :], start=False, stop=True).then_inc(z_done, 1)

                    for s in range(STEPS):
                        if s < TILES:
                            scores(s)
                        b, part = divmod(s - PV_LAG, PV_PARTS)
                        if 0 <= b < NB:
                            values(b, part)
                        if T_LAG <= s < TILES + T_LAG:
                            transposes(s - T_LAG)
                        for b in due(s, HT - 1 + T_LAG):
                            last_key(b)

                    def o_part(i):
                        if i >= 2:
                            wait(pe, o_lo, g, ET, i - 1)
                        out = ps_s[i % 2][:, 0:GTOK]
                        for h in range(2):
                            head = slice((2 * i + h) * QLEN, (2 * i + h + 1) * QLEN)
                            for d in range(DT):
                                mm = three_pass(pe, out, W["wv_hi"][:, d, i, h * DK:h * DK + P],
                                                W["wv_lo"][:, d, i, h * DK:h * DK + P],
                                                qk_hi[:, d, :, head], qk_lo[:, d, :, head],
                                                h == 0 and d == 0, h == 1 and d == DT - 1)
                        mm.then_inc(o_done, 1)

                    def y_part(i):
                        wait(pe, o_lo, g, ET, i + 1)
                        for tt in range(2):
                            cols = slice(tt * P, (tt + 1) * P)
                            mm = three_pass(pe, ps_x[:, tt, :], e_hi[i % 3][:, cols], e_lo[i % 3][:, cols],
                                            W["wo_hi"][:, i, :], W["wo_lo"][:, i, :],
                                            i == 0 and tt == 0, i == ET - 1 and tt == 1, skip_group_check=True)
                        mm.then_inc(wo_done, 1)

                    wait(pe, z_lo, g, DT * NB, DT * NB)
                    o_part(0)
                    for i in range(ET):
                        if i + 1 < ET:
                            o_part(i + 1)
                        y_part(i)

                groups(pe, body)


CHUNKS = GROUPS
CT = TT // CHUNKS
CTOK = CT * P
CB = CTOK // QLEN
FF = 4 * D
FT = FF // P
PAD = QLEN + 1
RUN = 2 * CB * PAD
LOW = -1e38
R_WEIGHTS = ("rr", "rk", "rv", "ro", "rg")


def recurrence(nc, A, W, dram):
    with ExitStack() as ctx:
        def sb(name, shape, dt=F32):
            return ctx.enter_context(nc.sbuf_tensor(name, shape, dt))

        def sem(name):
            return ctx.enter_context(nc.semaphore(name))

        def bank(name):
            return ctx.enter_context(nc.psum_tensor(name, [P, 512], F32))

        w_hi = {n: sb(n + "_hi", [P, DT, D], F32R) for n in R_WEIGHTS}
        w_lo = {n: sb(n + "_lo", [P, DT, D], F32R) for n in R_WEIGHTS}
        w_hi["fk"], w_lo["fk"] = sb("fk_hi", [P, DT, FF], F32R), sb("fk_lo", [P, DT, FF], F32R)
        w_hi["fv"], w_lo["fv"] = sb("fv_hi", [P, FT, D], F32R), sb("fv_lo", [P, FT, D], F32R)
        names = R_WEIGHTS + ("fk", "fv")
        raw = [sb(f"r_raw{i}", [P, DT * FF]) for i in range(2)]
        ln_wb = {n: sb(n, [P, D]) for n in ("ln1_w", "ln1_b", "ln2_w", "ln2_b")}
        decay_u = sb("decay_u", [P, 2 * DT])
        w_col = sb("w_col", [P, DT])
        w_run = sb("w_run", [P, DT, 2 * CB, PAD])
        gateT = sb("gateT", [P, DT, 8])
        gate_b = sb("gate_b", [P, 8])
        power = sb("r_power", [P, CT])

        zero_rows = sb("zero_rows", [P, 2 * D])
        x_in = sb("x_chunk", [P, CT, D])
        y_in = sb("y_chunk", [P, CT, D])
        n0 = sb("n0", [P, CT, D])
        n1 = sb("n1", [P, CT, D])
        stats = sb("r_stats", [P, 4, CT, 6])
        mv = sb("r_mv", [P, 4, CT, 2])
        veps = sb("r_veps", [P, 4, CT])
        rstd = sb("r_rstd", [P, 4, CT])
        nT_hi = sb("nT_hi", [P, DT, CTOK], F32R)
        nT_lo = sb("nT_lo", [P, DT, CTOK], F32R)
        hT = sb("hT", [P, DT, CTOK])
        gate_r = sb("gate_r", [P, DT, CTOK])
        k_run, v_run, p_run, f1_run, f2_run, fv_run, a_run, b_run = (
            sb(n + "_run", [P, DT, 2 * CB, PAD]) for n in ("k", "v", "p", "f1", "f2", "fv", "a", "b"))
        e1, e2, t1, t2 = (sb(n, [P, DT, 2 * CB, QLEN]) for n in ("e1", "e2", "t1", "t2"))
        rw = sb("rw", [P, DT, CTOK])
        rw_hi = sb("rw_hi", [P, DT, CTOK], F32R)
        rw_lo = sb("rw_lo", [P, DT, CTOK], F32R)
        relu = [sb(f"relu{i}", [P, 2 * CTOK]) for i in range(2)]
        sq = [sb(f"sq{i}", [P, 2 * CTOK]) for i in range(2)]
        kk_hi = sb("kk_hi", [P, FT, CTOK], F32R)
        kk_lo = sb("kk_lo", [P, FT, CTOK], F32R)
        sg = sb("sg", [P, CT, D])
        ps_t = [bank("ps_rt0"), bank("ps_rt1")]
        ps_m = [bank(f"ps_m{i}") for i in range(3)]
        ps_y = bank("ps_fv")
        ps_g = bank("ps_gate")

        passed = {n: sem("r_passed_" + n) for n in ("dve", "pool")}
        zero_set, zeroed = sem("zero_set"), sem("zeroed")
        w_in = [sem("rw_in0"), sem("rw_in1")]
        wr_hi, wr_lo = sem("wr_hi"), sem("wr_lo")
        small_in = sem("small_in")
        w_ready = sem("w_ready")
        pads = sem("pads")
        chunk_in = sem("chunk_in")
        x1_done = sem("x1_done")
        ln_stats, ln_mv, ln_veps, ln_rstd, ln_done = (sem("rln_" + n) for n in ("stats", "mv", "veps", "rstd", "done"))
        aff_done = sem("aff_done")
        t_done, t_hi, t_lo = sem("t_done"), sem("t_hi"), sem("t_lo")
        h_copied = sem("h_copied")
        m_done = sem("m_done")
        kv_copied = sem("kv_copied")
        r_gated = sem("r_gated")
        scan_p, args_done, exps_done, fv_done, scan_ab = (sem("wkv_" + n) for n in ("p", "args", "exps", "fv", "ab"))
        wkv_done = sem("wkv_done")
        rw_done = sem("rw_done")
        z_added = sem("z_added")
        relu_done, sq_done, kk_hi_done, kk_lo_done = (sem(n) for n in ("relu_done", "sq_done", "kk_hi_done", "kk_lo_done"))
        sg_done = sem("sg_done")
        y_done = sem("ff_done")
        x2_done = sem("x2_done")
        h_kept = sem("h_kept")
        lg_done = sem("lg_done")
        lg_copied = sem("lg_copied")

        sizes = {n: DT * D for n in R_WEIGHTS} | {"fk": DT * FF, "fv": FT * D}

        def flat(ap):
            return ap.rearrange("p a b -> p (a b)")

        with nc.Block() as block:
            @block.sync
            def _(sp):
                for n, c in (("decay_u", decay_u), ("gate_b", gate_b), ("ln1_w", ln_wb["ln1_w"]), ("ln1_b", ln_wb["ln1_b"]),
                             ("ln2_w", ln_wb["ln2_w"]), ("ln2_b", ln_wb["ln2_b"])):
                    src = A[n] if n == "decay_u" else A[n].to_broadcast([P, c.shape[1]])
                    sp.dma_start(c[:, :], src).then_inc(small_in, 16)
                sp.wait_ge(zero_set, 1)
                for n in range(SLOTS // (2 * P)):
                    sp.dma_start(dram["slots"][2 * P * n:2 * P * (n + 1), :].rearrange("(p r) d -> p (r d)", r=2),
                                 zero_rows[:, :]).then_inc(zeroed, 16)
                sp.dma_start(gateT[:, :, :], A["gateT"].rearrange("(t p) e -> p t e", p=P)).then_inc(small_in, 16)
                for j, n in enumerate(names):
                    if j >= 2:
                        sp.wait_ge(wr_lo, j - 1)
                    src = A[n].rearrange("(t p) e -> p t e", p=P)
                    dst = raw[j % 2][:, 0:sizes[n]].rearrange("p (t e) -> p t e", t=src.shape[1])
                    sp.dma_start(dst, src).then_inc(w_in[j % 2], 16)
                sp.wait_ge(zeroed, 16 * (SLOTS // (2 * P)))
                def body(c):
                    wait(sp, x2_done, c, 3, 0)
                    sp.dma_start(x_in[:, :, :], A["x"].rearrange("(c t p) d -> c p t d", p=P, t=CT)[c]).then_inc(chunk_in, 16)
                    sp.dma_start(y_in[:, :, :].rearrange("p t d -> p (t d)"), dram["y"][c]).then_inc(chunk_in, 16)

                turns(sp, CHUNKS, body)

            @block.gpsimd
            def _(pool):
                pool.memset(zero_rows[:, :], 0.0).then_inc(zero_set, 1)
                pool.memset(power[:, :], -0.5).then_inc(pads, 1)
                pool.memset(k_run[:, :, :, 0:1], LOW).then_inc(pads, 1)
                for run in (v_run, f1_run, f2_run, fv_run):
                    pool.memset(run[:, :, :, 0:1], 0.0).then_inc(pads, 1)
                pool.wait_ge(pads, 1)
                def body(c):
                    def root(n):
                        wait(pool, ln_veps, c, 4, n + 1)
                        pool.tensor_tensor(rstd[:, n, :], veps[:, n, :], power[:, :], ALU.pow).then_inc(ln_rstd, 1)

                    root(0)
                    root(1)
                    wait(pool, exps_done, c, 4, 2)
                    pool.tensor_tensor(fv_run[:, :, :, 1:PAD], f2_run[:, :, :, 1:PAD], v_run[:, :, :, 1:PAD],
                                       ALU.mult).then_inc(fv_done, 1)
                    root(2)
                    for i in range(FT // 2):
                        wait(pool, kk_hi_done, c, FT // 2, i + 1)
                        pair = slice(2 * i, 2 * i + 2)
                        pool.tensor_tensor(flat(kk_lo[:, pair, :]), sq[i % 2][:, :], f(flat(kk_hi[:, pair, :])),
                                           ALU.subtract).then_inc(kk_lo_done, 1)
                    root(3)
                    wait_alone(pool, ln_done, c, 4 * CT, 4 * CT, passed["pool"])
                    pool.tensor_copy(W["h"][:, bass.ts(c, CT), :], n1[:, :, :]).then_inc(h_kept, 1)

                turns(pool, CHUNKS, body)

            @block.vector
            def _(dve):
                dve.wait_ge(w_ready, 1)
                dve.tensor_scalar(w_col[:, :], w_col[:, :], -1.0, None, ALU.mult).then_inc(w_ready, 1)
                dve.memset(w_run[:, :, :, :], 0.0).then_inc(w_ready, 1)
                dve.wait_ge(w_ready, 3)
                for d in range(DT):
                    dve.tensor_scalar(w_run[:, d], w_run[:, d], w_col[:, d:d + 1], None, ALU.add).then_inc(w_ready, 1)
                dve.wait_ge(w_ready, 5)
                dve.memset(w_run[:, :, :, 0:1], LOW).then_inc(w_ready, 1)
                dve.wait_ge(w_ready, 6)
                for j, n in enumerate(names):
                    dve.wait_ge(wr_hi, j + 1)
                    dve.tensor_tensor(flat(w_lo[n][:, :, :]), raw[j % 2][:, 0:sizes[n]], f(flat(w_hi[n][:, :, :])),
                                      ALU.subtract).then_inc(wr_lo, 1)
                dve.wait_ge(small_in, 16 * 7)
                dve.wait_ge(pads, 6)

                def body(c):
                    def normalise(n, src, dst):
                        for t in range(CT):
                            dve.bn_stats(stats[:, n, t, :], src(t)).then_inc(ln_stats, 1)
                        for t in range(CT):
                            wait_alone(dve, ln_stats, c, 4 * CT, n * CT + t + 1, passed["dve"])
                            dve.bn_aggr(mv[:, n, t, :], stats[:, n, t, :]).then_inc(ln_mv, 1)
                        wait(dve, ln_mv, c, 4 * CT, (n + 1) * CT)
                        dve.tensor_scalar(veps[:, n, :], mv[:, n, :, 1], EPS, None, ALU.add).then_inc(ln_veps, 1)
                        wait(dve, ln_rstd, c, 4, n + 1)
                        for t in range(CT):
                            dve.tensor_scalar(dst(t), src(t), mv[:, n, t, 0:1], rstd[:, n, t:t + 1],
                                              ALU.subtract, ALU.mult).then_inc(ln_done, 1)
                        wait(dve, ln_done, c, 4 * CT, (n + 1) * CT)

                    def affine(n, name):
                        w, b = (ln_wb[name + p][:, :].unsqueeze(1).to_broadcast([P, CT, D]) for p in ("_w", "_b"))
                        dve.tensor_tensor(n1[:, :, :], n1[:, :, :], w, ALU.mult).then_inc(aff_done, 1)
                        wait(dve, aff_done, c, 4, 2 * n + 1)
                        dve.tensor_tensor(n1[:, :, :], n1[:, :, :], b, ALU.add).then_inc(aff_done, 1)

                    def rest_of_transpose(n):
                        wait(dve, t_hi, c, 2, n + 1)
                        dve.tensor_tensor(flat(nT_lo[:, :, :]), ps_t[n][:, :], f(flat(nT_hi[:, :, :])), ALU.subtract).then_inc(t_lo, 1)

                    wait(dve, chunk_in, c, 32, 32)
                    dve.tensor_tensor(x_in[:, :, :], x_in[:, :, :], y_in[:, :, :], ALU.add).then_inc(x1_done, 1)
                    wait(dve, x1_done, c, 1, 1)
                    normalise(0, lambda t: x_in[:, t, :], lambda t: n0[:, t, :])
                    wait(dve, h_kept, c, 1, 0)
                    normalise(1, lambda t: n0[:, t, :], lambda t: n1[:, t, :])
                    affine(0, "ln1")
                    rest_of_transpose(0)

                    steps, before = slice(1, PAD), slice(0, QLEN)

                    def whole(run):
                        return run[:, :, :, :].rearrange("p a b c -> p (a b c)")

                    def mix(op, n):
                        wait(dve, wkv_done, c, 9, n - 1)
                        op.then_inc(wkv_done, 1)

                    wait(dve, kv_copied, c, 4, 2)
                    dve.tensor_tensor_scan(whole(p_run), whole(w_run), whole(k_run), 0.0, ALU.add, ALU.max).then_inc(scan_p, 1)
                    wait(dve, scan_p, c, 1, 1)
                    for d in range(DT):
                        dve.scalar_tensor_tensor(f1_run[:, d, :, steps], p_run[:, d, :, before], w_col[:, d:d + 1],
                                                 p_run[:, d, :, steps], ALU.add, ALU.subtract).then_inc(args_done, 1)
                    dve.tensor_tensor(f2_run[:, :, :, steps], k_run[:, :, :, steps], p_run[:, :, :, steps],
                                      ALU.subtract).then_inc(args_done, 1)
                    for d in range(DT):
                        dve.scalar_tensor_tensor(t1[:, d], k_run[:, d, :, steps], decay_u[:, DT + d:DT + d + 1],
                                                 p_run[:, d, :, before], ALU.add, ALU.subtract).then_inc(args_done, 1)
                    wait(dve, args_done, c, 7, 5)
                    dve.tensor_scalar(e1[:, :, :, :], t1[:, :, :, :], -1.0, 0.0, ALU.mult, ALU.min).then_inc(args_done, 1)
                    dve.tensor_scalar(e2[:, :, :, :], t1[:, :, :, :], 0.0, None, ALU.min).then_inc(args_done, 1)
                    wait(dve, exps_done, c, 4, 2)
                    dve.tensor_tensor_scan(whole(b_run), whole(f1_run), whole(f2_run), 0.0, ALU.mult, ALU.add).then_inc(scan_ab, 1)
                    wait(dve, fv_done, c, 1, 1)
                    dve.tensor_tensor_scan(whole(a_run), whole(f1_run), whole(fv_run), 0.0, ALU.mult, ALU.add).then_inc(scan_ab, 1)
                    wait(dve, exps_done, c, 4, 4)
                    dve.tensor_tensor(t2[:, :, :, :], e2[:, :, :, :], v_run[:, :, :, steps], ALU.mult).then_inc(wkv_done, 1)
                    wait(dve, scan_ab, c, 2, 2)
                    dve.tensor_tensor(t1[:, :, :, :], e1[:, :, :, :], a_run[:, :, :, before], ALU.mult).then_inc(wkv_done, 1)
                    dve.tensor_tensor(e1[:, :, :, :], e1[:, :, :, :], b_run[:, :, :, before], ALU.mult).then_inc(wkv_done, 1)
                    wait(dve, wkv_done, c, 9, 3)
                    dve.tensor_tensor(e1[:, :, :, :], e1[:, :, :, :], e2[:, :, :, :], ALU.add).then_inc(wkv_done, 1)
                    dve.tensor_tensor(t1[:, :, :, :], t1[:, :, :, :], t2[:, :, :, :], ALU.add).then_inc(wkv_done, 1)
                    wait(dve, wkv_done, c, 9, 5)
                    dve.reciprocal(e1[:, :, :, :], e1[:, :, :, :]).then_inc(wkv_done, 1)
                    wait(dve, wkv_done, c, 9, 6)
                    dve.tensor_tensor(t1[:, :, :, :], t1[:, :, :, :], e1[:, :, :, :], ALU.mult).then_inc(wkv_done, 1)
                    wait(dve, wkv_done, c, 9, 7)
                    rw_v = rw[:, :, :].rearrange("p d (b t) -> p d b t", t=QLEN)
                    dve.tensor_tensor(rw_v, t1[:, :, 0:CB, :], t1[:, :, CB:2 * CB, ::-1], ALU.add).then_inc(wkv_done, 1)
                    wait(dve, r_gated, c, 1, 1)
                    wait(dve, wkv_done, c, 9, 8)
                    dve.scalar_tensor_tensor(rw[:, :, :], rw[:, :, :], 0.5, gate_r[:, :, :], ALU.mult, ALU.mult).then_inc(wkv_done, 1)
                    wait(dve, wkv_done, c, 9, 9)
                    dve.tensor_copy(rw_hi[:, :, :], rw[:, :, :]).then_inc(rw_done, 1)
                    wait(dve, rw_done, c, 2, 1)
                    dve.tensor_tensor(rw_lo[:, :, :], rw[:, :, :], f(rw_hi[:, :, :]), ALU.subtract).then_inc(rw_done, 1)

                    wait(dve, m_done, c, 9, 4)
                    dve.tensor_tensor(flat(n0[:, :, :]), flat(n0[:, :, :]), ps_m[0][:, :], ALU.add).then_inc(z_added, 1)
                    wait(dve, z_added, c, 1, 1)
                    normalise(2, lambda t: n0[:, t, :], lambda t: n1[:, t, :])
                    affine(1, "ln2")
                    rest_of_transpose(1)
                    for i in range(FT // 2):
                        wait(dve, sq_done, c, FT // 2, i + 1)
                        dve.tensor_copy(flat(kk_hi[:, 2 * i:2 * i + 2, :]), sq[i % 2][:, :]).then_inc(kk_hi_done, 1)
                    dve.tensor_tensor(x_in[:, :, :], x_in[:, :, :], n0[:, :, :], ALU.add).then_inc(x2_done, 1)
                    wait(dve, sg_done, c, 1, 1)
                    wait(dve, y_done, c, 1, 1)
                    dve.tensor_tensor(flat(sg[:, :, :]), flat(sg[:, :, :]), ps_y[:, :], ALU.mult).then_inc(x2_done, 1)
                    wait(dve, x2_done, c, 3, 2)
                    dve.tensor_tensor(W["x2"][:, bass.ts(c, CT), :], x_in[:, :, :], sg[:, :, :], ALU.add).then_inc(x2_done, 1)
                    wait_alone(dve, x2_done, c, 3, 3, passed["dve"])
                    normalise(3, lambda t: W["x2"][:, bass.ds(c * CT + t, 1), :].rearrange("p a d -> p (a d)"),
                              lambda t: n1[:, t, :])
                    wait(dve, lg_done, c, 1, 1)
                    dve.tensor_tensor(W["logits"][:, bass.ts(c, CT), :], ps_g[:, 0:CT * 8].rearrange("p (t e) -> p t e", e=8),
                                      gate_b[:, :].unsqueeze(1).to_broadcast([P, CT, 8]), ALU.add).then_inc(lg_copied, 1)

                turns(dve, CHUNKS, body)

            @block.scalar
            def _(act):
                act.wait_ge(small_in, 16 * 7)
                act.activation(w_col[:, :], decay_u[:, 0:DT], ACT.Exp).then_inc(w_ready, 1)
                for j, n in enumerate(names):
                    act.wait_ge(w_in[j % 2], 16 * (j // 2 + 1))
                    act.activation(flat(w_hi[n][:, :, :]), raw[j % 2][:, 0:sizes[n]], ACT.Copy).then_inc(wr_hi, 1)
                def body(c):
                    def transposed(n):
                        wait(act, t_done, c, 3, n + 1)
                        act.activation(flat(nT_hi[:, :, :]), ps_t[n][:, :], ACT.Copy).then_inc(t_hi, 1)

                    transposed(0)
                    for j, run in enumerate((k_run, v_run)):
                        wait(act, m_done, c, 9, j + 1)
                        src = ps_m[j][:, :].rearrange("p (d b t) -> p d b t", d=DT, t=QLEN)
                        act.activation(run[:, :, 0:CB, 1:PAD], src, ACT.Copy).then_inc(kv_copied, 1)
                        act.activation(run[:, :, CB:2 * CB, QLEN:0:-1], src, ACT.Copy).then_inc(kv_copied, 1)
                    wait(act, m_done, c, 9, 3)
                    act.activation(flat(gate_r[:, :, :]), ps_m[2][:, :], ACT.Sigmoid).then_inc(r_gated, 1)
                    for tile, need in ((f1_run[:, :, :, 1:PAD], 2), (f2_run[:, :, :, 1:PAD], 3), (e1[:, :, :, :], 6), (e2[:, :, :, :], 7)):
                        wait(act, args_done, c, 7, need)
                        act.activation(tile, tile, ACT.Exp).then_inc(exps_done, 1)
                    transposed(1)
                    for i in range(FT // 2):
                        wait(act, m_done, c, 9, 5 + i)
                        act.activation(relu[i % 2][:, :], ps_m[(4 + i) % 3][:, :], ACT.Relu).then_inc(relu_done, 1)
                        wait(act, relu_done, c, FT // 2, i + 1)
                        wait(act, kk_lo_done, c, FT // 2, i - 1) if i >= 2 else None
                        act.activation(sq[i % 2][:, :], relu[i % 2][:, :], ACT.Square).then_inc(sq_done, 1)
                    wait(act, m_done, c, 9, 9)
                    act.activation(flat(sg[:, :, :]), ps_m[2][:, :], ACT.Sigmoid).then_inc(sg_done, 1)
                    wait(act, t_done, c, 3, 3)
                    act.activation(flat(hT[:, :, :]), ps_t[0][:, :], ACT.Copy).then_inc(h_copied, 1)

                turns(act, CHUNKS, body)

            @block.tensor
            def _(pe):
                pe.wait_ge(wr_lo, len(names))
                def body(c):
                    def transposed(n, sem, per, count):
                        wait(pe, sem, c, per, count)
                        for d in range(DT):
                            for t in range(CT):
                                mm = pe.transpose(ps_t[n % 2][:, d * CTOK + t * P:d * CTOK + (t + 1) * P],
                                                  n1[:, t, d * P:(d + 1) * P], W["ident"][:, :])
                        mm.then_inc(t_done, 1)

                    def channels(bank, n, col):
                        for j in range(2):
                            for d in range(DT):
                                cols = slice((col + j) * P, (col + j + 1) * P)
                                mm = three_pass(pe, ps_m[bank][:, j * CTOK:(j + 1) * CTOK], w_hi[n][:, d, cols], w_lo[n][:, d, cols],
                                                nT_hi[:, d, :], nT_lo[:, d, :], d == 0, d == DT - 1)
                        mm.then_inc(m_done, 1)

                    def tokens(out, n, hi, lo, depth, sem):
                        for t in range(CT):
                            cols = slice(t * P, (t + 1) * P)
                            for d in range(depth):
                                mm = three_pass(pe, out[:, t * D:(t + 1) * D], hi[:, d, cols], lo[:, d, cols],
                                                w_hi[n][:, d, :], w_lo[n][:, d, :], d == 0, d == depth - 1)
                        mm.then_inc(sem, 1)

                    transposed(0, aff_done, 4, 2)
                    wait(pe, t_lo, c, 2, 1)
                    channels(0, "rk", 0)
                    channels(1, "rv", 0)
                    channels(2, "rr", 0)
                    wait(pe, kv_copied, c, 4, 2)
                    wait(pe, rw_done, c, 2, 2)
                    tokens(ps_m[0], "ro", rw_hi, rw_lo, DT, m_done)
                    transposed(1, aff_done, 4, 4)
                    wait(pe, t_lo, c, 2, 2)
                    for i, (sem, per, count) in enumerate(((kv_copied, 4, 4), (r_gated, 1, 1), (z_added, 1, 1), (relu_done, 4, 1))):
                        wait(pe, sem, c, per, count)
                        channels((4 + i) % 3, "fk", 2 * i)
                    wait(pe, relu_done, c, 4, 2)
                    tokens(ps_m[2], "rg", nT_hi, nT_lo, DT, m_done)
                    wait(pe, kk_lo_done, c, FT // 2, FT // 2)
                    tokens(ps_y, "fv", kk_hi, kk_lo, FT, y_done)
                    transposed(2, ln_done, 4 * CT, 4 * CT)
                    wait(pe, h_copied, c, 1, 1)
                    for t in range(CT):
                        for d in range(DT):
                            mm = pe.matmul(ps_g[:, t * 8:(t + 1) * 8], hT[:, d, t * P:(t + 1) * P], gateT[:, d, :],
                                           start=(d == 0), stop=(d == DT - 1))
                    mm.then_inc(lg_done, 1)

                turns(pe, CHUNKS, body)


EXPERTS = 8
CAP = -(-TOKENS * 5 // (4 * EXPERTS))
SLOTS = EXPERTS * CAP
HF = 4 * D
HFT = HF // P
SPLIT = [(0, P), (P, P), (2 * P, CAP - 2 * P)]


def experts(nc, A, W, dram, out):
    with ExitStack() as ctx:
        def sb(name, shape, dt=F32):
            return ctx.enter_context(nc.sbuf_tensor(name, shape, dt))

        def sem(name):
            return ctx.enter_context(nc.semaphore(name))

        def bank(name):
            return ctx.enter_context(nc.psum_tensor(name, [P, 512], F32))

        x2, h, logits = W["x2"], W["h"], W["logits"]
        tri = sb("tri", [P, P])
        ones = sb("ones", [P, P])
        e_iota = sb("e_iota", [P, EXPERTS])
        e_int = sb("e_int", [P, EXPERTS], mybir.dt.int32)
        tok = sb("tok", [P, TT])
        tok_int = sb("tok_int", [P, TT], mybir.dt.int32)
        zeros = sb("zeros16", [P, TT])
        m, total, rec, top, idx, pos, keep, slot, far, tw = (
            sb("gt_" + n, [P, TT]) for n in ("m", "total", "rec", "top", "idx", "pos", "keep", "slot", "far", "tw"))
        prob, eq, hot, tot, run, pre = (sb("gt_" + n, [P, TT, EXPERTS]) for n in ("prob", "eq", "hot", "tot", "run", "pre"))
        scatter_to = sb("scatter_to", [P, TT], U32)
        gather_from = sb("gather_from", [P, TT], U32)

        raw1 = [sb(f"raw1_{i}", [P, DT * HF]) for i in range(2)]
        raw2 = [sb(f"raw2_{i}", [P, HFT * D]) for i in range(2)]
        w1_hi, w1_lo = ([sb(f"w1_{p}{i}", [P, DT, HF], F32R) for i in range(2)] for p in ("hi", "lo"))
        w2_hi, w2_lo = ([sb(f"w2_{p}{i}", [P, HFT, D], F32R) for i in range(2)] for p in ("hi", "lo"))
        b1 = sb("b1", [P, EXPERTS, HFT])
        b2 = sb("b2", [P, EXPERTS, D])
        rows = [sb(f"rows{i}", [P, 3, D]) for i in range(2)]
        rT_hi = sb("rT_hi", [P, DT, CAP], F32R)
        rT_lo = sb("rT_lo", [P, DT, CAP], F32R)
        hid = [sb(f"hid{i}", [P, CAP]) for i in range(2)]
        hid_hi = sb("hid_hi", [P, HFT, CAP], F32R)
        hid_lo = sb("hid_lo", [P, HFT, CAP], F32R)
        eo = [sb(f"eo{i}", [P, 3, D]) for i in range(2)]

        ps_t = [bank("ps_et0"), bank("ps_et1")]
        ps_h = [bank(f"ps_h{i}") for i in range(3)]
        ps_y = [bank("ps_ey0"), bank("ps_ey1")]
        ps_c = bank("ps_count")

        masks = sem("masks")
        consts = sem("consts")
        b_in = sem("b_in")
        g_step = sem("gate_step")
        g_exp = sem("gate_exp")
        counted = sem("counted")
        slots_ready = sem("slots_ready")
        scattered = sem("scattered")
        w_in = [sem("ew_in0"), sem("ew_in1")]
        w_hi_done, w_lo_done = sem("ew_hi"), sem("ew_lo")
        rows_in = [sem("rows_in0"), sem("rows_in1")]
        t_done, t_hi, t_lo = sem("et_done"), sem("et_hi"), sem("et_lo")
        h_done, h_relu, h_hi, h_lo = sem("eh_done"), sem("eh_relu"), sem("eh_hi"), sem("eh_lo")
        y_done, y_copied = sem("ey_done"), sem("ey_copied")
        eo_stored = [sem("eo_stored0"), sem("eo_stored1")]
        gathered = sem("gathered")
        weighted = sem("weighted")
        summed = sem("summed")
        stored = sem("out_stored")

        PAIRS = EXPERTS // 2

        def flat(ap):
            return ap.rearrange("p a b -> p (a b)")

        with nc.Block() as block:
            @block.sync
            def _(sp):
                sp.dma_start(b1[:, :, :], A["b1"]).then_inc(b_in, 16)
                sp.dma_start(flat(b2[:, :, :]), A["b2"].to_broadcast([P, EXPERTS * D])).then_inc(b_in, 16)
                def body(j):
                    for i in range(2):
                        e = 2 * j + i
                        wait(sp, w_lo_done, j, 4, 2 * i - 2 + 2 * (1 - i))
                        sp.dma_start(raw1[i][:, :].rearrange("p (t n) -> p t n", t=DT),
                                     A["w1"].rearrange("e (t p) n -> e p t n", p=P)[e]).then_inc(w_in[i], 16)
                        sp.dma_start(raw2[i][:, :].rearrange("p (t n) -> p t n", t=HFT),
                                     A["w2"].rearrange("e (t p) n -> e p t n", p=P)[e]).then_inc(w_in[i], 16)
                        sp.wait_ge(scattered, 16 * TT)
                        wait(sp, t_done, j, 4, 0)
                        slots = dram["slots"][0:SLOTS, :].rearrange("(e s) d -> e s d", s=CAP)[e]
                        sp.dma_start(rows[i][:, 0:2, :], slots[0:2 * P, :].rearrange("(k p) d -> p k d", p=P)).then_inc(rows_in[i], 16)
                        sp.dma_start(rows[i][0:CAP - 2 * P, 2, :], slots[2 * P:CAP, :]).then_inc(rows_in[i], 16)

                turns(sp, PAIRS, body)

            @block.gpsimd
            def _(pool):
                pool.memset(ones[:, :], 1.0).then_inc(masks, 1)
                pool.memset(zeros[:, :], 0.0).then_inc(masks, 1)
                pool.iota(e_int[:, :], [[1, EXPERTS]], base=0, channel_multiplier=0).then_inc(masks, 1)
                pool.iota(tok_int[:, :], [[P, TT]], base=0, channel_multiplier=1).then_inc(masks, 1)
                pool.wait_ge(masks, 4)
                pool.affine_select(out=tri[:, :], in_=ones[:, :], compare_op=ALU.is_ge, fill=0.0, base=0,
                                   pattern=[[1, P]], channel_multiplier=-1).then_inc(masks, 1)
                pool.tensor_copy(e_iota[:, :], e_int[:, :]).then_inc(consts, 1)
                pool.tensor_copy(tok[:, :], tok_int[:, :]).then_inc(consts, 1)
                pool.wait_ge(slots_ready, 2)
                for t in range(TT):
                    pool.indirect_dma_start(out=dram["slots"], out_offset=bass.IndirectOffsetOnAxis(scatter_to[:, t:t + 1], 0),
                                            in_=h[:, t, :], in_offset=None).then_inc(scattered, 16)
                def body(j):
                    for i in range(2):
                        for k, (raw, hi, lo) in enumerate(((raw1, w1_hi, w1_lo), (raw2, w2_hi, w2_lo))):
                            wait(pool, w_hi_done, j, 4, 2 * i + k + 1)
                            pool.tensor_tensor(flat(lo[i][:, :, :]), raw[i][:, :], f(flat(hi[i][:, :, :])),
                                               ALU.subtract).then_inc(w_lo_done, 1)

                turns(pool, PAIRS, body)
                for i in range(2):
                    pool.wait_ge(eo_stored[i], 32 * PAIRS)
                for t in range(TT):
                    pool.indirect_dma_start(out=h[:, t, :], out_offset=None, in_=dram["results"],
                                            in_offset=bass.IndirectOffsetOnAxis(gather_from[:, t:t + 1], 0)).then_inc(gathered, 16)

            @block.vector
            def _(dve):
                done = 0

                def step(op):
                    nonlocal done
                    op.then_inc(g_step, 1)
                    done += 1
                    dve.wait_ge(g_step, done)

                def over(v):
                    return v[:, :].unsqueeze(2).to_broadcast([P, TT, EXPERTS])

                iota = e_iota[:, :].unsqueeze(1).to_broadcast([P, TT, EXPERTS])
                dve.wait_ge(consts, 2)
                step(dve.tensor_reduce(m[:, :], logits[:, :, :], AX_X, ALU.max))
                step(dve.tensor_tensor(prob[:, :, :], logits[:, :, :], over(m), ALU.subtract))
                dve.wait_ge(g_exp, 1)
                step(dve.tensor_reduce(total[:, :], prob[:, :, :], AX_X, ALU.add))
                step(dve.reciprocal(rec[:, :], total[:, :]))
                step(dve.tensor_tensor(prob[:, :, :], prob[:, :, :], over(rec), ALU.mult))
                step(dve.tensor_reduce(top[:, :], prob[:, :, :], AX_X, ALU.max))
                step(dve.tensor_tensor(eq[:, :, :], prob[:, :, :], over(top), ALU.is_equal))
                step(dve.tensor_scalar(eq[:, :, :], eq[:, :, :], -float(EXPERTS), float(EXPERTS), ALU.mult, ALU.add))
                step(dve.tensor_tensor(eq[:, :, :], eq[:, :, :], iota, ALU.add))
                step(dve.tensor_reduce(idx[:, :], eq[:, :, :], AX_X, ALU.min))
                step(dve.tensor_tensor(hot[:, :, :], iota, over(idx), ALU.is_equal))
                dve.wait_ge(counted, 2)
                step(dve.tensor_copy(tot[:, :, :], ps_c[:, P:2 * P].rearrange("p (t e) -> p t e", e=EXPERTS)))
                for e in range(EXPERTS):
                    dve.tensor_tensor_scan(run[:, :, e], tot[:, :, e], zeros[:, :], 0.0, ALU.add, ALU.add).then_inc(g_step, 1)
                done += EXPERTS
                dve.wait_ge(g_step, done)
                step(dve.tensor_tensor(run[:, :, :], run[:, :, :], tot[:, :, :], ALU.subtract))
                step(dve.tensor_tensor(pre[:, :, :], run[:, :, :], ps_c[:, 0:P].rearrange("p (t e) -> p t e", e=EXPERTS), ALU.add))
                step(dve.tensor_tensor(pre[:, :, :], pre[:, :, :], hot[:, :, :], ALU.mult))
                step(dve.tensor_reduce(pos[:, :], pre[:, :, :], AX_X, ALU.add))
                step(dve.tensor_scalar(pos[:, :], pos[:, :], 1.0, None, ALU.subtract))
                step(dve.tensor_scalar(keep[:, :], pos[:, :], float(CAP), None, ALU.is_lt))
                step(dve.tensor_tensor(tw[:, :], top[:, :], keep[:, :], ALU.mult))
                step(dve.tensor_tensor(pos[:, :], pos[:, :], keep[:, :], ALU.mult))
                step(dve.tensor_scalar(slot[:, :], idx[:, :], float(CAP), None, ALU.mult))
                step(dve.tensor_tensor(slot[:, :], slot[:, :], pos[:, :], ALU.add))
                dve.tensor_copy(gather_from[:, :], slot[:, :]).then_inc(slots_ready, 1)
                step(dve.tensor_scalar(far[:, :], tok[:, :], float(SLOTS), None, ALU.add))
                step(dve.tensor_tensor(slot[:, :], slot[:, :], far[:, :], ALU.subtract))
                step(dve.tensor_tensor(slot[:, :], slot[:, :], keep[:, :], ALU.mult))
                step(dve.tensor_tensor(slot[:, :], slot[:, :], far[:, :], ALU.add))
                dve.tensor_copy(scatter_to[:, :], slot[:, :]).then_inc(slots_ready, 1)

                dve.wait_ge(b_in, 32)
                def body(j):
                    for i in range(2):
                        for d in range(DT):
                            wait(dve, t_hi, j, 4, 2 * i + d + 1)
                            dve.tensor_tensor(rT_lo[:, d, :], ps_t[d][:, 0:CAP], f(rT_hi[:, d, :]), ALU.subtract).then_inc(t_lo, 1)
                        for k in range(HFT):
                            wait(dve, h_relu, j, 2 * HFT, HFT * i + k + 1)
                            dve.tensor_copy(hid_hi[:, k, :], hid[k % 2][:, :]).then_inc(h_hi, 1)
                            wait(dve, h_hi, j, 2 * HFT, HFT * i + k + 1)
                            dve.tensor_tensor(hid_lo[:, k, :], hid[k % 2][:, :], f(hid_hi[:, k, :]), ALU.subtract).then_inc(h_lo, 1)
                        wait(dve, eo_stored[i], j, 32, 0)
                        bias = b2[:, bass.ds(2 * j + i, 1), :].rearrange("p a d -> p (a d)")
                        for k in range(3):
                            wait(dve, y_done, j, 6, 3 * i + (2, 2, 3)[k])
                            r = slice(0, P) if k < 2 else slice(3 * P - CAP, P)
                            dve.tensor_tensor(eo[i][r, k, :], ps_y[k // 2][r, (k % 2) * D:(k % 2 + 1) * D], bias[r, :],
                                              ALU.add).then_inc(y_copied, 1)

                turns(dve, PAIRS, body)
                for t in range(TT):
                    dve.wait_ge(gathered, 16 * TT)
                    dve.scalar_tensor_tensor(x2[:, t, :], h[:, t, :], tw[:, t:t + 1], x2[:, t, :], ALU.mult, ALU.add).then_inc(summed, 1)

            @block.scalar
            def _(act):
                act.wait_ge(g_step, 2)
                act.activation(prob[:, :, :], prob[:, :, :], ACT.Exp).then_inc(g_exp, 1)
                act.wait_ge(b_in, 32)
                def body(j):
                    for i in range(2):
                        wait(act, w_in[i], j, 32, 32)
                        wait(act, y_done, j, 6, 0)
                        act.activation(flat(w1_hi[i][:, :, :]), raw1[i][:, :], ACT.Copy).then_inc(w_hi_done, 1)
                        act.activation(flat(w2_hi[i][:, :, :]), raw2[i][:, :], ACT.Copy).then_inc(w_hi_done, 1)
                        for d in range(DT):
                            wait(act, t_done, j, 4, 2 * i + d + 1)
                            act.activation(rT_hi[:, d, :], ps_t[d][:, 0:CAP], ACT.Copy).then_inc(t_hi, 1)
                        for k in range(HFT):
                            wait(act, h_done, j, 2 * HFT, HFT * i + k + 1)
                            if k >= 2:
                                wait(act, h_lo, j, 2 * HFT, HFT * i + k - 1)
                            act.activation(hid[k % 2][:, :], ps_h[k % 3][:, 0:CAP], ACT.Relu,
                                           bias=b1[:, bass.ds(2 * j + i, 1), k]).then_inc(h_relu, 1)
                        e = 2 * j + i
                        wait(act, y_copied, j, 6, 3 * i + 3)
                        slots = dram["results"].rearrange("(e s) d -> e s d", s=CAP)[e]
                        act.dma_start(slots[0:2 * P, :].rearrange("(k p) d -> p k d", p=P), eo[i][:, 0:2, :]).then_inc(eo_stored[i], 16)
                        act.dma_start(slots[2 * P:CAP, :], eo[i][3 * P - CAP:P, 2, :]).then_inc(eo_stored[i], 16)

                turns(act, PAIRS, body)
                for q in range(4):
                    n = TT // 4
                    act.wait_ge(summed, n * (q + 1))
                    act.dma_start(out.rearrange("(t p) d -> p t d", p=P)[:, q * n:(q + 1) * n, :],
                                  x2[:, q * n:(q + 1) * n, :]).then_inc(stored, 16)
                act.wait_ge(stored, 64)

            @block.tensor
            def _(pe):
                pe.wait_ge(masks, 5)
                pe.wait_ge(g_step, 11)
                hot_flat = flat(hot[:, :, :])
                pe.matmul(ps_c[:, 0:P], tri[:, :], hot_flat, start=True, stop=True).then_inc(counted, 1)
                pe.matmul(ps_c[:, P:2 * P], ones[:, :], hot_flat, start=True, stop=True).then_inc(counted, 1)
                def body(j):
                    for i in range(2):
                        wait(pe, rows_in[i], j, 32, 32)
                        for d in range(DT):
                            for k, (at, n) in enumerate(SPLIT):
                                mm = pe.transpose(ps_t[d][:, at:at + n], rows[i][0:n, k, d * P:(d + 1) * P], W["ident"][0:n, 0:n])
                            mm.then_inc(t_done, 1)
                        wait(pe, w_lo_done, j, 4, 2 * i + 2)
                        wait(pe, t_lo, j, 4, 2 * i + 2)
                        for k in range(HFT):
                            if k >= 3:
                                wait(pe, h_relu, j, 2 * HFT, HFT * i + k - 2)
                            for d in range(DT):
                                cols = slice(k * P, (k + 1) * P)
                                mm = three_pass(pe, ps_h[k % 3][:, 0:CAP], w1_hi[i][:, d, cols], w1_lo[i][:, d, cols],
                                                rT_hi[:, d, :], rT_lo[:, d, :], d == 0, d == DT - 1)
                            mm.then_inc(h_done, 1)
                        wait(pe, h_lo, j, 2 * HFT, HFT * (i + 1))
                        wait(pe, y_copied, j, 6, 3 * i)
                        for k, at in enumerate((0, P, CAP - P)):
                            for t in range(HFT):
                                mm = three_pass(pe, ps_y[k // 2][:, (k % 2) * D:(k % 2 + 1) * D], hid_hi[:, t, at:at + P],
                                                hid_lo[:, t, at:at + P], w2_hi[i][:, t, :], w2_lo[i][:, t, :], t == 0, t == HFT - 1)
                            mm.then_inc(y_done, 1)

                turns(pe, PAIRS, body)


def perceiver_layer(nc, A, out):
    dram = {n: nc.dram_tensor(n + "_scratch", [GROUPS, P, DT * GTOK], F32, kind="Internal").ap()
            for n in ("xT_hi", "xT_lo")}
    dram["y"] = nc.dram_tensor("y_scratch", [GROUPS, P, 2 * D], F32, kind="Internal").ap()
    dram["slots"] = nc.dram_tensor("slots_scratch", [SLOTS + TOKENS, D], F32, kind="Internal").ap()
    dram["results"] = nc.dram_tensor("results_scratch", [SLOTS, D], F32, kind="Internal").ap()
    with ExitStack() as ctx:
        def sb(name, shape, dt=F32):
            return ctx.enter_context(nc.sbuf_tensor(name, shape, dt))

        W = {"ident": sb("ident", [P, P])}
        with ExitStack() as inner:
            for part in ("hi", "lo"):
                for n, shape in (("wq", [P, DT, E]), ("wk", [P, ET, D]), ("wv", [P, DT, ET, 3 * DK]), ("wo", [P, ET, D])):
                    W[f"{n}_{part}"] = inner.enter_context(nc.sbuf_tensor(f"{n}_{part}", shape, F32R))
            for n, cols in (("bq", ET), ("bv", ET), ("cmap", TT * 4 * HT)):
                W[n] = inner.enter_context(nc.sbuf_tensor(n + "_col", [P, cols], F32))
            prepare(nc, A, W, dram)
            attention(nc, A, W, dram)
        W["x2"] = sb("x2", [P, TT, D])
        W["h"] = sb("h", [P, TT, D])
        W["logits"] = sb("logits", [P, TT, 8])
        recurrence(nc, A, W, dram)
        experts(nc, A, W, dram, out)


def columns(v):
    return v.reshape(-1, P).T


def layouts(i):
    import numpy as np
    c = i["ctx_1024"]
    full = c[:, :KC * P, :].reshape(BATCH, KC, P, D)
    return {k: np.ascontiguousarray(v) for k, v in {
        "x": i["x"].reshape(TOKENS, D),
        "wq_nat": i["L0_xattn_Wq"],
        "wqT": i["L0_xattn_Wq"].T,
        "wk": i["L0_xattn_Wk"],
        "wvT": i["L0_xattn_Wv"].T,
        "woT": i["L0_xattn_Wo"].T,
        "bq": columns(i["L0_xattn_bq"]), "bk": columns(i["L0_xattn_bk"]), "bv": columns(i["L0_xattn_bv"]),
        "ctxT": c.reshape(BATCH, KEYS, DT, P).transpose(0, 3, 2, 1),
        "ctxN": full.transpose(0, 2, 1, 3),
        "ctxL": c[:, KC * P:, :],
        "rr": i["L0_attn_Wr"].T, "rk": i["L0_attn_Wk"].T, "rv": i["L0_attn_Wv"].T, "ro": i["L0_attn_Wo"].T,
        "rg": i["L0_attn_Wfr"].T, "fk": i["L0_attn_Wfk"].T, "fv": i["L0_attn_Wfv"].T,
        "ln1_w": i["L0_attn_ln1_w"][None], "ln1_b": i["L0_attn_ln1_b"][None],
        "ln2_w": i["L0_attn_ln2_w"][None], "ln2_b": i["L0_attn_ln2_b"][None],
        "decay_u": np.concatenate([columns(i["L0_attn_decay"]), columns(i["L0_attn_u"])], 1),
        "w1": i["L0_ffn_w1"], "w2": i["L0_ffn_w2"],
        "b1": i["L0_ffn_b1"].reshape(EXPERTS, HFT, P).transpose(2, 0, 1),
        "b2": i["L0_ffn_b2"].reshape(1, -1),
        "gateT": i["L0_ffn_gate_w"].T, "gate_b": i["L0_ffn_gate_b"][None],
    }.items()}


def kernel(**inputs):
    import numpy as np
    import concourse.bacc as bacc
    from concourse.bass_utils import run_bass_kernel_spmd

    arrays = layouts({k: np.asarray(v) for k, v in inputs.items()})
    nc = bacc.Bacc("TRN2", target_bir_lowering=False, num_devices=1, dynamic_dma_scratch_size=4096)
    A = {k: nc.dram_tensor("in_" + k, v.shape, mybir.dt.from_np(v.dtype), kind="ExternalInput").ap() for k, v in arrays.items()}
    out = nc.dram_tensor("out", (TOKENS, D), F32, kind="ExternalOutput").ap()
    perceiver_layer(nc, A, out)
    r = run_bass_kernel_spmd(nc, [{"in_" + k: v for k, v in arrays.items()}], core_ids=[0])
    return r.results[0]["out"].reshape(BATCH, QLEN, D)
```

```python
from contextlib import ExitStack

import concourse.bass as bass
from concourse import mybir

F32 = mybir.dt.float32
F32R = mybir.dt.float32r
U32 = mybir.dt.uint32
ALU = mybir.AluOpType
ACT = mybir.ActivationFunctionType
AX_X = mybir.AxisListType.X

P = 128
BATCH, QLEN, D = 64, 32, 256
KEYS = 257
HEADS, DK = 16, 64
E = HEADS * DK
TOKENS = BATCH * QLEN
DT = D // P
ET = E // P
TT = TOKENS // P
NB = 8
GROUPS = BATCH // NB
GTOK = NB * QLEN
HT = HEADS * QLEN // P
TILES = NB * HT
KC = KEYS // P
KPAD = KEYS + 1
EPS = 1e-5
SCALE = DK ** -0.5



def wait(eng, sem, loop, per, count):
    value = loop * per + count
    if isinstance(value, int) and value <= 0:
        return
    eng.wait_ge(sem, value)


def turns(eng, n, body):
    body(0)
    with eng.Fori(1, n) as i:
        body(i)


def wait_alone(eng, sem, loop, per, count, passed):
    wait(eng, sem, loop, per, count)
    if not isinstance(loop, int):
        eng.sem_inc(passed, 1)


def three_pass(pe, out, w_hi, w_lo, m_hi, m_lo, first, last, **kw):
    pe.matmul(out, w_hi, m_hi, start=first, stop=False, **kw)
    pe.matmul(out, w_hi, m_lo, start=False, stop=False, **kw)
    return pe.matmul(out, w_lo, m_hi, start=False, stop=last, **kw)


def f(ap):
    return ap.bitcast(F32)


def identity(pool, ident, made):
    pool.memset(ident[:, :], 0.0).then_inc(made, 1)
    pool.wait_ge(made, 1)
    pool.affine_select(out=ident[:, :], in_=ident[:, :], compare_op=ALU.not_equal, fill=1.0, base=0,
                       pattern=[[-1, P]], channel_multiplier=1).then_inc(made, 1)


def three_zero(view):
    return view.rearrange("p d t (c k) -> p (d t) c k", k=DK)[:, :, 0:3:2, :]


def prepare(nc, A, W, dram):
    with ExitStack() as ctx:
        def sb(name, shape, dt=F32):
            return ctx.enter_context(nc.sbuf_tensor(name, shape, dt))

        def sem(name):
            return ctx.enter_context(nc.semaphore(name))

        x = sb("x_in", [P, TT, D])
        raw_wq = sb("raw_wq", [P, DT, E])
        raw_wk = sb("raw_wk", [P, ET, D])
        raw_wv = sb("raw_wv", [P, DT * ET, 2, DK])
        raw_wo = sb("raw_wo", [P, ET, D])
        wq_nat = sb("wq_nat", [P, ET, D])
        bk_col = sb("bk_col", [P, ET])
        bk_diag = sb("bk_diag", [P, ET, HEADS])
        stats = sb("ln_stats", [P, TT, 6])
        mv = sb("ln_mv", [P, TT, 2])
        veps = sb("ln_veps", [P, TT])
        power = sb("ln_power", [P, TT])
        rstd = sb("ln_rstd", [P, TT])
        xT_hi = sb("p_xT_hi", [P, 2, DT, GTOK], F32R)
        xT_lo = sb("p_xT_lo", [P, 2, DT, GTOK], F32R)
        g_hi = sb("g_hi", [P, DT, HEADS], F32R)
        g_lo = sb("g_lo", [P, DT, HEADS], F32R)
        g_raw = sb("g_raw", [P, DT, HEADS])
        c0 = sb("c0", [P, HEADS])
        c_tok = sb("c_tok", [P, TT, HEADS])
        ps_t = [ctx.enter_context(nc.psum_tensor(f"ps_t{i}", [P, DT, GTOK], F32)) for i in range(2)]
        ps_g = ctx.enter_context(nc.psum_tensor("ps_g", [P, DT, HEADS], F32))
        ps_c0 = ctx.enter_context(nc.psum_tensor("ps_c0", [P, HEADS], F32))
        ps_c = ctx.enter_context(nc.psum_tensor("ps_c", [P, TT, HEADS], F32))

        x_loaded = sem("x_loaded")
        b_loaded = sem("b_loaded")
        wq_loaded, wk_loaded, wv_loaded, wo_loaded = (sem(n + "_loaded") for n in ("wq", "wk", "wv", "wo"))
        w_hi_done = sem("w_hi_done")
        w_lo_dve = sem("w_lo_dve")
        w_lo_pool = sem("w_lo_pool")
        consts = sem("p_consts")
        diag_made = sem("diag_made")
        stats_done = sem("stats_done")
        mv_done = sem("mv_done")
        veps_done = sem("veps_done")
        rstd_done = sem("rstd_done")
        xn_done = sem("xn_done")
        xT_done = sem("xT_done")
        hi_done = sem("hi_done")
        lo_done = sem("lo_done")
        stored = [sem("stored_even"), sem("stored_odd")]
        g_done = sem("g_done")
        g_split = sem("g_split")
        c_done = sem("c_done")
        c_copied = sem("c_copied")

        with nc.Block() as block:
            @block.sync
            def _(sp):
                sp.dma_start(x[:, :, :], A["x"].rearrange("(t p) d -> p t d", p=P)).then_inc(x_loaded, 16)
                sp.dma_start(wq_nat[:, :, :], A["wq_nat"].rearrange("(t p) d -> p t d", p=P)).then_inc(b_loaded, 16)
                sp.dma_start(bk_col[:, :], A["bk"]).then_inc(b_loaded, 16)
                sp.dma_start(W["bq"][:, :], A["bq"]).then_inc(b_loaded, 16)
                sp.dma_start(W["bv"][:, :], A["bv"]).then_inc(b_loaded, 16)
                sp.dma_start(raw_wq[:, :, :], A["wqT"].rearrange("(t p) e -> p t e", p=P)).then_inc(wq_loaded, 16)
                sp.dma_start(raw_wk[:, :, :], A["wk"].rearrange("(t p) d -> p t d", p=P)).then_inc(wk_loaded, 16)
                sp.dma_start(raw_wv[:, :, :, :].rearrange("p a b c -> p (a b c)").rearrange("p (t e) -> p t e", t=DT),
                             A["wvT"].rearrange("(t p) e -> p t e", p=P)).then_inc(wv_loaded, 16)
                sp.dma_start(raw_wo[:, :, :], A["woT"].rearrange("(t p) d -> p t d", p=P)).then_inc(wo_loaded, 16)
                for g in range(GROUPS):
                    sp.wait_ge(lo_done, g + 1)
                    for name, part in (("xT_hi", xT_hi), ("xT_lo", xT_lo)):
                        sp.dma_start(dram[name][g], f(part[:, g % 2].rearrange("p a b -> p (a b)")))\
                          .then_inc(stored[g % 2], 16)
                for parity in range(2):
                    sp.wait_ge(stored[parity], 16 * GROUPS)

            @block.gpsimd
            def _(pool):
                identity(pool, W["ident"], consts)
                pool.memset(bk_diag[:, :, :], 0.0).then_inc(consts, 1)
                pool.memset(power[:, :], -0.5).then_inc(consts, 1)
                pool.wait_ge(consts, 4)
                pool.wait_ge(veps_done, 1)
                pool.tensor_tensor(rstd[:, :], veps[:, :], power[:, :], ALU.pow).then_inc(rstd_done, 1)
                for part in ("wv_hi", "wv_lo"):
                    pool.memset(f(W[part][:, :, :, DK:2 * DK]), 0.0).then_inc(w_lo_pool, 1)
                pool.wait_ge(w_hi_done, 3)
                pool.tensor_tensor(three_zero(W["wv_lo"][:, :, :, :]), raw_wv[:, :, :, :],
                                   f(three_zero(W["wv_hi"][:, :, :, :])), ALU.subtract).then_inc(w_lo_pool, 1)
                pool.wait_ge(w_hi_done, 4)
                pool.tensor_tensor(W["wo_lo"][:, :, :], raw_wo[:, :, :], f(W["wo_hi"][:, :, :]),
                                   ALU.subtract).then_inc(w_lo_pool, 1)

            @block.vector
            def _(dve):
                dve.wait_ge(b_loaded, 64)
                dve.wait_ge(consts, 3)
                flat = bk_diag[:, :, :].rearrange("p t h -> p (t h)")
                step = HEADS + 2
                dve.tensor_copy(flat[0:DK, 0:(ET - 1) * step + 1:step], bk_col[0:DK, :]).then_inc(diag_made, 1)
                dve.tensor_copy(flat[DK:P, 1:(ET - 1) * step + 2:step], bk_col[DK:P, :]).then_inc(diag_made, 1)
                dve.wait_ge(x_loaded, 16)
                for t in range(TT):
                    dve.bn_stats(stats[:, t, :], x[:, t, :]).then_inc(stats_done, 1)
                for t in range(TT):
                    dve.wait_ge(stats_done, t + 1)
                    dve.bn_aggr(mv[:, t, :], stats[:, t, :]).then_inc(mv_done, 1)
                dve.wait_ge(mv_done, TT)
                dve.tensor_scalar(veps[:, :], mv[:, :, 1], EPS, None, ALU.add).then_inc(veps_done, 1)
                dve.wait_ge(rstd_done, 1)
                for t in range(TT):
                    dve.tensor_scalar(x[:, t, :], x[:, t, :], mv[:, t, 0:1], rstd[:, t:t + 1],
                                      ALU.subtract, ALU.mult).then_inc(xn_done, 1)
                dve.wait_ge(g_done, 1)
                dve.tensor_copy(g_raw[:, :, :], ps_g[:, :, :]).then_inc(g_split, 1)
                dve.tensor_copy(c0[:, :], ps_c0[:, :]).then_inc(g_split, 1)
                dve.wait_ge(g_split, 2)
                dve.tensor_copy(g_hi[:, :, :], g_raw[:, :, :]).then_inc(g_split, 1)
                dve.wait_ge(g_split, 3)
                dve.tensor_tensor(g_lo[:, :, :], g_raw[:, :, :], f(g_hi[:, :, :]), ALU.subtract).then_inc(g_split, 1)
                for g in range(GROUPS):
                    dve.wait_ge(hi_done, g + 1)
                    if g >= 2:
                        dve.wait_ge(stored[g % 2], 32 * (g // 2))
                        dve.wait_ge(c_done, g - 1)
                    dve.tensor_tensor(xT_lo[:, g % 2], ps_t[g % 2][:, :, :], f(xT_hi[:, g % 2]),
                                      ALU.subtract).then_inc(lo_done, 1)
                dve.wait_ge(c_done, GROUPS)
                for t in range(TT):
                    dve.tensor_tensor(c_tok[:, t, :], ps_c[:, t, :], c0[:, :], ALU.add).then_inc(c_copied, 1)
                dve.wait_ge(c_copied, TT)
                dve.tensor_scalar(c_tok[:, :, :], c_tok[:, :, :], SCALE, None, ALU.mult).then_inc(c_copied, 1)
                dve.wait_ge(c_copied, TT + 1)
                for b in range(4):
                    for h in range(4):
                        src = c_tok[32 * b:32 * b + 32, :, :].rearrange("q t (a h) -> q t a h", h=4)[:, :, :, h]
                        dst = W["cmap"][32 * h:32 * h + 32, :].rearrange("q (t b a) -> q t b a", b=4, a=HT)[:, :, b, :]
                        dve.tensor_copy(dst, src).then_inc(c_copied, 1)
                dve.wait_ge(w_hi_done, 1)
                dve.tensor_tensor(W["wq_lo"][:, :, :], raw_wq[:, :, :], f(W["wq_hi"][:, :, :]),
                                  ALU.subtract).then_inc(w_lo_dve, 1)
                dve.wait_ge(w_hi_done, 2)
                dve.tensor_tensor(W["wk_lo"][:, :, :], raw_wk[:, :, :], f(W["wk_hi"][:, :, :]),
                                  ALU.subtract).then_inc(w_lo_dve, 1)

            @block.scalar
            def _(act):
                for g in range(GROUPS):
                    act.wait_ge(xT_done, g + 1)
                    if g >= 2:
                        act.wait_ge(stored[g % 2], 32 * (g // 2))
                        act.wait_ge(c_done, g - 1)
                    act.activation(xT_hi[:, g % 2], ps_t[g % 2][:, :, :], ACT.Copy).then_inc(hi_done, 1)
                act.wait_ge(wq_loaded, 16)
                act.activation(W["wq_hi"][:, :, :], raw_wq[:, :, :], ACT.Copy).then_inc(w_hi_done, 1)
                act.wait_ge(wk_loaded, 16)
                act.activation(W["wk_hi"][:, :, :], raw_wk[:, :, :], ACT.Copy).then_inc(w_hi_done, 1)
                act.wait_ge(wv_loaded, 16)
                act.activation(three_zero(W["wv_hi"][:, :, :, :]), raw_wv[:, :, :, :], ACT.Copy).then_inc(w_hi_done, 1)
                act.wait_ge(wo_loaded, 16)
                act.activation(W["wo_hi"][:, :, :], raw_wo[:, :, :], ACT.Copy).then_inc(w_hi_done, 1)

            @block.tensor
            def _(pe):
                pe.wait_ge(b_loaded, 64)
                pe.wait_ge(diag_made, 2)
                for d in range(DT):
                    for i in range(ET):
                        pe.matmul(ps_g[:, d, :], wq_nat[:, i, d * P:(d + 1) * P], bk_diag[:, i, :],
                                  start=(i == 0), stop=(i == ET - 1))
                for i in range(ET):
                    mm = pe.matmul(ps_c0[:, :], W["bq"][:, i:i + 1].to_broadcast([P, P]), bk_diag[:, i, :],
                                   start=(i == 0), stop=(i == ET - 1))
                mm.then_inc(g_done, 1)

                def q_dot_bk(g):
                    pe.wait_ge(lo_done, g + 1)
                    if g == 0:
                        pe.wait_ge(g_split, 4)
                    for half in range(2):
                        cols = slice(half * P, (half + 1) * P)
                        for d in range(DT):
                            mm = three_pass(pe, ps_c[:, 2 * g + half, :], xT_hi[:, g % 2, d, cols],
                                            xT_lo[:, g % 2, d, cols], g_hi[:, d, :], g_lo[:, d, :],
                                            d == 0, d == DT - 1)
                    mm.then_inc(c_done, 1)

                pe.wait_ge(consts, 2)
                for g in range(GROUPS):
                    pe.wait_ge(xn_done, 2 * g + 2)
                    for half in range(2):
                        for d in range(DT):
                            mm = pe.transpose(ps_t[g % 2][:, d, half * P:(half + 1) * P],
                                              x[:, 2 * g + half, d * P:(d + 1) * P], W["ident"][:, :])
                    mm.then_inc(xT_done, 1)
                    if g >= 1:
                        q_dot_bk(g - 1)
                q_dot_bk(GROUPS - 1)


T_LAG = 3
PV_PARTS = 4
PV_LAG = 9
ROUND_T, REST_T = 0, 1
ROUND_N, REST_N = 6, 7
P_HI, P_LO = (5, 7), (6, 8)
Z_HI, Z_LO = (10, 12), (11, 13)
STEPS = TILES - HT + Z_LO[1] + 1
RING = 8


def due(s, lag):
    b, t = divmod(s - lag, HT)
    return [b] if t == 0 and 0 <= b < NB else []


def both_due(s, lags):
    return [(b, part) for part in range(2) for b in due(s, lags[part])]


def attention(nc, A, W, dram):
    with ExitStack() as ctx:
        def sb(name, shape, dt=F32):
            return ctx.enter_context(nc.sbuf_tensor(name, shape, dt))

        def sem(name):
            return ctx.enter_context(nc.semaphore(name))

        xT_hi = sb("xT_hi", [P, DT, GTOK], F32R)
        xT_lo = sb("xT_lo", [P, DT, GTOK], F32R)
        cg = sb("cg", [P, TILES])
        e_hi = [sb(f"e_hi{i}", [P, GTOK], F32R) for i in range(3)]
        e_lo = [sb(f"e_lo{i}", [P, GTOK], F32R) for i in range(3)]
        qk_hi = sb("qk_hi", [P, DT, NB, HEADS * QLEN], F32R)
        qk_lo = sb("qk_lo", [P, DT, NB, HEADS * QLEN], F32R)
        raw_T = [sb(f"raw_T{i}", [P, DT, KPAD]) for i in range(2)]
        raw_N = [sb(f"raw_N{i}", [P, KC, D]) for i in range(2)]
        raw_L = [sb(f"raw_L{i}", [96, D]) for i in range(2)]
        ctxT_hi = [sb(f"ctxT_hi{i}", [P, DT, KPAD], F32R) for i in range(2)]
        ctxT_lo = [sb(f"ctxT_lo{i}", [P, DT, KPAD], F32R) for i in range(2)]
        ctxN_hi = [sb(f"ctxN_hi{i}", [P, KC, D], F32R) for i in range(2)]
        ctxN_lo = [sb(f"ctxN_lo{i}", [P, KC, D], F32R) for i in range(2)]
        ctxL = [sb(f"ctxL{i}", [96, D], F32R) for i in range(2)]
        probs = sb("probs", [P, RING, KEYS])
        pT_hi = [sb(f"pT_hi{i}", [P, KC, HEADS * QLEN], F32R) for i in range(2)]
        pT_lo = [sb(f"pT_lo{i}", [P, KC, HEADS * QLEN], F32R) for i in range(2)]
        pL = [sb(f"pL{i}", [96, HEADS * QLEN], F32R) for i in range(2)]
        mx = sb("mx", [P, TILES])
        mc = sb("mc", [P, TILES])
        neg = sb("neg", [P, TILES])
        total = sb("total", [P, TILES])
        rec = sb("rec", [P, TILES])
        y = sb("y", [P, 2, D])

        ps_s = [ctx.enter_context(nc.psum_tensor(f"ps_s{i}", [P, 512], F32)) for i in range(2)]
        ps_p = [ctx.enter_context(nc.psum_tensor(f"ps_p{i}", [P, KC, 2 * P], F32)) for i in range(2)]
        ps_l = ctx.enter_context(nc.psum_tensor("ps_l", [P, HEADS * QLEN], F32))
        ps_z = [ctx.enter_context(nc.psum_tensor(f"ps_z{i}", [P, 512], F32)) for i in range(2)]
        ps_x = ctx.enter_context(nc.psum_tensor("ps_x", [P, 2, D], F32))
        ps_x_flat = ps_x[:, :, :].rearrange("p a b -> p (a b)")
        qk_banks = [ps_z[0][:, :], ps_z[1][:, :], ps_x_flat]
        score_banks = [ps_s[0][:, :], ps_s[1][:, :], ps_x_flat]

        pads_zero = sem("pads_zero")
        passed = {n: sem("passed_" + n) for n in ("sp", "pool")}
        xT_in = sem("xT_in")
        rawT_in = [sem("rawT_in_even"), sem("rawT_in_odd")]
        rawN_in = [sem("rawN_in_even"), sem("rawN_in_odd")]
        ctxT_hi_done, ctxN_hi_done, ctxL_hi_done = (sem(f"ctx{n}_hi_done") for n in "TNL")
        ctxT_split, ctxN_split, ctxL_split = (sem(f"ctx{n}_split") for n in "TNL")
        cg_ready = sem("cg_ready")
        q_done, q_hi, q_lo = sem("q_done"), sem("q_hi"), sem("q_lo")
        qk_done, qk_hi_done, qk_lo_done = sem("qk_done"), sem("qk_hi_done"), sem("qk_lo_done")
        sc_done = sem("sc_done")
        max_done = sem("max_done")
        mc_done = sem("mc_done")
        neg_done = sem("neg_done")
        exp_done = sem("exp_done")
        rec_done = sem("rec_done")
        norm_done = sem("norm_done")
        tp_done = sem("tp_done")
        tpL_done = sem("tpL_done")
        pT_hi_done, pT_lo_done = sem("pT_hi_done"), sem("pT_lo_done")
        z_done, z_hi, z_lo = sem("z_done"), sem("z_hi"), sem("z_lo")
        o_done, o_hi, o_lo = sem("o_done"), sem("o_hi"), sem("o_lo")
        wo_done = sem("wo_done")
        y_copied = sem("y_copied")
        y_stored = sem("y_stored")

        ctxT_dram, ctxN_dram, ctxL_dram = A["ctxT"], A["ctxN"], A["ctxL"]

        def groups(eng, body):
            body(0)
            with eng.Fori(1, GROUPS - 1) as g:
                body(g)
            body(GROUPS - 1)

        with nc.Block() as block:
            @block.sync
            def _(sp):
                def load_T(b, i):
                    sp.dma_start(raw_T[i][:, :, 0:KEYS], ctxT_dram[b]).then_inc(rawT_in[i], 16)

                def load_N(b, i):
                    sp.dma_start(raw_N[i][:, :, :], ctxN_dram[b]).then_inc(rawN_in[i], 16)
                    sp.dma_start(raw_L[i][0:65:32, :], ctxL_dram[b].to_broadcast([3, D])).then_inc(rawN_in[i], 16)

                def load_x(g):
                    sp.dma_start(f(xT_hi[:, :, :].rearrange("p a b -> p (a b)")), dram["xT_hi"][g]).then_inc(xT_in, 16)
                    sp.dma_start(f(xT_lo[:, :, :].rearrange("p a b -> p (a b)")), dram["xT_lo"][g]).then_inc(xT_in, 16)

                def body(g):
                    last = isinstance(g, int) and g == GROUPS - 1
                    for b in range(NB):
                        if not (last and b == NB - 1):
                            wait(sp, ctxT_split, g, NB, b)
                            load_T(g * NB + b + 1, (b + 1) % 2)
                        wait_alone(sp, ctxN_split, g, NB, b - 1, passed["sp"])
                        wait_alone(sp, ctxL_split, g, NB, b - 1, passed["sp"])
                        load_N(g * NB + b, b % 2)
                    if not last:
                        wait(sp, q_done, g, ET, ET)
                        load_x(g + 1)
                    wait(sp, y_copied, g, 1, 1)
                    sp.dma_start(dram["y"][g], y[:, :, :].rearrange("p a b -> p (a b)")).then_inc(y_stored, 16)

                sp.wait_ge(pads_zero, 4)
                load_T(0, 0)
                load_x(0)
                groups(sp, body)
                sp.wait_ge(y_stored, 16 * GROUPS)

            @block.gpsimd
            def _(pool):
                def rest_T(g, b):
                    wait(pool, ctxT_hi_done, g, NB, b + 1)
                    pool.tensor_tensor(ctxT_lo[b % 2][:, :, :], raw_T[b % 2][:, :, :], f(ctxT_hi[b % 2][:, :, :]),
                                       ALU.subtract).then_inc(ctxT_split, 1)

                def body(g):
                    last = isinstance(g, int) and g == GROUPS - 1
                    for s in range(STEPS):
                        if s < TILES:
                            wait_alone(pool, rec_done, g, TILES, s + 1, passed["pool"])
                            pool.tensor_scalar(probs[:, s % RING, :], probs[:, s % RING, :], rec[:, s:s + 1], 1.0,
                                               ALU.mult, ALU.mult).then_inc(norm_done, 1)
                        for b in due(s, REST_T):
                            if not (last and b == NB - 1):
                                rest_T(g, b + 1)
                        for b in due(s, ROUND_N):
                            wait(pool, rawN_in[b % 2], g, 32 * NB // 2, 32 * (b // 2 + 1))
                            wait_alone(pool, z_done, g, DT * NB, DT * (b - 1), passed["pool"])
                            pool.tensor_copy(ctxL[b % 2][:, :], raw_L[b % 2][:, :]).then_inc(ctxL_hi_done, 1)
                        for b in due(s, REST_N):
                            wait(pool, ctxN_hi_done, g, NB, b + 1)
                            pool.tensor_tensor(ctxN_lo[b % 2][:, :, :], raw_N[b % 2][:, :, :],
                                               f(ctxN_hi[b % 2][:, :, :]), ALU.subtract).then_inc(ctxN_split, 1)

                for i in range(2):
                    pool.memset(raw_T[i][:, :, KEYS:KPAD], 0.0).then_inc(pads_zero, 1)
                    pool.memset(raw_L[i][:, :], 0.0).then_inc(pads_zero, 1)
                rest_T(0, 0)
                groups(pool, body)

            @block.vector
            def _(dve):
                def body(g):
                    wait(dve, exp_done, g, TILES, 0)
                    dve.tensor_copy(cg[:, :], W["cmap"][:, bass.ts(g, TILES)]).then_inc(cg_ready, 1)
                    def q_part(i):
                        wait(dve, q_hi, g, ET, i + 1)
                        dve.scalar_tensor_tensor(e_lo[i % 3][:, :], ps_s[i % 2][:, 0:GTOK], W["bq"][:, i:i + 1],
                                                 f(e_hi[i % 3][:, :]), ALU.add, ALU.subtract).then_inc(q_lo, 1)

                    q_part(0)
                    for i in range(ET):
                        if i + 1 < ET:
                            q_part(i + 1)
                        for h in (2 * i, 2 * i + 1):
                            wait(dve, qk_hi_done, g, HEADS, h + 1)
                            rows = (slice(None), slice(None), slice(None), slice(h * QLEN, (h + 1) * QLEN))
                            src = qk_banks[h % 3].rearrange("p (d b q) -> p d b q", d=DT, b=NB)
                            dve.tensor_tensor(qk_lo[rows], src, f(qk_hi[rows]), ALU.subtract).then_inc(qk_lo_done, 1)
                    wait(dve, cg_ready, g, 1, 1)
                    for s in range(STEPS):
                        if s < TILES:
                            wait(dve, sc_done, g, TILES, s + 1)
                            dve.tensor_reduce(mx[:, s:s + 1], score_banks[s % 3][:, 0:KEYS], AX_X, ALU.max).then_inc(max_done, 1)
                            wait(dve, max_done, g, TILES, s + 1)
                            dve.tensor_scalar(mc[:, s:s + 1], mx[:, s:s + 1], SCALE, cg[:, s:s + 1],
                                              ALU.mult, ALU.add).then_inc(mc_done, 1)
                            wait(dve, mc_done, g, TILES, s + 1)
                            dve.tensor_scalar(neg[:, s:s + 1], mc[:, s:s + 1], -1.0, cg[:, s:s + 1],
                                              ALU.mult, ALU.add).then_inc(neg_done, 1)
                        for b, dt in both_due(s, Z_LO):
                            wait(dve, z_hi, g, DT * NB, DT * b + dt + 1)
                            dve.tensor_tensor(qk_lo[:, dt, b, :], ps_z[dt][:, :], f(qk_hi[:, dt, b, :]),
                                              ALU.subtract).then_inc(z_lo, 1)
                        for b, half in both_due(s, P_LO):
                            wait(dve, pT_hi_done, g, 3 * NB, 3 * b + half + 1)
                            cols = slice(half * 2 * P, (half + 1) * 2 * P)
                            dve.tensor_tensor(pT_lo[b % 2][:, :, cols], ps_p[half][:, :, :],
                                              f(pT_hi[b % 2][:, :, cols]), ALU.subtract).then_inc(pT_lo_done, 1)
                        if s < TILES:
                            wait(dve, exp_done, g, TILES, s + 1)
                            dve.reciprocal(rec[:, s:s + 1], total[:, s:s + 1]).then_inc(rec_done, 1)
                        for b in due(s, P_LO[1]):
                            wait(dve, pT_hi_done, g, 3 * NB, 3 * b + 3)
                            dve.tensor_tensor(pL[b % 2][32:64, :], ps_l[32:64, :], f(pL[b % 2][32:64, :]),
                                              ALU.subtract).then_inc(pT_lo_done, 1)
                        for b in due(s, REST_N):
                            wait(dve, ctxL_hi_done, g, NB, b + 1)
                            dve.tensor_tensor(ctxL[b % 2][64:96, :], raw_L[b % 2][64:96, :],
                                              f(ctxL[b % 2][64:96, :]), ALU.subtract).then_inc(ctxL_split, 1)
                    for i in range(ET):
                        wait(dve, o_hi, g, ET, i + 1)
                        dve.scalar_tensor_tensor(e_lo[i % 3][:, :], ps_s[i % 2][:, 0:GTOK], W["bv"][:, i:i + 1],
                                                 f(e_hi[i % 3][:, :]), ALU.add, ALU.subtract).then_inc(o_lo, 1)

                groups(dve, body)

            @block.scalar
            def _(act):
                def round_T(g, b):
                    i = b % 2
                    wait(act, rawT_in[i], g, 16 * NB // 2, 16 * (b // 2 + 1))
                    wait(act, sc_done, g, TILES, HT * (b - 1))
                    act.activation(ctxT_hi[i][:, :, :], raw_T[i][:, :, :], ACT.Copy).then_inc(ctxT_hi_done, 1)

                def round_N(g, b):
                    i = b % 2
                    wait(act, rawN_in[i], g, 32 * NB // 2, 32 * (b // 2 + 1))
                    wait(act, z_done, g, DT * NB, DT * (b - 1))
                    act.activation(ctxN_hi[i][:, :, :], raw_N[i][:, :, :], ACT.Copy).then_inc(ctxN_hi_done, 1)

                def body(g):
                    last = isinstance(g, int) and g == GROUPS - 1

                    def q_part(i):
                        wait(act, q_done, g, ET, i + 1)
                        if i >= 3:
                            wait(act, qk_done, g, HEADS, 2 * (i - 3) + 2)
                        act.activation(e_hi[i % 3][:, :], ps_s[i % 2][:, 0:GTOK], ACT.Identity,
                                       bias=W["bq"][:, i:i + 1]).then_inc(q_hi, 1)

                    q_part(0)
                    for i in range(ET):
                        if i + 1 < ET:
                            q_part(i + 1)
                        for h in (2 * i, 2 * i + 1):
                            wait(act, qk_done, g, HEADS, h + 1)
                            rows = (slice(None), slice(None), slice(None), slice(h * QLEN, (h + 1) * QLEN))
                            src = qk_banks[h % 3].rearrange("p (d b q) -> p d b q", d=DT, b=NB)
                            act.activation(qk_hi[rows], src, ACT.Copy).then_inc(qk_hi_done, 1)
                    for s in range(STEPS):
                        if s < TILES:
                            if s >= RING and s % HT == 0:
                                wait(act, tpL_done, g, NB, s // HT - 1)
                            wait(act, neg_done, g, TILES, s + 1)
                            act.activation(probs[:, s % RING, :], score_banks[s % 3][:, 0:KEYS], ACT.Exp, bias=neg[:, s:s + 1],
                                           scale=SCALE, accum_out=total[:, s:s + 1]).then_inc(exp_done, 1)
                        for b, dt in both_due(s, Z_HI):
                            wait(act, z_done, g, DT * NB, DT * b + dt + 1)
                            act.activation(qk_hi[:, dt, b, :], ps_z[dt][:, :], ACT.Copy).then_inc(z_hi, 1)
                        for b, half in both_due(s, P_HI):
                            wait(act, tp_done, g, TILES, HT * b + 2 * half + 2)
                            if half == 0:
                                wait(act, z_done, g, DT * NB, DT * (b - 1))
                            act.activation(pT_hi[b % 2][:, :, half * 2 * P:(half + 1) * 2 * P], ps_p[half][:, :, :],
                                           ACT.Copy).then_inc(pT_hi_done, 1)
                        for b in due(s, P_HI[1]):
                            wait(act, tpL_done, g, NB, b + 1)
                            act.activation(pL[b % 2][:, :], ps_l[0:96, :], ACT.Copy).then_inc(pT_hi_done, 1)
                        for b in due(s, ROUND_T):
                            if not (last and b == NB - 1):
                                round_T(g, b + 1)
                        for b in due(s, ROUND_N):
                            round_N(g, b)
                    for i in range(ET):
                        wait(act, o_done, g, ET, i + 1)
                        if i >= 3:
                            wait(act, wo_done, g, ET, i - 2)
                        act.activation(e_hi[i % 3][:, :], ps_s[i % 2][:, 0:GTOK], ACT.Identity,
                                       bias=W["bv"][:, i:i + 1]).then_inc(o_hi, 1)
                    wait(act, wo_done, g, ET, ET)
                    wait(act, y_stored, g, 16, 0)
                    act.activation(y[:, :, :], ps_x[:, :, :], ACT.Copy).then_inc(y_copied, 1)

                act.wait_ge(pads_zero, 4)
                round_T(0, 0)
                groups(act, body)

            @block.tensor
            def _(pe):
                def body(g):
                    wait(pe, xT_in, g, 32, 32)

                    def q_part(i):
                        if i >= 2:
                            wait(pe, q_lo, g, ET, i - 1)
                        else:
                            wait(pe, o_lo, g, ET, 0)
                        for d in range(DT):
                            mm = three_pass(pe, ps_s[i % 2][:, 0:GTOK], W["wq_hi"][:, d, i * P:(i + 1) * P],
                                            W["wq_lo"][:, d, i * P:(i + 1) * P], xT_hi[:, d, :], xT_lo[:, d, :],
                                            d == 0, d == DT - 1)
                        mm.then_inc(q_done, 1)

                    def qk_part(h):
                        i, rows = h // 2, slice(DK * (h % 2), DK * (h % 2) + DK)
                        if h >= 3:
                            wait(pe, qk_lo_done, g, HEADS, h - 2)
                        elif h == 2:
                            wait(pe, y_copied, g, 1, 0)
                        wait(pe, q_lo, g, ET, i + 1)
                        for d in range(DT):
                            cols = slice(d * P, (d + 1) * P)
                            mm = three_pass(pe, qk_banks[h % 3][:, d * GTOK:(d + 1) * GTOK],
                                            W["wk_hi"][rows, i, cols], W["wk_lo"][rows, i, cols],
                                            e_hi[i % 3][rows, :], e_lo[i % 3][rows, :], True, True)
                        mm.then_inc(qk_done, 1)

                    q_part(0)
                    for i in range(ET):
                        if i + 1 < ET:
                            q_part(i + 1)
                        qk_part(2 * i)
                        qk_part(2 * i + 1)

                    def scores(s):
                        b, t = divmod(s, HT)
                        i, cols = b % 2, slice(t * P, (t + 1) * P)
                        if t == 0:
                            wait(pe, ctxT_split, g, NB, b + 1)
                        if b == 0:
                            wait(pe, qk_lo_done, g, HEADS, 4 * (t + 1) if t != 2 else HEADS - 1)
                        if s >= 3:
                            wait(pe, exp_done, g, TILES, s - 2)
                        for d in range(DT):
                            mm = three_pass(pe, score_banks[s % 3][:, 0:KPAD], qk_hi[:, d, b, cols], qk_lo[:, d, b, cols],
                                            ctxT_hi[i][:, d, :], ctxT_lo[i][:, d, :], d == 0, d == DT - 1)
                        mm.then_inc(sc_done, 1)

                    def transposes(s):
                        b, t = divmod(s, HT)
                        half, cols = t // 2, slice((t % 2) * P, (t % 2 + 1) * P)
                        wait(pe, norm_done, g, TILES, s + 1)
                        if t % 2 == 0:
                            wait(pe, pT_lo_done, g, 3 * NB, 3 * (b - 1) + half + 1)
                        for c in range(KC):
                            mm = pe.transpose(ps_p[half][:, c, cols], probs[:, s % RING, c * P:(c + 1) * P], W["ident"][:, :])
                        mm.then_inc(tp_done, 1)

                    def last_key(b):
                        wait(pe, pT_lo_done, g, 3 * NB, 3 * b)
                        for t in range(HT):
                            mm = pe.transpose(ps_l[0:96, t * P:(t + 1) * P],
                                              probs[:, (HT * b + t) % RING, KC * P:KEYS].to_broadcast([P, 96]), W["ident"][:, :])
                        mm.then_inc(tpL_done, 1)

                    def values(b, part):
                        dt, cols = part // 2, slice((part // 2) * P, (part // 2 + 1) * P)
                        i, out = b % 2, ps_z[part // 2][:, :]
                        if part == 0:
                            wait(pe, pT_lo_done, g, 3 * NB, 3 * (b + 1))
                            wait(pe, ctxN_split, g, NB, b + 1)
                            wait(pe, ctxL_split, g, NB, b + 1)
                        if part % 2 == 0:
                            if b >= 1:
                                wait(pe, z_lo, g, DT * NB, DT * (b - 1) + dt + 1)
                            three_pass(pe, out, ctxN_hi[i][:, 0, cols], ctxN_lo[i][:, 0, cols],
                                       pT_hi[i][:, 0, :], pT_lo[i][:, 0, :], True, False)
                            return
                        three_pass(pe, out, ctxN_hi[i][:, 1, cols], ctxN_lo[i][:, 1, cols],
                                   pT_hi[i][:, 1, :], pT_lo[i][:, 1, :], False, False)
                        pe.matmul(out, ctxL[i][:, cols], pL[i][:, :], start=False, stop=True).then_inc(z_done, 1)

                    for s in range(STEPS):
                        if s < TILES:
                            scores(s)
                        b, part = divmod(s - PV_LAG, PV_PARTS)
                        if 0 <= b < NB:
                            values(b, part)
                        if T_LAG <= s < TILES + T_LAG:
                            transposes(s - T_LAG)
                        for b in due(s, HT - 1 + T_LAG):
                            last_key(b)

                    def o_part(i):
                        if i >= 2:
                            wait(pe, o_lo, g, ET, i - 1)
                        out = ps_s[i % 2][:, 0:GTOK]
                        for h in range(2):
                            head = slice((2 * i + h) * QLEN, (2 * i + h + 1) * QLEN)
                            for d in range(DT):
                                mm = three_pass(pe, out, W["wv_hi"][:, d, i, h * DK:h * DK + P],
                                                W["wv_lo"][:, d, i, h * DK:h * DK + P],
                                                qk_hi[:, d, :, head], qk_lo[:, d, :, head],
                                                h == 0 and d == 0, h == 1 and d == DT - 1)
                        mm.then_inc(o_done, 1)

                    def y_part(i):
                        wait(pe, o_lo, g, ET, i + 1)
                        for tt in range(2):
                            cols = slice(tt * P, (tt + 1) * P)
                            mm = three_pass(pe, ps_x[:, tt, :], e_hi[i % 3][:, cols], e_lo[i % 3][:, cols],
                                            W["wo_hi"][:, i, :], W["wo_lo"][:, i, :],
                                            i == 0 and tt == 0, i == ET - 1 and tt == 1, skip_group_check=True)
                        mm.then_inc(wo_done, 1)

                    wait(pe, z_lo, g, DT * NB, DT * NB)
                    o_part(0)
                    for i in range(ET):
                        if i + 1 < ET:
                            o_part(i + 1)
                        y_part(i)

                groups(pe, body)


CHUNKS = GROUPS
CT = TT // CHUNKS
CTOK = CT * P
CB = CTOK // QLEN
FF = 4 * D
FT = FF // P
PAD = QLEN + 1
RUN = 2 * CB * PAD
LOW = -1e38
R_WEIGHTS = ("rr", "rk", "rv", "ro", "rg")


def recurrence(nc, A, W, dram):
    with ExitStack() as ctx:
        def sb(name, shape, dt=F32):
            return ctx.enter_context(nc.sbuf_tensor(name, shape, dt))

        def sem(name):
            return ctx.enter_context(nc.semaphore(name))

        def bank(name):
            return ctx.enter_context(nc.psum_tensor(name, [P, 512], F32))

        w_hi = {n: sb(n + "_hi", [P, DT, D], F32R) for n in R_WEIGHTS}
        w_lo = {n: sb(n + "_lo", [P, DT, D], F32R) for n in R_WEIGHTS}
        w_hi["fk"], w_lo["fk"] = sb("fk_hi", [P, DT, FF], F32R), sb("fk_lo", [P, DT, FF], F32R)
        w_hi["fv"], w_lo["fv"] = sb("fv_hi", [P, FT, D], F32R), sb("fv_lo", [P, FT, D], F32R)
        names = R_WEIGHTS + ("fk", "fv")
        ln_cols = sb("ln_cols", [P, 4, DT])
        decay_u = sb("decay_u", [P, 2 * DT])
        w_col = sb("w_col", [P, DT])
        w_run = sb("w_run", [P, DT, 2 * CB, PAD])
        gateT = sb("gateT", [P, DT, 8])
        gate_b = sb("gate_b", [P, 8])
        power = sb("r_power", [P, CT])

        zero_rows = sb("zero_rows", [P, 2 * D])
        x_in = sb("x_chunk", [P, CT, D])
        y_in = sb("y_chunk", [P, CT, D])
        n0 = sb("n0", [P, CT, D])
        n1 = sb("n1", [P, CT, D])
        z = sb("z", [P, CT, D])
        n2 = sb("n2", [P, CT, D])
        n3 = sb("n3", [P, CT, D])
        stats = sb("r_stats", [P, 4, CT, 6])
        mv = sb("r_mv", [P, 4, CT, 2])
        veps = sb("r_veps", [P, 4, CT])
        rstd = sb("r_rstd", [P, 4, CT])
        nT, nT_hi, nT_lo = ({st: sb(f"{n}_{st}", [P, DT, CTOK], dt) for st in "AB"}
                            for n, dt in (("nT", F32), ("nT_hi", F32R), ("nT_lo", F32R)))
        hT = sb("hT", [P, DT, CTOK])
        gate_r = sb("gate_r", [P, DT, CTOK])
        k_run, v_run, p_run, f1_run, f2_run, fv_run, a_run, b_run = (
            sb(n + "_run", [P, DT, 2 * CB, PAD]) for n in ("k", "v", "p", "f1", "f2", "fv", "a", "b"))
        pairs = [sb(f"pair{i}", [P, 2, DT, 2 * CB, QLEN]) for i in range(2)]
        e1, e2, t1, t2 = (pairs[i][:, j] for i in range(2) for j in range(2))
        raw = [pairs[i][:, :, :, :, :].rearrange("p a b c d -> p (a b c d)") for i in range(2)]
        rw = sb("rw", [P, DT, CTOK])
        rw_hi = sb("rw_hi", [P, DT, CTOK], F32R)
        rw_lo = sb("rw_lo", [P, DT, CTOK], F32R)
        relu = [sb(f"relu{i}", [P, 2 * CTOK]) for i in range(2)]
        sq = [sb(f"sq{i}", [P, 2 * CTOK]) for i in range(2)]
        kk_hi = sb("kk_hi", [P, FT, CTOK], F32R)
        kk_lo = sb("kk_lo", [P, FT, CTOK], F32R)
        sg = sb("sg", [P, CT, D])
        ps_t = {st: bank("ps_rt" + st) for st in "AB"}
        ps_m = [bank(f"ps_m{i}") for i in range(4)]
        ps_y = bank("ps_fv")
        ps_g = bank("ps_gate")

        passed = {n: sem("r_passed_" + n) for n in ("dve", "pool")}
        zero_set, zeroed = sem("zero_set"), sem("zeroed")
        w_in = [sem("rw_in0"), sem("rw_in1")]
        wr_hi, wr_lo = sem("wr_hi"), sem("wr_lo")
        small_in = sem("small_in")
        w_ready = sem("w_ready")
        pads = sem("pads")
        chunk_in = sem("chunk_in")
        x1_done = sem("x1_done")
        kv_copied = sem("kv_copied")
        r_gated = sem("r_gated")
        scanned, args_done, exps_done, fv_done = (sem("wkv_" + n) for n in ("scanned", "args", "exps", "fv"))
        den_done, e2v_done, num_done, wkv_done = sem("den_done"), sem("e2v_done"), sem("num_done"), sem("wkv_done")
        rw_hi_done, rw_lo_done = sem("rw_hi_done"), sem("rw_lo_done")
        z_added = sem("z_added")
        x1z_done = sem("x1z_done")
        relu_done, sq_done, kk_hi_done, kk_lo_done = (sem(n) for n in ("relu_done", "sq_done", "kk_hi_done", "kk_lo_done"))
        sg_done = sem("sg_done")
        y_done = sem("ff_done")
        gated = sem("ff_gated")
        x2_done = sem("x2_done")
        h_kept = sem("h_kept")
        hT_done, h_copied = sem("hT_done"), sem("h_copied")
        lg_done, lg_copied = sem("lg_done"), sem("lg_copied")
        ln_stats, ln_mv, ln_veps, ln_rstd, ln_done, t_done, t_full, t_hi, t_lo = (
            {st: sem(f"r{n}_{st}") for st in "AB"}
            for n in ("ln_stats", "ln_mv", "ln_veps", "ln_rstd", "ln_done", "t_done", "t_full", "t_hi", "t_lo"))
        mA_done, mB_done = sem("mA_done"), sem("mB_done")

        sizes = {n: DT * D for n in R_WEIGHTS} | {"fk": DT * FF, "fv": FT * D}

        def flat(ap):
            return ap.rearrange("p a b -> p (a b)")

        def of(st, per, count):
            return (per, count if st == "A" else count - per)

        def chunks(eng, body):
            body(0)
            body(1)
            with eng.Fori(2, CHUNKS - 1) as c:
                body(c)
            body(CHUNKS - 1)
            body(CHUNKS)

        def has(st, c):
            return not isinstance(c, int) or (c < CHUNKS if st == "A" else c >= 1)

        def x_tiles(c, st="A"):
            return bass.ds(c * CT - (0 if st == "A" else CT), CT)

        def x_tile(c, st, t):
            return W["x2"][:, bass.ds(c * CT + t - (0 if st == "A" else CT), 1), :].rearrange("p a d -> p (a d)")

        with nc.Block() as block:
            @block.sync
            def _(sp):
                for src, dst in ((A["decay_u"], decay_u[:, :]), (A["gate_b"].to_broadcast([P, 8]), gate_b[:, :]),
                                 (A["ln_cols"], flat(ln_cols[:, :, :])), (A["gateT"].rearrange("(t p) e -> p t e", p=P), gateT[:, :, :])):
                    sp.dma_start(dst, src).then_inc(small_in, 16)
                for j, n in enumerate(names):
                    if j >= 2:
                        sp.wait_ge(wr_lo, j - 1)
                    src = A[n].rearrange("(t p) e -> p t e", p=P)
                    dst = raw[j % 2][:, 0:sizes[n]].rearrange("p (t e) -> p t e", t=src.shape[1])
                    sp.dma_start(dst, src).then_inc(w_in[j % 2], 16)
                sp.wait_ge(zero_set, 1)
                for n in range(SLOTS // (2 * P)):
                    sp.dma_start(dram["slots"][2 * P * n:2 * P * (n + 1), :].rearrange("(p r) d -> p (r d)", r=2),
                                 zero_rows[:, :]).then_inc(zeroed, 16)

                def body(c):
                    wait(sp, x1_done, c, 1, 0)
                    sp.dma_start(x_in[:, :, :], A["x"].rearrange("(c t p) d -> c p t d", p=P, t=CT)[c]).then_inc(chunk_in, 16)
                    sp.dma_start(y_in[:, :, :].rearrange("p t d -> p (t d)"), dram["y"][c]).then_inc(chunk_in, 16)

                turns(sp, CHUNKS, body)
                sp.wait_ge(zeroed, 16 * (SLOTS // (2 * P)))

            @block.gpsimd
            def _(pool):
                pool.memset(power[:, :], -0.5).then_inc(pads, 1)
                pool.memset(k_run[:, :, :, 0:1], LOW).then_inc(pads, 1)
                for run in (v_run, f1_run, f2_run, fv_run):
                    pool.memset(run[:, :, :, 0:1], 0.0).then_inc(pads, 1)
                pool.memset(zero_rows[:, :], 0.0).then_inc(zero_set, 1)
                pool.wait_ge(pads, 1)

                def x1(c):
                    pool.tensor_tensor(W["x2"][:, x_tiles(c), :], x_in[:, :, :], y_in[:, :, :], ALU.add).then_inc(x1_done, 1)

                def body(c):
                    def root(st, n):
                        i = 2 * "AB".index(st) + n
                        wait(pool, ln_veps[st], c, *of(st, 2, n + 1))
                        pool.tensor_tensor(rstd[:, i, :], veps[:, i, :], power[:, :], ALU.pow).then_inc(ln_rstd[st], 1)

                    if has("A", c):
                        root("A", 0)
                    if has("B", c):
                        root("B", 0)
                    if has("A", c):
                        root("A", 1)
                        if not (isinstance(c, int) and c == CHUNKS - 1):
                            wait_alone(pool, chunk_in, c, 32, 64, passed["pool"])
                            x1(c + 1)
                        wait(pool, exps_done, c, 3, 2)
                        pool.tensor_tensor(fv_run[:, :, :, 1:PAD], f2_run[:, :, :, 1:PAD], v_run[:, :, :, 1:PAD],
                                           ALU.mult).then_inc(fv_done, 1)
                        wait(pool, exps_done, c, 3, 3)
                        pool.tensor_tensor(t2, e2, v_run[:, :, :, 1:PAD], ALU.mult).then_inc(e2v_done, 1)
                    if has("B", c):
                        for i in range(FT // 2):
                            wait(pool, kk_hi_done, c, *of("B", FT // 2, i + 1))
                            pair = slice(2 * i, 2 * i + 2)
                            pool.tensor_tensor(flat(kk_lo[:, pair, :]), sq[i % 2][:, :], f(flat(kk_hi[:, pair, :])),
                                               ALU.subtract).then_inc(kk_lo_done, 1)
                        root("B", 1)
                        wait_alone(pool, ln_done["B"], c, *of("B", 2 * CT, 2 * CT), passed["pool"])
                        pool.tensor_copy(W["h"][:, x_tiles(c, "B"), :], n3[:, :, :]).then_inc(h_kept, 1)
                    if has("A", c):
                        wait_alone(pool, z_added, c, 1, 1, passed["pool"])
                        pool.tensor_tensor(W["x2"][:, x_tiles(c), :], W["x2"][:, x_tiles(c), :], z[:, :, :],
                                           ALU.add).then_inc(x1z_done, 1)

                pool.wait_ge(chunk_in, 32)
                x1(0)
                chunks(pool, body)

            @block.vector
            def _(dve):
                dve.wait_ge(w_ready, 1)
                dve.tensor_scalar(w_col[:, :], w_col[:, :], -1.0, None, ALU.mult).then_inc(w_ready, 1)
                dve.memset(w_run[:, :, :, :], 0.0).then_inc(w_ready, 1)
                dve.wait_ge(w_ready, 3)
                for d in range(DT):
                    dve.tensor_scalar(w_run[:, d], w_run[:, d], w_col[:, d:d + 1], None, ALU.add).then_inc(w_ready, 1)
                dve.wait_ge(w_ready, 5)
                dve.memset(w_run[:, :, :, 0:1], LOW).then_inc(w_ready, 1)
                dve.wait_ge(w_ready, 6)
                for j, n in enumerate(names):
                    dve.wait_ge(wr_hi, j + 1)
                    dve.tensor_tensor(flat(w_lo[n][:, :, :]), raw[j % 2][:, 0:sizes[n]], f(flat(w_hi[n][:, :, :])),
                                      ALU.subtract).then_inc(wr_lo, 1)
                dve.wait_ge(wr_lo, len(names))
                dve.wait_ge(small_in, 16 * 4)
                dve.wait_ge(pads, 6)

                def body(c):
                    def moments(st, n, src):
                        i = 2 * "AB".index(st) + n
                        for t in range(CT):
                            dve.bn_stats(stats[:, i, t, :], src(t)).then_inc(ln_stats[st], 1)
                        for t in range(CT):
                            wait_alone(dve, ln_stats[st], c, *of(st, 2 * CT, n * CT + t + 1), passed["dve"])
                            dve.bn_aggr(mv[:, i, t, :], stats[:, i, t, :]).then_inc(ln_mv[st], 1)
                        wait(dve, ln_mv[st], c, *of(st, 2 * CT, (n + 1) * CT))
                        dve.tensor_scalar(veps[:, i, :], mv[:, i, :, 1], EPS, None, ALU.add).then_inc(ln_veps[st], 1)

                    def normalise(st, n, src, dst):
                        i = 2 * "AB".index(st) + n
                        wait(dve, ln_rstd[st], c, *of(st, 2, n + 1))
                        for t in range(CT):
                            dve.tensor_scalar(dst(t), src(t), mv[:, i, t, 0:1], rstd[:, i, t:t + 1],
                                              ALU.subtract, ALU.mult).then_inc(ln_done[st], 1)

                    def transposed_input(st):
                        wait(dve, t_done[st], c, *of(st, 1, 1))
                        i = 2 * "AB".index(st)
                        for d in range(DT):
                            dve.tensor_scalar(nT[st][:, d, :], ps_t[st][:, d * CTOK:(d + 1) * CTOK], ln_cols[:, i, d:d + 1],
                                              ln_cols[:, i + 1, d:d + 1], ALU.mult, ALU.add).then_inc(t_full[st], 1)
                        wait(dve, t_full[st], c, *of(st, DT, DT))
                        wait(dve, t_hi[st], c, *of(st, DT, DT))
                        dve.tensor_tensor(nT_lo[st][:, :, :], nT[st][:, :, :], f(nT_hi[st][:, :, :]), ALU.subtract).then_inc(t_lo[st], 1)

                    steps, before = slice(1, PAD), slice(0, QLEN)

                    def whole(run):
                        return run[:, :, :, :].rearrange("p a b c -> p (a b c)")

                    def exponents():
                        wait(dve, kv_copied, c, 4, 2)
                        dve.tensor_tensor_scan(whole(p_run), whole(w_run), whole(k_run), 0.0, ALU.add, ALU.max).then_inc(scanned, 1)
                        wait(dve, scanned, c, 3, 1)
                        for d in range(DT):
                            dve.scalar_tensor_tensor(f1_run[:, d, :, steps], p_run[:, d, :, before], w_col[:, d:d + 1],
                                                     p_run[:, d, :, steps], ALU.add, ALU.subtract).then_inc(args_done, 1)
                        dve.tensor_tensor(f2_run[:, :, :, steps], k_run[:, :, :, steps], p_run[:, :, :, steps],
                                          ALU.subtract).then_inc(args_done, 1)
                        for d in range(DT):
                            dve.scalar_tensor_tensor(t1[:, d], k_run[:, d, :, steps], decay_u[:, DT + d:DT + d + 1],
                                                     p_run[:, d, :, before], ALU.add, ALU.subtract).then_inc(args_done, 1)
                        wait(dve, args_done, c, 7, 5)
                        dve.tensor_scalar(e1, t1, -1.0, 0.0, ALU.mult, ALU.min).then_inc(args_done, 1)
                        dve.tensor_scalar(e2, t1, 0.0, None, ALU.min).then_inc(args_done, 1)

                    def time_mixing():
                        wait(dve, exps_done, c, 3, 2)
                        dve.tensor_tensor_scan(whole(b_run), whole(f1_run), whole(f2_run), 0.0, ALU.mult, ALU.add).then_inc(scanned, 1)
                        wait(dve, exps_done, c, 3, 3)
                        wait(dve, scanned, c, 3, 2)
                        dve.tensor_tensor(t1, e1, b_run[:, :, :, before], ALU.mult).then_inc(den_done, 1)
                        wait(dve, den_done, c, 3, 1)
                        dve.tensor_tensor(t1, t1, e2, ALU.add).then_inc(den_done, 1)
                        wait(dve, den_done, c, 3, 2)
                        dve.reciprocal(t1, t1).then_inc(den_done, 1)
                        wait(dve, fv_done, c, 1, 1)
                        dve.tensor_tensor_scan(whole(a_run), whole(f1_run), whole(fv_run), 0.0, ALU.mult, ALU.add).then_inc(scanned, 1)
                        wait(dve, scanned, c, 3, 3)
                        dve.tensor_tensor(e1, e1, a_run[:, :, :, before], ALU.mult).then_inc(num_done, 1)
                        wait(dve, num_done, c, 3, 1)
                        wait(dve, e2v_done, c, 1, 1)
                        dve.tensor_tensor(e1, e1, t2, ALU.add).then_inc(num_done, 1)
                        wait(dve, num_done, c, 3, 2)
                        wait(dve, den_done, c, 3, 3)
                        dve.tensor_tensor(e1, e1, t1, ALU.mult).then_inc(num_done, 1)
                        wait(dve, num_done, c, 3, 3)
                        rw_v = rw[:, :, :].rearrange("p d (b t) -> p d b t", t=QLEN)
                        dve.tensor_tensor(rw_v, e1[:, :, 0:CB, :], e1[:, :, CB:2 * CB, ::-1], ALU.add).then_inc(wkv_done, 1)
                        wait(dve, r_gated, c, 1, 1)
                        wait(dve, wkv_done, c, 2, 1)
                        dve.scalar_tensor_tensor(rw[:, :, :], rw[:, :, :], 0.5, gate_r[:, :, :], ALU.mult, ALU.mult).then_inc(wkv_done, 1)

                    if has("A", c):
                        wait_alone(dve, x1_done, c, 1, 1, passed["dve"])
                        moments("A", 0, lambda t: x_tile(c, "A", t))
                    if has("B", c):
                        wait(dve, z_added, c, 1, 0)
                        moments("B", 0, lambda t: z[:, t, :])
                    if has("A", c):
                        normalise("A", 0, lambda t: x_tile(c, "A", t), lambda t: n0[:, t, :])
                        wait(dve, ln_done["A"], c, 2 * CT, CT)
                        moments("A", 1, lambda t: n0[:, t, :])
                    if has("B", c):
                        normalise("B", 0, lambda t: z[:, t, :], lambda t: n2[:, t, :])
                    if has("A", c):
                        normalise("A", 1, lambda t: n0[:, t, :], lambda t: n1[:, t, :])
                    if has("B", c):
                        transposed_input("B")
                    if has("A", c):
                        transposed_input("A")
                        exponents()
                        time_mixing()
                        wait(dve, rw_hi_done, c, 1, 1)
                        dve.tensor_tensor(rw_lo[:, :, :], rw[:, :, :], f(rw_hi[:, :, :]), ALU.subtract).then_inc(rw_lo_done, 1)
                    if has("B", c):
                        wait(dve, sg_done, c, *of("B", 1, 1))
                        wait(dve, y_done, c, *of("B", 1, 1))
                        dve.tensor_tensor(flat(sg[:, :, :]), flat(sg[:, :, :]), ps_y[:, :], ALU.mult).then_inc(gated, 1)
                        wait(dve, x1z_done, c, *of("B", 1, 1))
                        wait(dve, gated, c, *of("B", 1, 1))
                        dve.tensor_tensor(W["x2"][:, x_tiles(c, "B"), :], W["x2"][:, x_tiles(c, "B"), :], sg[:, :, :],
                                          ALU.add).then_inc(x2_done, 1)
                        wait_alone(dve, x2_done, c, *of("B", 1, 1), passed["dve"])
                        moments("B", 1, lambda t: x_tile(c, "B", t))
                    if has("A", c):
                        wait(dve, mA_done, c, 4, 4)
                        dve.tensor_tensor(flat(z[:, :, :]), flat(n0[:, :, :]), ps_m[0][:, :], ALU.add).then_inc(z_added, 1)
                    if has("B", c):
                        wait(dve, h_kept, c, *of("B", 1, 0))
                        normalise("B", 1, lambda t: x_tile(c, "B", t), lambda t: n3[:, t, :])

                chunks(dve, body)
                dve.wait_ge(lg_copied, CHUNKS)
                dve.tensor_tensor(W["logits"][:, :, :], W["logits"][:, :, :], gate_b[:, :].unsqueeze(1).to_broadcast([P, TT, 8]),
                                  ALU.add).then_inc(lg_copied, 1)

            @block.scalar
            def _(act):
                act.wait_ge(small_in, 16 * 4)
                act.activation(w_col[:, :], decay_u[:, 0:DT], ACT.Exp).then_inc(w_ready, 1)
                for j, n in enumerate(names):
                    act.wait_ge(w_in[j % 2], 16 * (j // 2 + 1))
                    act.activation(flat(w_hi[n][:, :, :]), raw[j % 2][:, 0:sizes[n]], ACT.Copy).then_inc(wr_hi, 1)

                def body(c):
                    def transposed_input(st):
                        for d in range(DT):
                            wait(act, t_full[st], c, *of(st, DT, d + 1))
                            act.activation(nT_hi[st][:, d, :], nT[st][:, d, :], ACT.Copy).then_inc(t_hi[st], 1)

                    if has("B", c):
                        transposed_input("B")
                    if has("A", c):
                        transposed_input("A")
                        for j, run in enumerate((k_run, v_run)):
                            wait(act, mA_done, c, 4, j + 1)
                            src = ps_m[j][:, :].rearrange("p (d b t) -> p d b t", d=DT, t=QLEN)
                            act.activation(run[:, :, 0:CB, 1:PAD], src, ACT.Copy).then_inc(kv_copied, 1)
                            act.activation(run[:, :, CB:2 * CB, QLEN:0:-1], src, ACT.Copy).then_inc(kv_copied, 1)
                        for tile, need in ((f1_run[:, :, :, 1:PAD], 2), (f2_run[:, :, :, 1:PAD], 3), (pairs[0][:, :, :, :, :], 7)):
                            wait(act, args_done, c, 7, need)
                            act.activation(tile, tile, ACT.Exp).then_inc(exps_done, 1)
                        wait(act, mA_done, c, 4, 3)
                        act.activation(flat(gate_r[:, :, :]), ps_m[2][:, :], ACT.Sigmoid).then_inc(r_gated, 1)
                    if has("B", c):
                        wait(act, mB_done, c, *of("B", 5, 1))
                        wait(act, x2_done, c, *of("B", 1, 0))
                        act.activation(flat(sg[:, :, :]), ps_m[3][:, :], ACT.Sigmoid).then_inc(sg_done, 1)
                        for i in range(FT // 2):
                            wait(act, mB_done, c, *of("B", 5, 2 + i))
                            act.activation(relu[i % 2][:, :], ps_m[i][:, :], ACT.Relu).then_inc(relu_done, 1)
                            wait(act, relu_done, c, *of("B", FT // 2, i + 1))
                            if i >= 2:
                                wait(act, kk_lo_done, c, *of("B", FT // 2, i - 1))
                            act.activation(sq[i % 2][:, :], relu[i % 2][:, :], ACT.Square).then_inc(sq_done, 1)
                            wait(act, sq_done, c, *of("B", FT // 2, i + 1))
                            act.activation(flat(kk_hi[:, 2 * i:2 * i + 2, :]), sq[i % 2][:, :], ACT.Copy).then_inc(kk_hi_done, 1)
                    if has("A", c):
                        wait(act, wkv_done, c, 2, 2)
                        act.activation(rw_hi[:, :, :], rw[:, :, :], ACT.Copy).then_inc(rw_hi_done, 1)
                    if has("B", c):
                        wait(act, hT_done, c, *of("B", 1, 1))
                        act.activation(flat(hT[:, :, :]), ps_t["B"][:, :], ACT.Copy).then_inc(h_copied, 1)
                        wait(act, lg_done, c, *of("B", 1, 1))
                        act.activation(W["logits"][:, x_tiles(c, "B"), :], ps_g[:, 0:CT * 8].rearrange("p (t e) -> p t e", e=8),
                                       ACT.Copy).then_inc(lg_copied, 1)

                chunks(act, body)

            @block.tensor
            def _(pe):
                pe.wait_ge(wr_lo, len(names))

                def body(c):
                    def transpose(st, n_in, done):
                        for d in range(DT):
                            for t in range(CT):
                                mm = pe.transpose(ps_t[st][:, d * CTOK + t * P:d * CTOK + (t + 1) * P],
                                                  n_in[:, t, d * P:(d + 1) * P], W["ident"][:, :])
                        mm.then_inc(done, 1)

                    def channels(st, bank, n, col, done):
                        for j in range(2):
                            for d in range(DT):
                                cols = slice((col + j) * P, (col + j + 1) * P)
                                mm = three_pass(pe, ps_m[bank][:, j * CTOK:(j + 1) * CTOK], w_hi[n][:, d, cols], w_lo[n][:, d, cols],
                                                nT_hi[st][:, d, :], nT_lo[st][:, d, :], d == 0, d == DT - 1)
                        mm.then_inc(done, 1)

                    def tokens(out, n, hi, lo, depth, done):
                        for t in range(CT):
                            cols = slice(t * P, (t + 1) * P)
                            for d in range(depth):
                                mm = three_pass(pe, out[:, t * D:(t + 1) * D], hi[:, d, cols], lo[:, d, cols],
                                                w_hi[n][:, d, :], w_lo[n][:, d, :], d == 0, d == depth - 1)
                        mm.then_inc(done, 1)

                    if has("B", c):
                        wait(pe, ln_done["B"], c, *of("B", 2 * CT, CT))
                        wait(pe, h_copied, c, *of("B", 1, 0))
                        transpose("B", n2, t_done["B"])
                    if has("A", c):
                        wait(pe, ln_done["A"], c, 2 * CT, 2 * CT)
                        wait(pe, t_lo["A"], c, 1, 0)
                        transpose("A", n1, t_done["A"])
                        wait(pe, t_lo["A"], c, 1, 1)
                        wait(pe, z_added, c, 1, 0)
                        channels("A", 0, "rk", 0, mA_done)
                        wait(pe, relu_done, c, *of("B", FT // 2, 0))
                        channels("A", 1, "rv", 0, mA_done)
                        channels("A", 2, "rr", 0, mA_done)
                    if has("B", c):
                        wait(pe, t_lo["B"], c, *of("B", 1, 1))
                        wait(pe, relu_done, c, *of("B", FT // 2, 0))
                        tokens(ps_m[3], "rg", nT_hi["B"], nT_lo["B"], DT, mB_done)
                        for i in range(FT // 2):
                            if i == 3:
                                wait(pe, sg_done, c, *of("B", 1, 1))
                            elif has("A", c):
                                wait(pe, *((kv_copied, c, 4, 2), (kv_copied, c, 4, 4), (r_gated, c, 1, 1))[i])
                            channels("B", i, "fk", 2 * i, mB_done)
                        wait(pe, kk_lo_done, c, *of("B", FT // 2, FT // 2))
                        wait(pe, gated, c, *of("B", 1, 0))
                        tokens(ps_y, "fv", kk_hi, kk_lo, FT, y_done)
                    if has("A", c):
                        wait(pe, rw_lo_done, c, 1, 1)
                        if has("B", c):
                            wait(pe, relu_done, c, *of("B", FT // 2, 1))
                        else:
                            wait(pe, kv_copied, c, 4, 2)
                        tokens(ps_m[0], "ro", rw_hi, rw_lo, DT, mA_done)
                    if has("B", c):
                        wait(pe, ln_done["B"], c, *of("B", 2 * CT, 2 * CT))
                        transpose("B", n3, hT_done)
                        wait(pe, h_copied, c, *of("B", 1, 1))
                        wait(pe, lg_copied, c, *of("B", 1, 0))
                        for t in range(CT):
                            for d in range(DT):
                                mm = pe.matmul(ps_g[:, t * 8:(t + 1) * 8], hT[:, d, t * P:(t + 1) * P], gateT[:, d, :],
                                               start=(d == 0), stop=(d == DT - 1))
                        mm.then_inc(lg_done, 1)

                chunks(pe, body)


EXPERTS = 8
CAP = -(-TOKENS * 5 // (4 * EXPERTS))
SLOTS = EXPERTS * CAP
HF = 4 * D
HFT = HF // P
SPLIT = [(0, P), (P, P), (2 * P, CAP - 2 * P)]


def experts(nc, A, W, dram, out):
    with ExitStack() as ctx:
        def sb(name, shape, dt=F32):
            return ctx.enter_context(nc.sbuf_tensor(name, shape, dt))

        def sem(name):
            return ctx.enter_context(nc.semaphore(name))

        def bank(name):
            return ctx.enter_context(nc.psum_tensor(name, [P, 512], F32))

        x2, h, logits = W["x2"], W["h"], W["logits"]
        tri = sb("tri", [P, P])
        ones = sb("ones", [P, P])
        e_iota = sb("e_iota", [P, EXPERTS])
        e_int = sb("e_int", [P, EXPERTS], mybir.dt.int32)
        tok = sb("tok", [P, TT])
        tok_int = sb("tok_int", [P, TT], mybir.dt.int32)
        zeros = sb("zeros16", [P, TT])
        m, total, rec, top, idx, pos, keep, slot, far, tw = (
            sb("gt_" + n, [P, TT]) for n in ("m", "total", "rec", "top", "idx", "pos", "keep", "slot", "far", "tw"))
        prob, eq, hot, tot, run, pre = (sb("gt_" + n, [P, TT, EXPERTS]) for n in ("prob", "eq", "hot", "tot", "run", "pre"))
        scatter_to = sb("scatter_to", [P, TT], U32)
        gather_from = sb("gather_from", [P, TT], U32)

        raw1 = [sb(f"raw1_{i}", [P, DT * HF]) for i in range(2)]
        raw2 = [sb(f"raw2_{i}", [P, HFT * D]) for i in range(2)]
        w1_hi, w1_lo = ([sb(f"w1_{p}{i}", [P, DT, HF], F32R) for i in range(2)] for p in ("hi", "lo"))
        w2_hi, w2_lo = ([sb(f"w2_{p}{i}", [P, HFT, D], F32R) for i in range(2)] for p in ("hi", "lo"))
        b1 = sb("b1", [P, EXPERTS, HFT])
        b2 = sb("b2", [P, EXPERTS, D])
        rows = [sb(f"rows{i}", [P, 3, D]) for i in range(2)]
        rT_hi = sb("rT_hi", [P, DT, CAP], F32R)
        rT_lo = sb("rT_lo", [P, DT, CAP], F32R)
        hid = [sb(f"hid{i}", [P, CAP]) for i in range(2)]
        hid_hi = sb("hid_hi", [P, HFT, CAP], F32R)
        hid_lo = sb("hid_lo", [P, HFT, CAP], F32R)
        eo = [sb(f"eo{i}", [P, 3, D]) for i in range(2)]

        ps_t = [bank("ps_et0"), bank("ps_et1")]
        ps_h = [bank(f"ps_h{i}") for i in range(3)]
        ps_y = [bank("ps_ey0"), bank("ps_ey1")]
        ps_c = bank("ps_count")

        masks = sem("masks")
        consts = sem("consts")
        b_in = sem("b_in")
        g_step = sem("gate_step")
        g_exp = sem("gate_exp")
        counted = sem("counted")
        slots_ready = sem("slots_ready")
        scattered = sem("scattered")
        w_in = [sem("ew_in0"), sem("ew_in1")]
        w_hi_done, w_lo_done = sem("ew_hi"), sem("ew_lo")
        rows_in = [sem("rows_in0"), sem("rows_in1")]
        t_done, t_hi, t_lo = sem("et_done"), sem("et_hi"), sem("et_lo")
        h_done, h_relu, h_hi, h_lo = sem("eh_done"), sem("eh_relu"), sem("eh_hi"), sem("eh_lo")
        y_done, y_copied = sem("ey_done"), sem("ey_copied")
        eo_stored = [sem("eo_stored0"), sem("eo_stored1")]
        gathered = sem("gathered")
        summed = sem("summed")
        stored = sem("out_stored")

        PAIRS = EXPERTS // 2

        def flat(ap):
            return ap.rearrange("p a b -> p (a b)")

        with nc.Block() as block:
            @block.sync
            def _(sp):
                sp.dma_start(b1[:, :, :], A["b1"]).then_inc(b_in, 16)
                sp.dma_start(flat(b2[:, :, :]), A["b2"].to_broadcast([P, EXPERTS * D])).then_inc(b_in, 16)
                def body(j):
                    for i in range(2):
                        e = 2 * j + i
                        wait(sp, w_lo_done, j, 4, 2 * i - 2 + 2 * (1 - i))
                        sp.dma_start(raw1[i][:, :].rearrange("p (t n) -> p t n", t=DT),
                                     A["w1"].rearrange("e (t p) n -> e p t n", p=P)[e]).then_inc(w_in[i], 16)
                        sp.dma_start(raw2[i][:, :].rearrange("p (t n) -> p t n", t=HFT),
                                     A["w2"].rearrange("e (t p) n -> e p t n", p=P)[e]).then_inc(w_in[i], 16)
                        sp.wait_ge(scattered, 16 * TT)
                        wait(sp, t_done, j, 4, 0)
                        slots = dram["slots"][0:SLOTS, :].rearrange("(e s) d -> e s d", s=CAP)[e]
                        sp.dma_start(rows[i][:, 0:2, :], slots[0:2 * P, :].rearrange("(k p) d -> p k d", p=P)).then_inc(rows_in[i], 16)
                        sp.dma_start(rows[i][0:CAP - 2 * P, 2, :], slots[2 * P:CAP, :]).then_inc(rows_in[i], 16)

                turns(sp, PAIRS, body)

            @block.gpsimd
            def _(pool):
                pool.memset(ones[:, :], 1.0).then_inc(masks, 1)
                pool.memset(zeros[:, :], 0.0).then_inc(masks, 1)
                pool.iota(e_int[:, :], [[1, EXPERTS]], base=0, channel_multiplier=0).then_inc(masks, 1)
                pool.iota(tok_int[:, :], [[P, TT]], base=0, channel_multiplier=1).then_inc(masks, 1)
                pool.wait_ge(masks, 4)
                pool.affine_select(out=tri[:, :], in_=ones[:, :], compare_op=ALU.is_ge, fill=0.0, base=0,
                                   pattern=[[1, P]], channel_multiplier=-1).then_inc(masks, 1)
                pool.tensor_copy(e_iota[:, :], e_int[:, :]).then_inc(consts, 1)
                pool.tensor_copy(tok[:, :], tok_int[:, :]).then_inc(consts, 1)
                pool.wait_ge(slots_ready, 2)
                for t in range(TT):
                    pool.indirect_dma_start(out=dram["slots"], out_offset=bass.IndirectOffsetOnAxis(scatter_to[:, t:t + 1], 0),
                                            in_=h[:, t, :], in_offset=None).then_inc(scattered, 16)
                def body(j):
                    for i in range(2):
                        for k, (raw, hi, lo) in enumerate(((raw1, w1_hi, w1_lo), (raw2, w2_hi, w2_lo))):
                            wait(pool, w_hi_done, j, 4, 2 * i + k + 1)
                            pool.tensor_tensor(flat(lo[i][:, :, :]), raw[i][:, :], f(flat(hi[i][:, :, :])),
                                               ALU.subtract).then_inc(w_lo_done, 1)

                turns(pool, PAIRS, body)
                for i in range(2):
                    pool.wait_ge(eo_stored[i], 32 * PAIRS)
                for t in range(TT):
                    pool.indirect_dma_start(out=h[:, t, :], out_offset=None, in_=dram["results"],
                                            in_offset=bass.IndirectOffsetOnAxis(gather_from[:, t:t + 1], 0)).then_inc(gathered, 16)

            @block.vector
            def _(dve):
                done = 0

                def step(op):
                    nonlocal done
                    op.then_inc(g_step, 1)
                    done += 1
                    dve.wait_ge(g_step, done)

                def over(v):
                    return v[:, :].unsqueeze(2).to_broadcast([P, TT, EXPERTS])

                iota = e_iota[:, :].unsqueeze(1).to_broadcast([P, TT, EXPERTS])
                dve.wait_ge(consts, 2)
                step(dve.tensor_reduce(m[:, :], logits[:, :, :], AX_X, ALU.max))
                step(dve.tensor_tensor(prob[:, :, :], logits[:, :, :], over(m), ALU.subtract))
                dve.wait_ge(g_exp, 1)
                step(dve.tensor_reduce(total[:, :], prob[:, :, :], AX_X, ALU.add))
                step(dve.reciprocal(rec[:, :], total[:, :]))
                step(dve.tensor_tensor(prob[:, :, :], prob[:, :, :], over(rec), ALU.mult))
                step(dve.tensor_reduce(top[:, :], prob[:, :, :], AX_X, ALU.max))
                step(dve.tensor_tensor(eq[:, :, :], prob[:, :, :], over(top), ALU.is_equal))
                step(dve.tensor_scalar(eq[:, :, :], eq[:, :, :], -float(EXPERTS), float(EXPERTS), ALU.mult, ALU.add))
                step(dve.tensor_tensor(eq[:, :, :], eq[:, :, :], iota, ALU.add))
                step(dve.tensor_reduce(idx[:, :], eq[:, :, :], AX_X, ALU.min))
                step(dve.tensor_tensor(hot[:, :, :], iota, over(idx), ALU.is_equal))
                dve.wait_ge(counted, 2)
                step(dve.tensor_copy(tot[:, :, :], ps_c[:, P:2 * P].rearrange("p (t e) -> p t e", e=EXPERTS)))
                for e in range(EXPERTS):
                    dve.tensor_tensor_scan(run[:, :, e], tot[:, :, e], zeros[:, :], 0.0, ALU.add, ALU.add).then_inc(g_step, 1)
                done += EXPERTS
                dve.wait_ge(g_step, done)
                step(dve.tensor_tensor(run[:, :, :], run[:, :, :], tot[:, :, :], ALU.subtract))
                step(dve.tensor_tensor(pre[:, :, :], run[:, :, :], ps_c[:, 0:P].rearrange("p (t e) -> p t e", e=EXPERTS), ALU.add))
                step(dve.tensor_tensor(pre[:, :, :], pre[:, :, :], hot[:, :, :], ALU.mult))
                step(dve.tensor_reduce(pos[:, :], pre[:, :, :], AX_X, ALU.add))
                step(dve.tensor_scalar(pos[:, :], pos[:, :], 1.0, None, ALU.subtract))
                step(dve.tensor_scalar(keep[:, :], pos[:, :], float(CAP), None, ALU.is_lt))
                step(dve.tensor_tensor(tw[:, :], top[:, :], keep[:, :], ALU.mult))
                step(dve.tensor_tensor(pos[:, :], pos[:, :], keep[:, :], ALU.mult))
                step(dve.tensor_scalar(slot[:, :], idx[:, :], float(CAP), None, ALU.mult))
                step(dve.tensor_tensor(slot[:, :], slot[:, :], pos[:, :], ALU.add))
                dve.tensor_copy(gather_from[:, :], slot[:, :]).then_inc(slots_ready, 1)
                step(dve.tensor_scalar(far[:, :], tok[:, :], float(SLOTS), None, ALU.add))
                step(dve.tensor_tensor(slot[:, :], slot[:, :], far[:, :], ALU.subtract))
                step(dve.tensor_tensor(slot[:, :], slot[:, :], keep[:, :], ALU.mult))
                step(dve.tensor_tensor(slot[:, :], slot[:, :], far[:, :], ALU.add))
                dve.tensor_copy(scatter_to[:, :], slot[:, :]).then_inc(slots_ready, 1)

                dve.wait_ge(b_in, 32)
                def body(j):
                    for i in range(2):
                        for d in range(DT):
                            wait(dve, t_hi, j, 4, 2 * i + d + 1)
                            dve.tensor_tensor(rT_lo[:, d, :], ps_t[d][:, 0:CAP], f(rT_hi[:, d, :]), ALU.subtract).then_inc(t_lo, 1)
                        for k in range(HFT):
                            wait(dve, h_relu, j, 2 * HFT, HFT * i + k + 1)
                            dve.tensor_copy(hid_hi[:, k, :], hid[k % 2][:, :]).then_inc(h_hi, 1)
                            wait(dve, h_hi, j, 2 * HFT, HFT * i + k + 1)
                            dve.tensor_tensor(hid_lo[:, k, :], hid[k % 2][:, :], f(hid_hi[:, k, :]), ALU.subtract).then_inc(h_lo, 1)
                        wait(dve, eo_stored[i], j, 32, 0)
                        bias = b2[:, bass.ds(2 * j + i, 1), :].rearrange("p a d -> p (a d)")
                        for k in range(3):
                            wait(dve, y_done, j, 6, 3 * i + (2, 2, 3)[k])
                            r = slice(0, P) if k < 2 else slice(3 * P - CAP, P)
                            dve.tensor_tensor(eo[i][r, k, :], ps_y[k // 2][r, (k % 2) * D:(k % 2 + 1) * D], bias[r, :],
                                              ALU.add).then_inc(y_copied, 1)

                turns(dve, PAIRS, body)
                for t in range(TT):
                    dve.wait_ge(gathered, 16 * TT)
                    dve.scalar_tensor_tensor(x2[:, t, :], h[:, t, :], tw[:, t:t + 1], x2[:, t, :], ALU.mult, ALU.add).then_inc(summed, 1)

            @block.scalar
            def _(act):
                act.wait_ge(g_step, 2)
                act.activation(prob[:, :, :], prob[:, :, :], ACT.Exp).then_inc(g_exp, 1)
                act.wait_ge(b_in, 32)
                def body(j):
                    for i in range(2):
                        wait(act, w_in[i], j, 32, 32)
                        wait(act, y_done, j, 6, 0)
                        act.activation(flat(w1_hi[i][:, :, :]), raw1[i][:, :], ACT.Copy).then_inc(w_hi_done, 1)
                        act.activation(flat(w2_hi[i][:, :, :]), raw2[i][:, :], ACT.Copy).then_inc(w_hi_done, 1)
                        for d in range(DT):
                            wait(act, t_done, j, 4, 2 * i + d + 1)
                            act.activation(rT_hi[:, d, :], ps_t[d][:, 0:CAP], ACT.Copy).then_inc(t_hi, 1)
                        for k in range(HFT):
                            wait(act, h_done, j, 2 * HFT, HFT * i + k + 1)
                            if k >= 2:
                                wait(act, h_lo, j, 2 * HFT, HFT * i + k - 1)
                            act.activation(hid[k % 2][:, :], ps_h[k % 3][:, 0:CAP], ACT.Relu,
                                           bias=b1[:, bass.ds(2 * j + i, 1), k]).then_inc(h_relu, 1)
                        e = 2 * j + i
                        wait(act, y_copied, j, 6, 3 * i + 3)
                        slots = dram["results"].rearrange("(e s) d -> e s d", s=CAP)[e]
                        act.dma_start(slots[0:2 * P, :].rearrange("(k p) d -> p k d", p=P), eo[i][:, 0:2, :]).then_inc(eo_stored[i], 16)
                        act.dma_start(slots[2 * P:CAP, :], eo[i][3 * P - CAP:P, 2, :]).then_inc(eo_stored[i], 16)

                turns(act, PAIRS, body)
                for q in range(4):
                    n = TT // 4
                    act.wait_ge(summed, n * (q + 1))
                    act.dma_start(out.rearrange("(t p) d -> p t d", p=P)[:, q * n:(q + 1) * n, :],
                                  x2[:, q * n:(q + 1) * n, :]).then_inc(stored, 16)
                act.wait_ge(stored, 64)

            @block.tensor
            def _(pe):
                pe.wait_ge(masks, 5)
                pe.wait_ge(g_step, 11)
                hot_flat = flat(hot[:, :, :])
                pe.matmul(ps_c[:, 0:P], tri[:, :], hot_flat, start=True, stop=True).then_inc(counted, 1)
                pe.matmul(ps_c[:, P:2 * P], ones[:, :], hot_flat, start=True, stop=True).then_inc(counted, 1)
                def body(j):
                    for i in range(2):
                        wait(pe, rows_in[i], j, 32, 32)
                        for d in range(DT):
                            for k, (at, n) in enumerate(SPLIT):
                                mm = pe.transpose(ps_t[d][:, at:at + n], rows[i][0:n, k, d * P:(d + 1) * P], W["ident"][0:n, 0:n])
                            mm.then_inc(t_done, 1)
                        wait(pe, w_lo_done, j, 4, 2 * i + 2)
                        wait(pe, t_lo, j, 4, 2 * i + 2)
                        for k in range(HFT):
                            if k >= 3:
                                wait(pe, h_relu, j, 2 * HFT, HFT * i + k - 2)
                            for d in range(DT):
                                cols = slice(k * P, (k + 1) * P)
                                mm = three_pass(pe, ps_h[k % 3][:, 0:CAP], w1_hi[i][:, d, cols], w1_lo[i][:, d, cols],
                                                rT_hi[:, d, :], rT_lo[:, d, :], d == 0, d == DT - 1)
                            mm.then_inc(h_done, 1)
                        wait(pe, h_lo, j, 2 * HFT, HFT * (i + 1))
                        wait(pe, y_copied, j, 6, 3 * i)
                        for k, at in enumerate((0, P, CAP - P)):
                            for t in range(HFT):
                                mm = three_pass(pe, ps_y[k // 2][:, (k % 2) * D:(k % 2 + 1) * D], hid_hi[:, t, at:at + P],
                                                hid_lo[:, t, at:at + P], w2_hi[i][:, t, :], w2_lo[i][:, t, :], t == 0, t == HFT - 1)
                            mm.then_inc(y_done, 1)

                turns(pe, PAIRS, body)


def perceiver_layer(nc, A, out):
    dram = {n: nc.dram_tensor(n + "_scratch", [GROUPS, P, DT * GTOK], F32, kind="Internal").ap()
            for n in ("xT_hi", "xT_lo")}
    dram["y"] = nc.dram_tensor("y_scratch", [GROUPS, P, 2 * D], F32, kind="Internal").ap()
    dram["slots"] = nc.dram_tensor("slots_scratch", [SLOTS + TOKENS, D], F32, kind="Internal").ap()
    dram["results"] = nc.dram_tensor("results_scratch", [SLOTS, D], F32, kind="Internal").ap()
    with ExitStack() as ctx:
        def sb(name, shape, dt=F32):
            return ctx.enter_context(nc.sbuf_tensor(name, shape, dt))

        W = {"ident": sb("ident", [P, P])}
        with ExitStack() as inner:
            for part in ("hi", "lo"):
                for n, shape in (("wq", [P, DT, E]), ("wk", [P, ET, D]), ("wv", [P, DT, ET, 3 * DK]), ("wo", [P, ET, D])):
                    W[f"{n}_{part}"] = inner.enter_context(nc.sbuf_tensor(f"{n}_{part}", shape, F32R))
            for n, cols in (("bq", ET), ("bv", ET), ("cmap", TT * 4 * HT)):
                W[n] = inner.enter_context(nc.sbuf_tensor(n + "_col", [P, cols], F32))
            prepare(nc, A, W, dram)
            attention(nc, A, W, dram)
        W["x2"] = sb("x2", [P, TT, D])
        W["h"] = sb("h", [P, TT, D])
        W["logits"] = sb("logits", [P, TT, 8])
        recurrence(nc, A, W, dram)
        experts(nc, A, W, dram, out)


def columns(v):
    return v.reshape(-1, P).T


def layouts(i):
    import numpy as np
    c = i["ctx_1024"]
    full = c[:, :KC * P, :].reshape(BATCH, KC, P, D)
    return {k: np.ascontiguousarray(v) for k, v in {
        "x": i["x"].reshape(TOKENS, D),
        "wq_nat": i["L0_xattn_Wq"],
        "wqT": i["L0_xattn_Wq"].T,
        "wk": i["L0_xattn_Wk"],
        "wvT": i["L0_xattn_Wv"].T,
        "woT": i["L0_xattn_Wo"].T,
        "bq": columns(i["L0_xattn_bq"]), "bk": columns(i["L0_xattn_bk"]), "bv": columns(i["L0_xattn_bv"]),
        "ctxT": c.reshape(BATCH, KEYS, DT, P).transpose(0, 3, 2, 1),
        "ctxN": full.transpose(0, 2, 1, 3),
        "ctxL": c[:, KC * P:, :],
        "rr": i["L0_attn_Wr"].T, "rk": i["L0_attn_Wk"].T, "rv": i["L0_attn_Wv"].T, "ro": i["L0_attn_Wo"].T,
        "rg": i["L0_attn_Wfr"].T, "fk": i["L0_attn_Wfk"].T, "fv": i["L0_attn_Wfv"].T,
        "ln_cols": np.concatenate([columns(i["L0_attn_" + n]) for n in ("ln1_w", "ln1_b", "ln2_w", "ln2_b")], 1),
        "decay_u": np.concatenate([columns(i["L0_attn_decay"]), columns(i["L0_attn_u"])], 1),
        "w1": i["L0_ffn_w1"], "w2": i["L0_ffn_w2"],
        "b1": i["L0_ffn_b1"].reshape(EXPERTS, HFT, P).transpose(2, 0, 1),
        "b2": i["L0_ffn_b2"].reshape(1, -1),
        "gateT": i["L0_ffn_gate_w"].T, "gate_b": i["L0_ffn_gate_b"][None],
    }.items()}


def kernel(**inputs):
    import numpy as np
    import concourse.bacc as bacc
    from concourse.bass_utils import run_bass_kernel_spmd

    arrays = layouts({k: np.asarray(v) for k, v in inputs.items()})
    nc = bacc.Bacc("TRN2", target_bir_lowering=False, num_devices=1, dynamic_dma_scratch_size=4096)
    A = {k: nc.dram_tensor("in_" + k, v.shape, mybir.dt.from_np(v.dtype), kind="ExternalInput").ap() for k, v in arrays.items()}
    out = nc.dram_tensor("out", (TOKENS, D), F32, kind="ExternalOutput").ap()
    perceiver_layer(nc, A, out)
    r = run_bass_kernel_spmd(nc, [{"in_" + k: v for k, v in arrays.items()}], core_ids=[0])
    return r.results[0]["out"].reshape(BATCH, QLEN, D)
```

```python
from contextlib import ExitStack

import concourse.bass as bass
from concourse import mybir

F32 = mybir.dt.float32
F32R = mybir.dt.float32r
U32 = mybir.dt.uint32
ALU = mybir.AluOpType
ACT = mybir.ActivationFunctionType
AX_X = mybir.AxisListType.X

P = 128
BATCH, QLEN, D = 64, 32, 256
KEYS = 257
HEADS, DK = 16, 64
E = HEADS * DK
TOKENS = BATCH * QLEN
DT = D // P
ET = E // P
TT = TOKENS // P
NB = 8
GROUPS = BATCH // NB
GTOK = NB * QLEN
HT = HEADS * QLEN // P
TILES = NB * HT
KC = KEYS // P
KPAD = KEYS + 1
EPS = 1e-5
SCALE = DK ** -0.5



def wait(eng, sem, loop, per, count):
    value = loop * per + count
    if isinstance(value, int) and value <= 0:
        return
    eng.wait_ge(sem, value)


def turns(eng, n, body):
    body(0)
    with eng.Fori(1, n) as i:
        body(i)


def wait_alone(eng, sem, loop, per, count, passed):
    wait(eng, sem, loop, per, count)
    if not isinstance(loop, int):
        eng.sem_inc(passed, 1)


def three_pass(pe, out, w_hi, w_lo, m_hi, m_lo, first, last, **kw):
    pe.matmul(out, w_hi, m_hi, start=first, stop=False, **kw)
    pe.matmul(out, w_hi, m_lo, start=False, stop=False, **kw)
    return pe.matmul(out, w_lo, m_hi, start=False, stop=last, **kw)


def f(ap):
    return ap.bitcast(F32)


def identity(pool, ident, made):
    pool.memset(ident[:, :], 0.0).then_inc(made, 1)
    pool.wait_ge(made, 1)
    pool.affine_select(out=ident[:, :], in_=ident[:, :], compare_op=ALU.not_equal, fill=1.0, base=0,
                       pattern=[[-1, P]], channel_multiplier=1).then_inc(made, 1)


def three_zero(view):
    return view.rearrange("p d t (c k) -> p (d t) c k", k=DK)[:, :, 0:3:2, :]


def prepare(nc, A, W, dram):
    with ExitStack() as ctx:
        def sb(name, shape, dt=F32):
            return ctx.enter_context(nc.sbuf_tensor(name, shape, dt))

        def sem(name):
            return ctx.enter_context(nc.semaphore(name))

        x = sb("x_in", [P, TT, D])
        raw_wq = sb("raw_wq", [P, DT, E])
        raw_wk = sb("raw_wk", [P, ET, D])
        raw_wv = sb("raw_wv", [P, DT * ET, 2, DK])
        raw_wo = sb("raw_wo", [P, ET, D])
        wq_nat = sb("wq_nat", [P, ET, D])
        bk_col = sb("bk_col", [P, ET])
        bk_diag = sb("bk_diag", [P, ET, HEADS])
        stats = sb("ln_stats", [P, TT, 6])
        mv = sb("ln_mv", [P, TT, 2])
        veps = sb("ln_veps", [P, TT])
        power = sb("ln_power", [P, TT])
        rstd = sb("ln_rstd", [P, TT])
        xT_hi = sb("p_xT_hi", [P, 2, DT, GTOK], F32R)
        xT_lo = sb("p_xT_lo", [P, 2, DT, GTOK], F32R)
        g_hi = sb("g_hi", [P, DT, HEADS], F32R)
        g_lo = sb("g_lo", [P, DT, HEADS], F32R)
        g_raw = sb("g_raw", [P, DT, HEADS])
        c0 = sb("c0", [P, HEADS])
        c_tok = sb("c_tok", [P, TT, HEADS])
        ps_t = [ctx.enter_context(nc.psum_tensor(f"ps_t{i}", [P, DT, GTOK], F32)) for i in range(2)]
        ps_g = ctx.enter_context(nc.psum_tensor("ps_g", [P, DT, HEADS], F32))
        ps_c0 = ctx.enter_context(nc.psum_tensor("ps_c0", [P, HEADS], F32))
        ps_c = ctx.enter_context(nc.psum_tensor("ps_c", [P, TT, HEADS], F32))

        x_loaded = sem("x_loaded")
        b_loaded = sem("b_loaded")
        wq_loaded, wk_loaded, wv_loaded, wo_loaded = (sem(n + "_loaded") for n in ("wq", "wk", "wv", "wo"))
        w_hi_done = sem("w_hi_done")
        w_lo_dve = sem("w_lo_dve")
        w_lo_pool = sem("w_lo_pool")
        consts = sem("p_consts")
        diag_made = sem("diag_made")
        stats_done = sem("stats_done")
        mv_done = sem("mv_done")
        veps_done = sem("veps_done")
        rstd_done = sem("rstd_done")
        xn_done = sem("xn_done")
        xT_done = sem("xT_done")
        hi_done = sem("hi_done")
        lo_done = sem("lo_done")
        stored = [sem("stored_even"), sem("stored_odd")]
        g_done = sem("g_done")
        g_split = sem("g_split")
        c_done = sem("c_done")
        c_copied = sem("c_copied")

        with nc.Block() as block:
            @block.sync
            def _(sp):
                sp.dma_start(x[:, :, :], A["x"].rearrange("(t p) d -> p t d", p=P)).then_inc(x_loaded, 16)
                sp.dma_start(wq_nat[:, :, :], A["wq_nat"].rearrange("(t p) d -> p t d", p=P)).then_inc(b_loaded, 16)
                sp.dma_start(bk_col[:, :], A["bk"]).then_inc(b_loaded, 16)
                sp.dma_start(W["bq"][:, :], A["bq"]).then_inc(b_loaded, 16)
                sp.dma_start(W["bv"][:, :], A["bv"]).then_inc(b_loaded, 16)
                sp.dma_start(raw_wq[:, :, :], A["wqT"].rearrange("(t p) e -> p t e", p=P)).then_inc(wq_loaded, 16)
                sp.dma_start(raw_wk[:, :, :], A["wk"].rearrange("(t p) d -> p t d", p=P)).then_inc(wk_loaded, 16)
                sp.dma_start(raw_wv[:, :, :, :].rearrange("p a b c -> p (a b c)").rearrange("p (t e) -> p t e", t=DT),
                             A["wvT"].rearrange("(t p) e -> p t e", p=P)).then_inc(wv_loaded, 16)
                sp.dma_start(raw_wo[:, :, :], A["woT"].rearrange("(t p) d -> p t d", p=P)).then_inc(wo_loaded, 16)
                for g in range(GROUPS):
                    sp.wait_ge(lo_done, g + 1)
                    for name, part in (("xT_hi", xT_hi), ("xT_lo", xT_lo)):
                        sp.dma_start(dram[name][g], f(part[:, g % 2].rearrange("p a b -> p (a b)")))\
                          .then_inc(stored[g % 2], 16)
                for parity in range(2):
                    sp.wait_ge(stored[parity], 16 * GROUPS)

            @block.gpsimd
            def _(pool):
                identity(pool, W["ident"], consts)
                pool.memset(bk_diag[:, :, :], 0.0).then_inc(consts, 1)
                pool.memset(power[:, :], -0.5).then_inc(consts, 1)
                pool.wait_ge(consts, 4)
                pool.wait_ge(veps_done, 1)
                pool.tensor_tensor(rstd[:, :], veps[:, :], power[:, :], ALU.pow).then_inc(rstd_done, 1)
                for part in ("wv_hi", "wv_lo"):
                    pool.memset(f(W[part][:, :, :, DK:2 * DK]), 0.0).then_inc(w_lo_pool, 1)
                pool.wait_ge(w_hi_done, 3)
                pool.tensor_tensor(three_zero(W["wv_lo"][:, :, :, :]), raw_wv[:, :, :, :],
                                   f(three_zero(W["wv_hi"][:, :, :, :])), ALU.subtract).then_inc(w_lo_pool, 1)
                pool.wait_ge(w_hi_done, 4)
                pool.tensor_tensor(W["wo_lo"][:, :, :], raw_wo[:, :, :], f(W["wo_hi"][:, :, :]),
                                   ALU.subtract).then_inc(w_lo_pool, 1)

            @block.vector
            def _(dve):
                dve.wait_ge(b_loaded, 64)
                dve.wait_ge(consts, 3)
                flat = bk_diag[:, :, :].rearrange("p t h -> p (t h)")
                step = HEADS + 2
                dve.tensor_copy(flat[0:DK, 0:(ET - 1) * step + 1:step], bk_col[0:DK, :]).then_inc(diag_made, 1)
                dve.tensor_copy(flat[DK:P, 1:(ET - 1) * step + 2:step], bk_col[DK:P, :]).then_inc(diag_made, 1)
                dve.wait_ge(x_loaded, 16)
                for t in range(TT):
                    dve.bn_stats(stats[:, t, :], x[:, t, :]).then_inc(stats_done, 1)
                for t in range(TT):
                    dve.wait_ge(stats_done, t + 1)
                    dve.bn_aggr(mv[:, t, :], stats[:, t, :]).then_inc(mv_done, 1)
                dve.wait_ge(mv_done, TT)
                dve.tensor_scalar(veps[:, :], mv[:, :, 1], EPS, None, ALU.add).then_inc(veps_done, 1)
                dve.wait_ge(rstd_done, 1)
                for t in range(TT):
                    dve.tensor_scalar(x[:, t, :], x[:, t, :], mv[:, t, 0:1], rstd[:, t:t + 1],
                                      ALU.subtract, ALU.mult).then_inc(xn_done, 1)
                dve.wait_ge(g_done, 1)
                dve.tensor_copy(g_raw[:, :, :], ps_g[:, :, :]).then_inc(g_split, 1)
                dve.tensor_copy(c0[:, :], ps_c0[:, :]).then_inc(g_split, 1)
                dve.wait_ge(g_split, 2)
                dve.tensor_copy(g_hi[:, :, :], g_raw[:, :, :]).then_inc(g_split, 1)
                dve.wait_ge(g_split, 3)
                dve.tensor_tensor(g_lo[:, :, :], g_raw[:, :, :], f(g_hi[:, :, :]), ALU.subtract).then_inc(g_split, 1)
                for g in range(GROUPS):
                    dve.wait_ge(hi_done, g + 1)
                    if g >= 2:
                        dve.wait_ge(stored[g % 2], 32 * (g // 2))
                        dve.wait_ge(c_done, g - 1)
                    dve.tensor_tensor(xT_lo[:, g % 2], ps_t[g % 2][:, :, :], f(xT_hi[:, g % 2]),
                                      ALU.subtract).then_inc(lo_done, 1)
                dve.wait_ge(c_done, GROUPS)
                for t in range(TT):
                    dve.tensor_tensor(c_tok[:, t, :], ps_c[:, t, :], c0[:, :], ALU.add).then_inc(c_copied, 1)
                dve.wait_ge(c_copied, TT)
                dve.tensor_scalar(c_tok[:, :, :], c_tok[:, :, :], SCALE, None, ALU.mult).then_inc(c_copied, 1)
                dve.wait_ge(c_copied, TT + 1)
                for b in range(4):
                    for h in range(4):
                        src = c_tok[32 * b:32 * b + 32, :, :].rearrange("q t (a h) -> q t a h", h=4)[:, :, :, h]
                        dst = W["cmap"][32 * h:32 * h + 32, :].rearrange("q (t b a) -> q t b a", b=4, a=HT)[:, :, b, :]
                        dve.tensor_copy(dst, src).then_inc(c_copied, 1)
                dve.wait_ge(w_hi_done, 1)
                dve.tensor_tensor(W["wq_lo"][:, :, :], raw_wq[:, :, :], f(W["wq_hi"][:, :, :]),
                                  ALU.subtract).then_inc(w_lo_dve, 1)
                dve.wait_ge(w_hi_done, 2)
                dve.tensor_tensor(W["wk_lo"][:, :, :], raw_wk[:, :, :], f(W["wk_hi"][:, :, :]),
                                  ALU.subtract).then_inc(w_lo_dve, 1)

            @block.scalar
            def _(act):
                for g in range(GROUPS):
                    act.wait_ge(xT_done, g + 1)
                    if g >= 2:
                        act.wait_ge(stored[g % 2], 32 * (g // 2))
                        act.wait_ge(c_done, g - 1)
                    act.activation(xT_hi[:, g % 2], ps_t[g % 2][:, :, :], ACT.Copy).then_inc(hi_done, 1)
                act.wait_ge(wq_loaded, 16)
                act.activation(W["wq_hi"][:, :, :], raw_wq[:, :, :], ACT.Copy).then_inc(w_hi_done, 1)
                act.wait_ge(wk_loaded, 16)
                act.activation(W["wk_hi"][:, :, :], raw_wk[:, :, :], ACT.Copy).then_inc(w_hi_done, 1)
                act.wait_ge(wv_loaded, 16)
                act.activation(three_zero(W["wv_hi"][:, :, :, :]), raw_wv[:, :, :, :], ACT.Copy).then_inc(w_hi_done, 1)
                act.wait_ge(wo_loaded, 16)
                act.activation(W["wo_hi"][:, :, :], raw_wo[:, :, :], ACT.Copy).then_inc(w_hi_done, 1)

            @block.tensor
            def _(pe):
                pe.wait_ge(b_loaded, 64)
                pe.wait_ge(diag_made, 2)
                for d in range(DT):
                    for i in range(ET):
                        pe.matmul(ps_g[:, d, :], wq_nat[:, i, d * P:(d + 1) * P], bk_diag[:, i, :],
                                  start=(i == 0), stop=(i == ET - 1))
                for i in range(ET):
                    mm = pe.matmul(ps_c0[:, :], W["bq"][:, i:i + 1].to_broadcast([P, P]), bk_diag[:, i, :],
                                   start=(i == 0), stop=(i == ET - 1))
                mm.then_inc(g_done, 1)

                def q_dot_bk(g):
                    pe.wait_ge(lo_done, g + 1)
                    if g == 0:
                        pe.wait_ge(g_split, 4)
                    for half in range(2):
                        cols = slice(half * P, (half + 1) * P)
                        for d in range(DT):
                            mm = three_pass(pe, ps_c[:, 2 * g + half, :], xT_hi[:, g % 2, d, cols],
                                            xT_lo[:, g % 2, d, cols], g_hi[:, d, :], g_lo[:, d, :],
                                            d == 0, d == DT - 1)
                    mm.then_inc(c_done, 1)

                pe.wait_ge(consts, 2)
                for g in range(GROUPS):
                    pe.wait_ge(xn_done, 2 * g + 2)
                    for half in range(2):
                        for d in range(DT):
                            mm = pe.transpose(ps_t[g % 2][:, d, half * P:(half + 1) * P],
                                              x[:, 2 * g + half, d * P:(d + 1) * P], W["ident"][:, :])
                    mm.then_inc(xT_done, 1)
                    if g >= 1:
                        q_dot_bk(g - 1)
                q_dot_bk(GROUPS - 1)


T_LAG = 3
PV_PARTS = 4
PV_LAG = 10
ROUND_T, REST_T = 0, 1
ROUND_N, REST_N = 6, 7
P_HI, P_LO = (5, 7), (6, 8)
Z_HI, Z_LO = (12, 14), (13, 15)
STEPS = TILES - HT + Z_LO[1] + 1
EARLY = 3
RING = 8


def due(s, lag):
    b, t = divmod(s - lag, HT)
    return [b] if t == 0 and 0 <= b < NB else []


def early_step(i):
    t, odd = divmod(i - 2, 2)
    return [t] if not odd and 0 <= t < EARLY else []


def both_due(s, lags):
    return [(b, part) for part in range(2) for b in due(s, lags[part])]


def attention(nc, A, W, dram):
    with ExitStack() as ctx:
        def sb(name, shape, dt=F32):
            return ctx.enter_context(nc.sbuf_tensor(name, shape, dt))

        def sem(name):
            return ctx.enter_context(nc.semaphore(name))

        xT_hi = sb("xT_hi", [P, DT, GTOK], F32R)
        xT_lo = sb("xT_lo", [P, DT, GTOK], F32R)
        cg = sb("cg", [P, TILES])
        e_hi = [sb(f"e_hi{i}", [P, GTOK], F32R) for i in range(3)]
        e_lo = [sb(f"e_lo{i}", [P, GTOK], F32R) for i in range(3)]
        qk_hi = sb("qk_hi", [P, DT, NB, HEADS * QLEN], F32R)
        qk_lo = sb("qk_lo", [P, DT, NB, HEADS * QLEN], F32R)
        raw_T = [sb(f"raw_T{i}", [P, DT, KPAD]) for i in range(2)]
        raw_N = [sb(f"raw_N{i}", [P, KC, D]) for i in range(2)]
        raw_L = [sb(f"raw_L{i}", [96, D]) for i in range(2)]
        ctxT_hi = [sb(f"ctxT_hi{i}", [P, DT, KPAD], F32R) for i in range(2)]
        ctxT_lo = [sb(f"ctxT_lo{i}", [P, DT, KPAD], F32R) for i in range(2)]
        ctxN_hi = [sb(f"ctxN_hi{i}", [P, KC, D], F32R) for i in range(2)]
        ctxN_lo = [sb(f"ctxN_lo{i}", [P, KC, D], F32R) for i in range(2)]
        ctxL = [sb(f"ctxL{i}", [96, D], F32R) for i in range(2)]
        probs = sb("probs", [P, RING, KEYS])
        pT_hi = [sb(f"pT_hi{i}", [P, KC, HEADS * QLEN], F32R) for i in range(2)]
        pT_lo = [sb(f"pT_lo{i}", [P, KC, HEADS * QLEN], F32R) for i in range(2)]
        pL = [sb(f"pL{i}", [96, HEADS * QLEN], F32R) for i in range(2)]
        mx = sb("mx", [P, TILES])
        mc = sb("mc", [P, TILES])
        neg = sb("neg", [P, TILES])
        total = sb("total", [P, TILES])
        rec = sb("rec", [P, TILES])
        y = sb("y", [P, 2, D])

        ps_s = [ctx.enter_context(nc.psum_tensor(f"ps_s{i}", [P, 512], F32)) for i in range(2)]
        ps_p = [ctx.enter_context(nc.psum_tensor(f"ps_p{i}", [P, KC, 2 * P], F32)) for i in range(2)]
        ps_l = ctx.enter_context(nc.psum_tensor("ps_l", [P, HEADS * QLEN], F32))
        ps_z = [ctx.enter_context(nc.psum_tensor(f"ps_z{i}", [P, 512], F32)) for i in range(2)]
        ps_x = ctx.enter_context(nc.psum_tensor("ps_x", [P, 2, D], F32))
        ps_x_flat = ps_x[:, :, :].rearrange("p a b -> p (a b)")
        q_banks = [ps_p[i][:, :, :].rearrange("p a b -> p (a b)")[:, 0:GTOK] for i in range(2)]
        qk_banks = [ps_z[0][:, :], ps_z[1][:, :], ps_l[:, :]]
        z_banks = [ps_z[0][:, :], ps_z[1][:, :], ps_x_flat]

        def z_bank(b, dt):
            return z_banks[(DT * b + dt) % 3]


        pads_zero = sem("pads_zero")
        passed = {n: sem("passed_" + n) for n in ("sp", "pool")}
        xT_in = sem("xT_in")
        rawT_in = [sem("rawT_in_even"), sem("rawT_in_odd")]
        rawN_in = [sem("rawN_in_even"), sem("rawN_in_odd")]
        ctxT_hi_done, ctxN_hi_done, ctxL_hi_done = (sem(f"ctx{n}_hi_done") for n in "TNL")
        ctxT_split, ctxN_split, ctxL_split = (sem(f"ctx{n}_split") for n in "TNL")
        cg_ready = sem("cg_ready")
        q_done, q_hi, q_lo = sem("q_done"), sem("q_hi"), sem("q_lo")
        qk_done, qk_hi_done, qk_lo_done = sem("qk_done"), sem("qk_hi_done"), sem("qk_lo_done")
        sc_done = sem("sc_done")
        max_done = sem("max_done")
        mc_done = sem("mc_done")
        neg_done = sem("neg_done")
        exp_done = sem("exp_done")
        rec_done = sem("rec_done")
        norm_done = sem("norm_done")
        tp_done = sem("tp_done")
        tpL_done = sem("tpL_done")
        pT_hi_done, pT_lo_done = sem("pT_hi_done"), sem("pT_lo_done")
        z_done, z_hi, z_lo = sem("z_done"), sem("z_hi"), sem("z_lo")
        o_done, o_hi, o_lo = sem("o_done"), sem("o_hi"), sem("o_lo")
        wo_done = sem("wo_done")
        y_copied = sem("y_copied")
        y_stored = sem("y_stored")

        ctxT_dram, ctxN_dram, ctxL_dram = A["ctxT"], A["ctxN"], A["ctxL"]

        def groups(eng, body):
            body(0)
            with eng.Fori(1, GROUPS - 1) as g:
                body(g)
            body(GROUPS - 1)

        with nc.Block() as block:
            @block.sync
            def _(sp):
                def load_T(b, i):
                    sp.dma_start(raw_T[i][:, :, 0:KEYS], ctxT_dram[b]).then_inc(rawT_in[i], 16)

                def load_N(b, i):
                    sp.dma_start(raw_N[i][:, :, :], ctxN_dram[b]).then_inc(rawN_in[i], 16)
                    sp.dma_start(raw_L[i][0:65:32, :], ctxL_dram[b].to_broadcast([3, D])).then_inc(rawN_in[i], 16)

                def load_x(g):
                    sp.dma_start(f(xT_hi[:, :, :].rearrange("p a b -> p (a b)")), dram["xT_hi"][g]).then_inc(xT_in, 16)
                    sp.dma_start(f(xT_lo[:, :, :].rearrange("p a b -> p (a b)")), dram["xT_lo"][g]).then_inc(xT_in, 16)

                def body(g):
                    last = isinstance(g, int) and g == GROUPS - 1
                    for b in range(NB):
                        if not (last and b == NB - 1):
                            wait(sp, ctxT_split, g, NB, b)
                            load_T(g * NB + b + 1, (b + 1) % 2)
                        wait_alone(sp, ctxN_split, g, NB, b - 1, passed["sp"])
                        wait_alone(sp, ctxL_split, g, NB, b - 1, passed["sp"])
                        load_N(g * NB + b, b % 2)
                    if not last:
                        wait(sp, q_done, g, ET, ET)
                        load_x(g + 1)
                    wait(sp, y_copied, g, 1, 1)
                    sp.dma_start(dram["y"][g], y[:, :, :].rearrange("p a b -> p (a b)")).then_inc(y_stored, 16)

                sp.wait_ge(pads_zero, 4)
                load_T(0, 0)
                load_x(0)
                groups(sp, body)
                sp.wait_ge(y_stored, 16 * GROUPS)

            @block.gpsimd
            def _(pool):
                def rest_T(g, b):
                    wait(pool, ctxT_hi_done, g, NB, b + 1)
                    pool.tensor_tensor(ctxT_lo[b % 2][:, :, :], raw_T[b % 2][:, :, :], f(ctxT_hi[b % 2][:, :, :]),
                                       ALU.subtract).then_inc(ctxT_split, 1)

                def body(g):
                    last = isinstance(g, int) and g == GROUPS - 1
                    for s in range(STEPS):
                        if s < TILES:
                            wait_alone(pool, rec_done, g, TILES, s + 1, passed["pool"])
                            pool.tensor_scalar(probs[:, s % RING, :], probs[:, s % RING, :], rec[:, s:s + 1], 1.0,
                                               ALU.mult, ALU.mult).then_inc(norm_done, 1)
                        for b in due(s, REST_T):
                            if not (last and b == NB - 1):
                                rest_T(g, b + 1)
                        for b in due(s, ROUND_N):
                            wait(pool, rawN_in[b % 2], g, 32 * NB // 2, 32 * (b // 2 + 1))
                            wait_alone(pool, z_done, g, DT * NB, DT * (b - 1), passed["pool"])
                            pool.tensor_copy(ctxL[b % 2][:, :], raw_L[b % 2][:, :]).then_inc(ctxL_hi_done, 1)
                        for b in due(s, REST_N):
                            wait(pool, ctxN_hi_done, g, NB, b + 1)
                            pool.tensor_tensor(ctxN_lo[b % 2][:, :, :], raw_N[b % 2][:, :, :],
                                               f(ctxN_hi[b % 2][:, :, :]), ALU.subtract).then_inc(ctxN_split, 1)

                for i in range(2):
                    pool.memset(raw_T[i][:, :, KEYS:KPAD], 0.0).then_inc(pads_zero, 1)
                    pool.memset(raw_L[i][:, :], 0.0).then_inc(pads_zero, 1)
                rest_T(0, 0)
                groups(pool, body)

            @block.vector
            def _(dve):
                def body(g):
                    wait(dve, exp_done, g, TILES, 0)
                    dve.tensor_copy(cg[:, :], W["cmap"][:, bass.ts(g, TILES)]).then_inc(cg_ready, 1)
                    def maximum(s):
                        if s < TILES:
                            wait(dve, sc_done, g, TILES, s + 1)
                            dve.tensor_reduce(mx[:, s:s + 1], ps_s[s % 2][:, 0:KEYS], AX_X, ALU.max).then_inc(max_done, 1)
                            wait(dve, max_done, g, TILES, s + 1)
                            dve.tensor_scalar(mc[:, s:s + 1], mx[:, s:s + 1], SCALE, cg[:, s:s + 1],
                                              ALU.mult, ALU.add).then_inc(mc_done, 1)
                            wait(dve, mc_done, g, TILES, s + 1)
                            dve.tensor_scalar(neg[:, s:s + 1], mc[:, s:s + 1], -1.0, cg[:, s:s + 1],
                                              ALU.mult, ALU.add).then_inc(neg_done, 1)

                    def reciprocal(s):
                        if s < TILES:
                            wait(dve, exp_done, g, TILES, s + 1)
                            dve.reciprocal(rec[:, s:s + 1], total[:, s:s + 1]).then_inc(rec_done, 1)

                    def step(s):
                        maximum(s)
                        for b, dt in both_due(s, Z_LO):
                            wait(dve, z_hi, g, DT * NB, DT * b + dt + 1)
                            dve.tensor_tensor(qk_lo[:, dt, b, :], z_bank(b, dt), f(qk_hi[:, dt, b, :]),
                                              ALU.subtract).then_inc(z_lo, 1)
                        for b, half in both_due(s, P_LO):
                            wait(dve, pT_hi_done, g, 3 * NB, 3 * b + half + 1)
                            cols = slice(half * 2 * P, (half + 1) * 2 * P)
                            dve.tensor_tensor(pT_lo[b % 2][:, :, cols], ps_p[half][:, :, :],
                                              f(pT_hi[b % 2][:, :, cols]), ALU.subtract).then_inc(pT_lo_done, 1)
                        reciprocal(s)
                        for b in due(s, P_LO[1]):
                            wait(dve, pT_hi_done, g, 3 * NB, 3 * b + 3)
                            dve.tensor_tensor(pL[b % 2][32:64, :], ps_l[32:64, :], f(pL[b % 2][32:64, :]),
                                              ALU.subtract).then_inc(pT_lo_done, 1)
                        for b in due(s, REST_N):
                            wait(dve, ctxL_hi_done, g, NB, b + 1)
                            dve.tensor_tensor(ctxL[b % 2][64:96, :], raw_L[b % 2][64:96, :],
                                              f(ctxL[b % 2][64:96, :]), ALU.subtract).then_inc(ctxL_split, 1)

                    def q_part(i):
                        wait(dve, q_hi, g, ET, i + 1)
                        dve.scalar_tensor_tensor(e_lo[i % 3][:, :], q_banks[i % 2], W["bq"][:, i:i + 1],
                                                 f(e_hi[i % 3][:, :]), ALU.add, ALU.subtract).then_inc(q_lo, 1)

                    wait(dve, cg_ready, g, 1, 1)
                    q_part(0)
                    for i in range(ET):
                        if i + 1 < ET:
                            q_part(i + 1)
                        for h in (2 * i, 2 * i + 1):
                            wait(dve, qk_hi_done, g, HEADS, h + 1)
                            rows = (slice(None), slice(None), slice(None), slice(h * QLEN, (h + 1) * QLEN))
                            src = qk_banks[h % 3].rearrange("p (d b q) -> p d b q", d=DT, b=NB)
                            dve.tensor_tensor(qk_lo[rows], src, f(qk_hi[rows]), ALU.subtract).then_inc(qk_lo_done, 1)
                        for s in early_step(i):
                            maximum(s)
                        for s in early_step(i - 2):
                            reciprocal(s)
                    reciprocal(EARLY - 1)
                    for s in range(EARLY, STEPS):
                        step(s)
                    for i in range(ET):
                        wait(dve, o_hi, g, ET, i + 1)
                        dve.scalar_tensor_tensor(e_lo[i % 3][:, :], ps_s[i % 2][:, 0:GTOK], W["bv"][:, i:i + 1],
                                                 f(e_hi[i % 3][:, :]), ALU.add, ALU.subtract).then_inc(o_lo, 1)

                groups(dve, body)

            @block.scalar
            def _(act):
                def round_T(g, b):
                    i = b % 2
                    wait(act, rawT_in[i], g, 16 * NB // 2, 16 * (b // 2 + 1))
                    wait(act, sc_done, g, TILES, HT * (b - 1))
                    act.activation(ctxT_hi[i][:, :, :], raw_T[i][:, :, :], ACT.Copy).then_inc(ctxT_hi_done, 1)

                def round_N(g, b):
                    i = b % 2
                    wait(act, rawN_in[i], g, 32 * NB // 2, 32 * (b // 2 + 1))
                    wait(act, z_done, g, DT * NB, DT * (b - 1))
                    act.activation(ctxN_hi[i][:, :, :], raw_N[i][:, :, :], ACT.Copy).then_inc(ctxN_hi_done, 1)

                def body(g):
                    last = isinstance(g, int) and g == GROUPS - 1

                    def step(s):
                        if s < TILES:
                            if s >= RING and s % HT == 0:
                                wait(act, tpL_done, g, NB, s // HT - 1)
                            wait(act, neg_done, g, TILES, s + 1)
                            act.activation(probs[:, s % RING, :], ps_s[s % 2][:, 0:KEYS], ACT.Exp, bias=neg[:, s:s + 1],
                                           scale=SCALE, accum_out=total[:, s:s + 1]).then_inc(exp_done, 1)
                        for b, dt in both_due(s, Z_HI):
                            wait(act, z_done, g, DT * NB, DT * b + dt + 1)
                            act.activation(qk_hi[:, dt, b, :], z_bank(b, dt), ACT.Copy).then_inc(z_hi, 1)
                        for b, half in both_due(s, P_HI):
                            wait(act, tp_done, g, TILES, HT * b + 2 * half + 2)
                            if half == 0:
                                wait(act, z_done, g, DT * NB, DT * (b - 1))
                            act.activation(pT_hi[b % 2][:, :, half * 2 * P:(half + 1) * 2 * P], ps_p[half][:, :, :],
                                           ACT.Copy).then_inc(pT_hi_done, 1)
                        for b in due(s, P_HI[1]):
                            wait(act, tpL_done, g, NB, b + 1)
                            act.activation(pL[b % 2][:, :], ps_l[0:96, :], ACT.Copy).then_inc(pT_hi_done, 1)
                        for b in due(s, ROUND_T):
                            if not (last and b == NB - 1):
                                round_T(g, b + 1)
                        for b in due(s, ROUND_N):
                            round_N(g, b)

                    def q_part(i):
                        wait(act, q_done, g, ET, i + 1)
                        if i >= 3:
                            wait(act, qk_done, g, HEADS, 2 * (i - 3) + 2)
                        act.activation(e_hi[i % 3][:, :], q_banks[i % 2], ACT.Identity,
                                       bias=W["bq"][:, i:i + 1]).then_inc(q_hi, 1)

                    q_part(0)
                    for i in range(ET):
                        if i + 1 < ET:
                            q_part(i + 1)
                        for h in (2 * i, 2 * i + 1):
                            wait(act, qk_done, g, HEADS, h + 1)
                            rows = (slice(None), slice(None), slice(None), slice(h * QLEN, (h + 1) * QLEN))
                            src = qk_banks[h % 3].rearrange("p (d b q) -> p d b q", d=DT, b=NB)
                            act.activation(qk_hi[rows], src, ACT.Copy).then_inc(qk_hi_done, 1)
                        for s in early_step(i - 1):
                            step(s)
                    for s in range(EARLY, STEPS):
                        step(s)
                    for i in range(ET):
                        wait(act, o_done, g, ET, i + 1)
                        if i >= 3:
                            wait(act, wo_done, g, ET, i - 2)
                        act.activation(e_hi[i % 3][:, :], ps_s[i % 2][:, 0:GTOK], ACT.Identity,
                                       bias=W["bv"][:, i:i + 1]).then_inc(o_hi, 1)
                    wait(act, wo_done, g, ET, ET)
                    wait(act, y_stored, g, 16, 0)
                    act.activation(y[:, :, :], ps_x[:, :, :], ACT.Copy).then_inc(y_copied, 1)

                act.wait_ge(pads_zero, 4)
                round_T(0, 0)
                groups(act, body)

            @block.tensor
            def _(pe):
                def body(g):
                    wait(pe, xT_in, g, 32, 32)

                    def q_part(i):
                        if i >= 2:
                            wait(pe, q_lo, g, ET, i - 1)
                        for d in range(DT):
                            mm = three_pass(pe, q_banks[i % 2], W["wq_hi"][:, d, i * P:(i + 1) * P],
                                            W["wq_lo"][:, d, i * P:(i + 1) * P], xT_hi[:, d, :], xT_lo[:, d, :],
                                            d == 0, d == DT - 1)
                        mm.then_inc(q_done, 1)

                    def qk_part(h):
                        i, rows = h // 2, slice(DK * (h % 2), DK * (h % 2) + DK)
                        if h >= 3:
                            wait(pe, qk_lo_done, g, HEADS, h - 2)
                        wait(pe, q_lo, g, ET, i + 1)
                        for d in range(DT):
                            cols = slice(d * P, (d + 1) * P)
                            mm = three_pass(pe, qk_banks[h % 3][:, d * GTOK:(d + 1) * GTOK],
                                            W["wk_hi"][rows, i, cols], W["wk_lo"][rows, i, cols],
                                            e_hi[i % 3][rows, :], e_lo[i % 3][rows, :], True, True)
                        mm.then_inc(qk_done, 1)

                    def scores(s):
                        b, t = divmod(s, HT)
                        i, cols = b % 2, slice(t * P, (t + 1) * P)
                        if t == 0:
                            wait(pe, ctxT_split, g, NB, b + 1)
                        if b == 0:
                            wait(pe, qk_lo_done, g, HEADS, 4 * (t + 1))
                        if s >= 2:
                            wait(pe, exp_done, g, TILES, s - 1)
                        for d in range(DT):
                            mm = three_pass(pe, ps_s[s % 2][:, 0:KPAD], qk_hi[:, d, b, cols], qk_lo[:, d, b, cols],
                                            ctxT_hi[i][:, d, :], ctxT_lo[i][:, d, :], d == 0, d == DT - 1)
                        mm.then_inc(sc_done, 1)

                    def transposes(s):
                        b, t = divmod(s, HT)
                        half, cols = t // 2, slice((t % 2) * P, (t % 2 + 1) * P)
                        wait(pe, norm_done, g, TILES, s + 1)
                        if t % 2 == 0:
                            wait(pe, pT_lo_done, g, 3 * NB, 3 * (b - 1) + half + 1)
                        for c in range(KC):
                            mm = pe.transpose(ps_p[half][:, c, cols], probs[:, s % RING, c * P:(c + 1) * P], W["ident"][:, :])
                        mm.then_inc(tp_done, 1)

                    def last_key(b):
                        wait(pe, pT_lo_done, g, 3 * NB, 3 * b)
                        for t in range(HT):
                            mm = pe.transpose(ps_l[0:96, t * P:(t + 1) * P],
                                              probs[:, (HT * b + t) % RING, KC * P:KEYS].to_broadcast([P, 96]), W["ident"][:, :])
                        mm.then_inc(tpL_done, 1)

                    def values(b, part):
                        dt, cols = part // 2, slice((part // 2) * P, (part // 2 + 1) * P)
                        i, out = b % 2, z_bank(b, dt)
                        if part == 0:
                            wait(pe, pT_lo_done, g, 3 * NB, 3 * (b + 1))
                            wait(pe, ctxN_split, g, NB, b + 1)
                            wait(pe, ctxL_split, g, NB, b + 1)
                        if part % 2 == 0:
                            if DT * b + dt >= 3:
                                wait(pe, z_lo, g, DT * NB, DT * b + dt - 2)
                            elif DT * b + dt == 2:
                                wait(pe, y_copied, g, 1, 0)
                            three_pass(pe, out, ctxN_hi[i][:, 0, cols], ctxN_lo[i][:, 0, cols],
                                       pT_hi[i][:, 0, :], pT_lo[i][:, 0, :], True, False)
                            return
                        three_pass(pe, out, ctxN_hi[i][:, 1, cols], ctxN_lo[i][:, 1, cols],
                                   pT_hi[i][:, 1, :], pT_lo[i][:, 1, :], False, False)
                        pe.matmul(out, ctxL[i][:, cols], pL[i][:, :], start=False, stop=True).then_inc(z_done, 1)

                    def step(s):
                        if s < TILES:
                            scores(s)
                        b, part = divmod(s - PV_LAG, PV_PARTS)
                        if 0 <= b < NB:
                            values(b, part)
                        if T_LAG <= s < TILES + T_LAG:
                            transposes(s - T_LAG)
                        for b in due(s, HT - 1 + T_LAG):
                            last_key(b)

                    q_part(0)
                    for i in range(ET):
                        if i + 1 < ET:
                            q_part(i + 1)
                        qk_part(2 * i)
                        qk_part(2 * i + 1)
                        for s in early_step(i):
                            step(s)
                    for s in range(EARLY, STEPS):
                        step(s)

                    def o_part(i):
                        if i >= 2:
                            wait(pe, o_lo, g, ET, i - 1)
                        out = ps_s[i % 2][:, 0:GTOK]
                        for h in range(2):
                            head = slice((2 * i + h) * QLEN, (2 * i + h + 1) * QLEN)
                            for d in range(DT):
                                mm = three_pass(pe, out, W["wv_hi"][:, d, i, h * DK:h * DK + P],
                                                W["wv_lo"][:, d, i, h * DK:h * DK + P],
                                                qk_hi[:, d, :, head], qk_lo[:, d, :, head],
                                                h == 0 and d == 0, h == 1 and d == DT - 1)
                        mm.then_inc(o_done, 1)

                    def y_part(i):
                        wait(pe, o_lo, g, ET, i + 1)
                        for tt in range(2):
                            cols = slice(tt * P, (tt + 1) * P)
                            mm = three_pass(pe, ps_x[:, tt, :], e_hi[i % 3][:, cols], e_lo[i % 3][:, cols],
                                            W["wo_hi"][:, i, :], W["wo_lo"][:, i, :],
                                            i == 0 and tt == 0, i == ET - 1 and tt == 1, skip_group_check=True)
                        mm.then_inc(wo_done, 1)

                    wait(pe, z_lo, g, DT * NB, DT * NB)
                    o_part(0)
                    for i in range(ET):
                        if i + 1 < ET:
                            o_part(i + 1)
                        y_part(i)

                groups(pe, body)


CHUNKS = GROUPS
CT = TT // CHUNKS
CTOK = CT * P
CB = CTOK // QLEN
FF = 4 * D
FT = FF // P
PAD = QLEN + 1
RUN = 2 * CB * PAD
LOW = -1e38
CROSS_AT = 2
R_WEIGHTS = ("rr", "rk", "rv", "ro", "rg")


def recurrence(nc, A, W, dram):
    with ExitStack() as ctx:
        def sb(name, shape, dt=F32):
            return ctx.enter_context(nc.sbuf_tensor(name, shape, dt))

        def sem(name):
            return ctx.enter_context(nc.semaphore(name))

        def bank(name):
            return ctx.enter_context(nc.psum_tensor(name, [P, 512], F32))

        w_hi = {n: sb(n + "_hi", [P, DT, D], F32R) for n in R_WEIGHTS}
        w_lo = {n: sb(n + "_lo", [P, DT, D], F32R) for n in R_WEIGHTS}
        w_hi["fk"], w_lo["fk"] = sb("fk_hi", [P, DT, FF], F32R), sb("fk_lo", [P, DT, FF], F32R)
        w_hi["fv"], w_lo["fv"] = sb("fv_hi", [P, FT, D], F32R), sb("fv_lo", [P, FT, D], F32R)
        names = R_WEIGHTS + ("fk", "fv")
        ln_cols = sb("ln_cols", [P, 4, DT])
        decay_u = sb("decay_u", [P, 2 * DT])
        w_col = sb("w_col", [P, DT])
        w_run = sb("w_run", [P, DT, 2 * CB, PAD])
        gateT = sb("gateT", [P, DT, 8])
        gate_b = sb("gate_b", [P, 8])
        power = sb("r_power", [P, CT])

        zero_rows = sb("zero_rows", [P, 2 * D])
        x_in = sb("x_chunk", [P, CT, D])
        y_in = sb("y_chunk", [P, CT, D])
        n0 = sb("n0", [P, CT, D])
        n1 = sb("n1", [P, CT, D])
        z = sb("z", [P, CT, D])
        n2 = sb("n2", [P, CT, D])
        n3 = sb("n3", [P, CT, D])
        stats = sb("r_stats", [P, 4, CT, 6])
        mv = sb("r_mv", [P, 4, CT, 2])
        veps = sb("r_veps", [P, 4, CT])
        rstd = sb("r_rstd", [P, 4, CT])
        nT, nT_hi, nT_lo = ({st: sb(f"{n}_{st}", [P, DT, CTOK], dt) for st in "AB"}
                            for n, dt in (("nT", F32), ("nT_hi", F32R), ("nT_lo", F32R)))
        hT = sb("hT", [P, DT, CTOK])
        gate_r = sb("gate_r", [P, DT, CTOK])
        k_run, v_run, p_run, f1_run, f2_run, fv_run, a_run, b_run = (
            sb(n + "_run", [P, DT, 2 * CB, PAD]) for n in ("k", "v", "p", "f1", "f2", "fv", "a", "b"))
        pairs = [sb(f"pair{i}", [P, 2, DT, 2 * CB, QLEN]) for i in range(2)]
        e1, e2, t1, t2 = (pairs[i][:, j] for i in range(2) for j in range(2))
        raw = [pairs[i][:, :, :, :, :].rearrange("p a b c d -> p (a b c d)") for i in range(2)]
        rw, both, crossing = (sb(n, [P, DT, CTOK]) for n in ("rw", "both", "crossing"))
        rw_hi = sb("rw_hi", [P, DT, CTOK], F32R)
        rw_lo = sb("rw_lo", [P, DT, CTOK], F32R)
        relu = [sb(f"relu{i}", [P, 2 * CTOK]) for i in range(2)]
        sq = [sb(f"sq{i}", [P, 2 * CTOK]) for i in range(2)]
        kk_hi = sb("kk_hi", [P, FT, CTOK], F32R)
        kk_lo = sb("kk_lo", [P, FT, CTOK], F32R)
        sg = sb("sg", [P, CT, D])
        ps_t = {st: bank("ps_rt" + st) for st in "AB"}
        ps_m = [bank(f"ps_m{i}") for i in range(4)]
        ps_y = bank("ps_fv")
        ps_g = bank("ps_gate")

        passed = {n: sem("r_passed_" + n) for n in ("dve", "pool")}
        zeroed = sem("zeroed")
        w_in = [sem("rw_in0"), sem("rw_in1")]
        wr_hi, wr_lo = sem("wr_hi"), sem("wr_lo")
        small_in = sem("small_in")
        w_ready = sem("w_ready")
        pads = sem("pads")
        chunk_in = sem("chunk_in")
        x1_done = sem("x1_done")
        kv_copied = sem("kv_copied")
        r_gated = sem("r_gated")
        scanned, args_done, exps_done, fv_done = (sem("wkv_" + n) for n in ("scanned", "args", "exps", "fv"))
        den_done, e2v_done, num_done, wkv_done = sem("den_done"), sem("e2v_done"), sem("num_done"), sem("wkv_done")
        crossed, rw_hi_done, rw_lo_done = sem("crossed"), sem("rw_hi_done"), sem("rw_lo_done")
        z_added = sem("z_added")
        x1z_done = sem("x1z_done")
        relu_done, sq_done, kk_hi_done, kk_lo_done = (sem(n) for n in ("relu_done", "sq_done", "kk_hi_done", "kk_lo_done"))
        sg_done = sem("sg_done")
        y_done = sem("ff_done")
        gated = sem("ff_gated")
        x2_done = sem("x2_done")
        h_kept = sem("h_kept")
        hT_done, h_copied = sem("hT_done"), sem("h_copied")
        lg_done, lg_copied = sem("lg_done"), sem("lg_copied")
        ln_stats, ln_mv, ln_veps, ln_rstd, ln_done, t_done, t_full, t_hi, t_lo = (
            {st: sem(f"r{n}_{st}") for st in "AB"}
            for n in ("ln_stats", "ln_mv", "ln_veps", "ln_rstd", "ln_done", "t_done", "t_full", "t_hi", "t_lo"))
        mA_done, mB_done = sem("mA_done"), sem("mB_done")

        sizes = {n: DT * D for n in R_WEIGHTS} | {"fk": DT * FF, "fv": FT * D}

        def flat(ap):
            return ap.rearrange("p a b -> p (a b)")

        def directions(v):
            return v[:, :, 0:CB, :], v[:, :, CB:2 * CB, ::-1]

        def by_batch(v):
            return v[:, :, :].rearrange("p d (b t) -> p d b t", t=QLEN)

        def of(st, per, count):
            return (per, count if st == "A" else count - per)

        def chunks(eng, body):
            body(0)
            body(1)
            with eng.Fori(2, CHUNKS - 1) as c:
                body(c)
            body(CHUNKS - 1)
            body(CHUNKS)

        def has(st, c):
            return not isinstance(c, int) or (c < CHUNKS if st == "A" else c >= 1)

        def x_tiles(c, st="A"):
            return bass.ds(c * CT - (0 if st == "A" else CT), CT)

        def x_tile(c, st, t):
            return W["x2"][:, bass.ds(c * CT + t - (0 if st == "A" else CT), 1), :].rearrange("p a d -> p (a d)")

        with nc.Block() as block:
            @block.sync
            def _(sp):
                for src, dst in ((A["decay_u"], decay_u[:, :]), (A["gate_b"].to_broadcast([P, 8]), gate_b[:, :]),
                                 (A["ln_cols"], flat(ln_cols[:, :, :])), (A["gateT"].rearrange("(t p) e -> p t e", p=P), gateT[:, :, :])):
                    sp.dma_start(dst, src).then_inc(small_in, 16)
                for j, n in enumerate(names):
                    if j >= 2:
                        sp.wait_ge(wr_lo, j - 1)
                    src = A[n].rearrange("(t p) e -> p t e", p=P)
                    dst = raw[j % 2][:, 0:sizes[n]].rearrange("p (t e) -> p t e", t=src.shape[1])
                    sp.dma_start(dst, src).then_inc(w_in[j % 2], 16)
                sp.wait_ge(pads, 7)
                for n in range(SLOTS // (2 * P)):
                    sp.dma_start(dram["slots"][2 * P * n:2 * P * (n + 1), :].rearrange("(p r) d -> p (r d)", r=2),
                                 zero_rows[:, :]).then_inc(zeroed, 16)

                def body(c):
                    wait(sp, x1_done, c, 1, 0)
                    sp.dma_start(x_in[:, :, :], A["x"].rearrange("(c t p) d -> c p t d", p=P, t=CT)[c]).then_inc(chunk_in, 16)
                    sp.dma_start(y_in[:, :, :].rearrange("p t d -> p (t d)"), dram["y"][c]).then_inc(chunk_in, 16)

                turns(sp, CHUNKS, body)
                sp.wait_ge(zeroed, 16 * (SLOTS // (2 * P)))

            @block.gpsimd
            def _(pool):
                pool.memset(power[:, :], -0.5).then_inc(pads, 1)
                pool.memset(k_run[:, :, :, 0:1], LOW).then_inc(pads, 1)
                for run in (v_run, f1_run, f2_run, fv_run):
                    pool.memset(run[:, :, :, 0:1], 0.0).then_inc(pads, 1)
                pool.memset(zero_rows[:, :], 0.0).then_inc(pads, 1)
                pool.wait_ge(pads, 1)

                def x1(c):
                    pool.tensor_tensor(W["x2"][:, x_tiles(c), :], x_in[:, :, :], y_in[:, :, :], ALU.add).then_inc(x1_done, 1)

                def body(c):
                    def root(st, n):
                        i = 2 * "AB".index(st) + n
                        wait(pool, ln_veps[st], c, *of(st, 2, n + 1))
                        pool.tensor_tensor(rstd[:, i, :], veps[:, i, :], power[:, :], ALU.pow).then_inc(ln_rstd[st], 1)

                    def rest_of_pair(i):
                        wait(pool, kk_hi_done, c, *of("B", FT // 2, i + 1))
                        pair = slice(2 * i, 2 * i + 2)
                        pool.tensor_tensor(flat(kk_lo[:, pair, :]), sq[i % 2][:, :], f(flat(kk_hi[:, pair, :])),
                                           ALU.subtract).then_inc(kk_lo_done, 1)

                    if has("A", c):
                        root("A", 0)
                    if has("B", c):
                        root("B", 0)
                    if has("A", c):
                        root("A", 1)
                        if not (isinstance(c, int) and c == CHUNKS - 1):
                            wait_alone(pool, chunk_in, c, 32, 64, passed["pool"])
                            x1(c + 1)
                        wait(pool, exps_done, c, 3, 1)
                        pool.tensor_tensor(fv_run[:, :, :, 1:PAD], f2_run[:, :, :, 1:PAD], v_run[:, :, :, 1:PAD],
                                           ALU.mult).then_inc(fv_done, 1)
                        if has("B", c):
                            rest_of_pair(0)
                        wait(pool, exps_done, c, 3, 3)
                        pool.tensor_tensor(t2, e2, v_run[:, :, :, 1:PAD], ALU.mult).then_inc(e2v_done, 1)
                    def cross():
                        num, den = directions(e1), directions(t1)
                        wait(pool, den_done, c, 4, 2)
                        wait(pool, num_done, c, 3, 2)
                        pool.tensor_tensor(by_batch(rw), num[0], den[1], ALU.mult).then_inc(crossed, 1)
                        pool.tensor_tensor(by_batch(crossing), num[1], den[0], ALU.mult).then_inc(crossed, 1)

                    if has("A", c) and not has("B", c):
                        cross()
                    if has("B", c):
                        if not has("A", c):
                            rest_of_pair(0)
                        for i in range(1, FT // 2):
                            if i == CROSS_AT and has("A", c):
                                cross()
                            rest_of_pair(i)
                        root("B", 1)
                    if has("A", c):
                        wait_alone(pool, z_added, c, 1, 1, passed["pool"])
                        pool.tensor_tensor(W["x2"][:, x_tiles(c), :], W["x2"][:, x_tiles(c), :], z[:, :, :],
                                           ALU.add).then_inc(x1z_done, 1)

                pool.wait_ge(chunk_in, 32)
                x1(0)
                chunks(pool, body)

            @block.vector
            def _(dve):
                dve.wait_ge(w_ready, 1)
                dve.tensor_scalar(w_col[:, :], w_col[:, :], -1.0, None, ALU.mult).then_inc(w_ready, 1)
                dve.memset(w_run[:, :, :, :], 0.0).then_inc(w_ready, 1)
                dve.wait_ge(w_ready, 3)
                for d in range(DT):
                    dve.tensor_scalar(w_run[:, d], w_run[:, d], w_col[:, d:d + 1], None, ALU.add).then_inc(w_ready, 1)
                dve.wait_ge(w_ready, 5)
                dve.memset(w_run[:, :, :, 0:1], LOW).then_inc(w_ready, 1)
                dve.wait_ge(w_ready, 6)
                for j, n in enumerate(names):
                    dve.wait_ge(wr_hi, j + 1)
                    dve.tensor_tensor(flat(w_lo[n][:, :, :]), raw[j % 2][:, 0:sizes[n]], f(flat(w_hi[n][:, :, :])),
                                      ALU.subtract).then_inc(wr_lo, 1)
                dve.wait_ge(wr_lo, len(names))
                dve.wait_ge(small_in, 16 * 4)
                dve.wait_ge(pads, 6)

                def body(c):
                    def moments(st, n, src):
                        i = 2 * "AB".index(st) + n
                        for t in range(CT):
                            dve.bn_stats(stats[:, i, t, :], src(t)).then_inc(ln_stats[st], 1)
                        for t in range(CT):
                            wait_alone(dve, ln_stats[st], c, *of(st, 2 * CT, n * CT + t + 1), passed["dve"])
                            dve.bn_aggr(mv[:, i, t, :], stats[:, i, t, :]).then_inc(ln_mv[st], 1)
                        wait(dve, ln_mv[st], c, *of(st, 2 * CT, (n + 1) * CT))
                        dve.tensor_scalar(veps[:, i, :], mv[:, i, :, 1], EPS, None, ALU.add).then_inc(ln_veps[st], 1)

                    def normalise(st, n, src, dst):
                        i = 2 * "AB".index(st) + n
                        wait(dve, ln_rstd[st], c, *of(st, 2, n + 1))
                        for t in range(CT):
                            dve.tensor_scalar(dst(t), src(t), mv[:, i, t, 0:1], rstd[:, i, t:t + 1],
                                              ALU.subtract, ALU.mult).then_inc(ln_done[st], 1)

                    def rest_of_input(st):
                        wait(dve, t_hi[st], c, *of(st, DT, DT))
                        dve.tensor_tensor(nT_lo[st][:, :, :], nT[st][:, :, :], f(nT_hi[st][:, :, :]), ALU.subtract).then_inc(t_lo[st], 1)

                    steps, before = slice(1, PAD), slice(0, QLEN)

                    def whole(run):
                        return run[:, :, :, :].rearrange("p a b c -> p (a b c)")

                    def exponents():
                        wait(dve, kv_copied, c, 4, 2)
                        dve.tensor_tensor_scan(whole(p_run), whole(w_run), whole(k_run), 0.0, ALU.add, ALU.max).then_inc(scanned, 1)
                        wait(dve, scanned, c, 3, 1)
                        dve.tensor_tensor(f2_run[:, :, :, steps], k_run[:, :, :, steps], p_run[:, :, :, steps],
                                          ALU.subtract).then_inc(args_done, 1)
                        for d in range(DT):
                            dve.scalar_tensor_tensor(f1_run[:, d, :, steps], p_run[:, d, :, before], w_col[:, d:d + 1],
                                                     p_run[:, d, :, steps], ALU.add, ALU.subtract).then_inc(args_done, 1)
                        for d in range(DT):
                            dve.scalar_tensor_tensor(t1[:, d], k_run[:, d, :, steps], decay_u[:, DT + d:DT + d + 1],
                                                     p_run[:, d, :, before], ALU.add, ALU.subtract).then_inc(args_done, 1)
                        wait(dve, args_done, c, 7, 5)
                        dve.tensor_scalar(e1, t1, -1.0, 0.0, ALU.mult, ALU.min).then_inc(args_done, 1)
                        dve.tensor_scalar(e2, t1, 0.0, None, ALU.min).then_inc(args_done, 1)

                    def time_mixing():
                        wait(dve, exps_done, c, 3, 2)
                        dve.tensor_tensor_scan(whole(b_run), whole(f1_run), whole(f2_run), 0.0, ALU.mult, ALU.add).then_inc(scanned, 1)
                        wait(dve, fv_done, c, 1, 1)
                        dve.tensor_tensor_scan(whole(a_run), whole(f1_run), whole(fv_run), 0.0, ALU.mult, ALU.add).then_inc(scanned, 1)
                        wait(dve, exps_done, c, 3, 3)
                        wait(dve, scanned, c, 3, 2)
                        dve.tensor_tensor(t1, e1, b_run[:, :, :, before], ALU.mult).then_inc(den_done, 1)
                        wait(dve, scanned, c, 3, 3)
                        dve.tensor_tensor(e1, e1, a_run[:, :, :, before], ALU.mult).then_inc(num_done, 1)
                        wait(dve, den_done, c, 4, 1)
                        dve.tensor_tensor(t1, t1, e2, ALU.add).then_inc(den_done, 1)
                        wait(dve, num_done, c, 3, 1)
                        wait(dve, e2v_done, c, 1, 1)
                        dve.tensor_tensor(e1, e1, t2, ALU.add).then_inc(num_done, 1)
                        den = directions(t1)
                        wait(dve, den_done, c, 4, 2)
                        dve.tensor_tensor(by_batch(both), den[0], den[1], ALU.mult).then_inc(den_done, 1)
                        wait(dve, den_done, c, 4, 3)
                        dve.reciprocal(both[:, :, :], both[:, :, :]).then_inc(den_done, 1)
                        wait(dve, crossed, c, 2, 2)
                        dve.tensor_tensor(rw[:, :, :], rw[:, :, :], crossing[:, :, :], ALU.add).then_inc(num_done, 1)
                        wait(dve, den_done, c, 4, 4)
                        wait(dve, r_gated, c, 1, 1)
                        dve.scalar_tensor_tensor(both[:, :, :], both[:, :, :], 0.5, gate_r[:, :, :], ALU.mult, ALU.mult).then_inc(wkv_done, 1)
                        wait(dve, num_done, c, 3, 3)
                        wait(dve, wkv_done, c, 2, 1)
                        dve.tensor_tensor(rw[:, :, :], rw[:, :, :], both[:, :, :], ALU.mult).then_inc(wkv_done, 1)

                    if has("A", c):
                        wait_alone(dve, x1_done, c, 1, 1, passed["dve"])
                        moments("A", 0, lambda t: x_tile(c, "A", t))
                    if has("B", c):
                        wait(dve, z_added, c, 1, 0)
                        moments("B", 0, lambda t: z[:, t, :])
                    if has("A", c):
                        normalise("A", 0, lambda t: x_tile(c, "A", t), lambda t: n0[:, t, :])
                        wait(dve, ln_done["A"], c, 2 * CT, CT)
                        moments("A", 1, lambda t: n0[:, t, :])
                    if has("B", c):
                        normalise("B", 0, lambda t: z[:, t, :], lambda t: n2[:, t, :])
                    if has("A", c):
                        normalise("A", 1, lambda t: n0[:, t, :], lambda t: n1[:, t, :])
                    if has("B", c):
                        wait(dve, t_done["B"], c, *of("B", 1, 1))
                        for d in range(DT):
                            dve.tensor_scalar(nT["B"][:, d, :], ps_t["B"][:, d * CTOK:(d + 1) * CTOK], ln_cols[:, 2, d:d + 1],
                                              ln_cols[:, 3, d:d + 1], ALU.mult, ALU.add).then_inc(t_full["B"], 1)
                    if has("A", c):
                        for d in range(DT):
                            wait(dve, t_full["A"], c, DT, d + 1)
                            dve.tensor_copy(nT_hi["A"][:, d, :], nT["A"][:, d, :]).then_inc(t_hi["A"], 1)
                        rest_of_input("A")
                    if has("B", c):
                        wait(dve, t_full["B"], c, *of("B", DT, DT))
                        rest_of_input("B")
                    if has("A", c):
                        exponents()
                        time_mixing()
                        wait(dve, wkv_done, c, 2, 2)
                        dve.tensor_copy(rw_hi[:, :, :], rw[:, :, :]).then_inc(rw_hi_done, 1)
                        wait(dve, rw_hi_done, c, 1, 1)
                        dve.tensor_tensor(rw_lo[:, :, :], rw[:, :, :], f(rw_hi[:, :, :]), ALU.subtract).then_inc(rw_lo_done, 1)
                    if has("B", c):
                        wait(dve, sg_done, c, *of("B", 1, 1))
                        wait(dve, y_done, c, *of("B", 1, 1))
                        dve.tensor_tensor(flat(sg[:, :, :]), flat(sg[:, :, :]), ps_y[:, :], ALU.mult).then_inc(gated, 1)
                        wait(dve, x1z_done, c, *of("B", 1, 1))
                        wait(dve, gated, c, *of("B", 1, 1))
                        dve.tensor_tensor(W["x2"][:, x_tiles(c, "B"), :], W["x2"][:, x_tiles(c, "B"), :], sg[:, :, :],
                                          ALU.add).then_inc(x2_done, 1)
                        wait_alone(dve, x2_done, c, *of("B", 1, 1), passed["dve"])
                        moments("B", 1, lambda t: x_tile(c, "B", t))
                    if has("A", c):
                        wait(dve, mA_done, c, 4, 4)
                        dve.tensor_tensor(flat(z[:, :, :]), flat(n0[:, :, :]), ps_m[0][:, :], ALU.add).then_inc(z_added, 1)
                    if has("B", c):
                        wait(dve, h_kept, c, *of("B", 1, 0))
                        normalise("B", 1, lambda t: x_tile(c, "B", t), lambda t: n3[:, t, :])

                chunks(dve, body)
                dve.wait_ge(lg_copied, CHUNKS)
                dve.tensor_tensor(W["logits"][:, :, :], W["logits"][:, :, :], gate_b[:, :].unsqueeze(1).to_broadcast([P, TT, 8]),
                                  ALU.add).then_inc(lg_copied, 1)

            @block.scalar
            def _(act):
                act.wait_ge(small_in, 16 * 4)
                act.activation(w_col[:, :], decay_u[:, 0:DT], ACT.Exp).then_inc(w_ready, 1)
                for j, n in enumerate(names):
                    act.wait_ge(w_in[j % 2], 16 * (j // 2 + 1))
                    act.activation(flat(w_hi[n][:, :, :]), raw[j % 2][:, 0:sizes[n]], ACT.Copy).then_inc(wr_hi, 1)

                def body(c):
                    def weight_and_bias():
                        wait(act, t_done["A"], c, 1, 1)
                        for d in range(DT):
                            act.activation(nT["A"][:, d, :], ps_t["A"][:, d * CTOK:(d + 1) * CTOK], ACT.Identity,
                                           bias=ln_cols[:, 1, d:d + 1], scale=ln_cols[:, 0, d:d + 1]).then_inc(t_full["A"], 1)

                    def rounded_input():
                        for d in range(DT):
                            wait(act, t_full["B"], c, *of("B", DT, d + 1))
                            act.activation(nT_hi["B"][:, d, :], nT["B"][:, d, :], ACT.Copy).then_inc(t_hi["B"], 1)

                    def exponential(tile, need):
                        wait(act, args_done, c, 7, need)
                        act.activation(tile, tile, ACT.Exp).then_inc(exps_done, 1)

                    def hidden_pair(i):
                        wait(act, mB_done, c, *of("B", 5, 2 + i))
                        act.activation(relu[i % 2][:, :], ps_m[i][:, :], ACT.Relu).then_inc(relu_done, 1)
                        wait(act, relu_done, c, *of("B", FT // 2, i + 1))
                        if i >= 2:
                            wait(act, kk_lo_done, c, *of("B", FT // 2, i - 1))
                        act.activation(sq[i % 2][:, :], relu[i % 2][:, :], ACT.Square).then_inc(sq_done, 1)
                        wait(act, sq_done, c, *of("B", FT // 2, i + 1))
                        act.activation(flat(kk_hi[:, 2 * i:2 * i + 2, :]), sq[i % 2][:, :], ACT.Copy).then_inc(kk_hi_done, 1)

                    if has("A", c):
                        weight_and_bias()
                    if has("B", c):
                        rounded_input()
                    if has("A", c):
                        for j, run in enumerate((k_run, v_run)):
                            wait(act, mA_done, c, 4, j + 1)
                            src = ps_m[j][:, :].rearrange("p (d b t) -> p d b t", d=DT, t=QLEN)
                            act.activation(run[:, :, 0:CB, 1:PAD], src, ACT.Copy).then_inc(kv_copied, 1)
                            act.activation(run[:, :, CB:2 * CB, QLEN:0:-1], src, ACT.Copy).then_inc(kv_copied, 1)
                        exponential(f2_run[:, :, :, 1:PAD], 1)
                        exponential(f1_run[:, :, :, 1:PAD], 3)
                    if has("B", c):
                        hidden_pair(0)
                    if has("A", c):
                        exponential(pairs[0][:, :, :, :, :], 7)
                        wait(act, mA_done, c, 4, 3)
                        act.activation(flat(gate_r[:, :, :]), ps_m[2][:, :], ACT.Sigmoid).then_inc(r_gated, 1)
                    if has("B", c):
                        wait(act, mB_done, c, *of("B", 5, 1))
                        wait(act, x2_done, c, *of("B", 1, 0))
                        act.activation(flat(sg[:, :, :]), ps_m[3][:, :], ACT.Sigmoid).then_inc(sg_done, 1)
                        for i in range(1, FT // 2):
                            hidden_pair(i)
                    if has("B", c):
                        wait(act, hT_done, c, *of("B", 1, 1))
                        act.activation(flat(hT[:, :, :]), ps_t["B"][:, :], ACT.Copy).then_inc(h_copied, 1)
                        act.activation(W["h"][:, x_tiles(c, "B"), :], n3[:, :, :], ACT.Copy).then_inc(h_kept, 1)
                        wait(act, lg_done, c, *of("B", 1, 1))
                        act.activation(W["logits"][:, x_tiles(c, "B"), :], ps_g[:, 0:CT * 8].rearrange("p (t e) -> p t e", e=8),
                                       ACT.Copy).then_inc(lg_copied, 1)

                chunks(act, body)

            @block.tensor
            def _(pe):
                pe.wait_ge(wr_lo, len(names))

                def body(c):
                    def transpose(st, n_in, done):
                        for d in range(DT):
                            for t in range(CT):
                                mm = pe.transpose(ps_t[st][:, d * CTOK + t * P:d * CTOK + (t + 1) * P],
                                                  n_in[:, t, d * P:(d + 1) * P], W["ident"][:, :])
                        mm.then_inc(done, 1)

                    def channels(st, bank, n, col, done):
                        for j in range(2):
                            for d in range(DT):
                                cols = slice((col + j) * P, (col + j + 1) * P)
                                mm = three_pass(pe, ps_m[bank][:, j * CTOK:(j + 1) * CTOK], w_hi[n][:, d, cols], w_lo[n][:, d, cols],
                                                nT_hi[st][:, d, :], nT_lo[st][:, d, :], d == 0, d == DT - 1)
                        mm.then_inc(done, 1)

                    def keys():
                        def passes(w, m, first, last):
                            for j in range(2):
                                for d in range(DT):
                                    mm = pe.matmul(ps_m[0][:, j * CTOK:(j + 1) * CTOK], w[:, d, j * P:(j + 1) * P], m[:, d, :],
                                                   start=first and j == 0 and d == 0, stop=last and j == 1 and d == DT - 1,
                                                   skip_group_check=True)
                            return mm

                        wait(pe, t_hi["A"], c, DT, DT)
                        passes(w_hi["rk"], nT_hi["A"], True, False)
                        passes(w_lo["rk"], nT_hi["A"], False, False)
                        wait(pe, t_lo["A"], c, 1, 1)
                        passes(w_hi["rk"], nT_lo["A"], False, True).then_inc(mA_done, 1)

                    def tokens(out, n, hi, lo, done):
                        for t in range(CT):
                            cols = slice(t * P, (t + 1) * P)
                            for d in range(DT):
                                mm = three_pass(pe, out[:, t * D:(t + 1) * D], hi[:, d, cols], lo[:, d, cols],
                                                w_hi[n][:, d, :], w_lo[n][:, d, :], d == 0, d == DT - 1)
                        mm.then_inc(done, 1)

                    if has("B", c):
                        wait(pe, ln_done["B"], c, *of("B", 2 * CT, CT))
                        wait(pe, h_copied, c, *of("B", 1, 0))
                        transpose("B", n2, t_done["B"])
                    if has("A", c):
                        wait(pe, ln_done["A"], c, 2 * CT, 2 * CT)
                        wait(pe, t_lo["A"], c, 1, 0)
                        transpose("A", n1, t_done["A"])
                    if has("A", c):
                        wait(pe, z_added, c, 1, 0)
                        keys()
                        wait(pe, relu_done, c, *of("B", FT // 2, 0))
                        channels("A", 1, "rv", 0, mA_done)
                        channels("A", 2, "rr", 0, mA_done)
                    if has("B", c):
                        wait(pe, t_lo["B"], c, *of("B", 1, 1))
                        wait(pe, relu_done, c, *of("B", FT // 2, 0))
                        tokens(ps_m[3], "rg", nT_hi["B"], nT_lo["B"], mB_done)
                        for i in range(FT // 2):
                            if i == 3:
                                wait(pe, sg_done, c, *of("B", 1, 1))
                            elif has("A", c):
                                wait(pe, *((kv_copied, c, 4, 2), (kv_copied, c, 4, 4), (r_gated, c, 1, 1))[i])
                            channels("B", i, "fk", 2 * i, mB_done)
                        wait(pe, gated, c, *of("B", 1, 0))
                        for d in range(FT):
                            if d % 2 == 0:
                                wait(pe, kk_lo_done, c, *of("B", FT // 2, d // 2 + 1))
                            for t in range(CT):
                                cols = slice(t * P, (t + 1) * P)
                                mm = three_pass(pe, ps_y[:, t * D:(t + 1) * D], kk_hi[:, d, cols], kk_lo[:, d, cols],
                                                w_hi["fv"][:, d, :], w_lo["fv"][:, d, :], d == 0 and t == 0,
                                                d == FT - 1 and t == CT - 1, skip_group_check=True)
                        mm.then_inc(y_done, 1)
                    if has("A", c):
                        wait(pe, rw_lo_done, c, 1, 1)
                        if has("B", c):
                            wait(pe, relu_done, c, *of("B", FT // 2, 1))
                        else:
                            wait(pe, kv_copied, c, 4, 2)
                        tokens(ps_m[0], "ro", rw_hi, rw_lo, mA_done)
                    if has("B", c):
                        wait(pe, ln_done["B"], c, *of("B", 2 * CT, 2 * CT))
                        transpose("B", n3, hT_done)
                        wait(pe, h_copied, c, *of("B", 1, 1))
                        wait(pe, lg_copied, c, *of("B", 1, 0))
                        for t in range(CT):
                            for d in range(DT):
                                mm = pe.matmul(ps_g[:, t * 8:(t + 1) * 8], hT[:, d, t * P:(t + 1) * P], gateT[:, d, :],
                                               start=(d == 0), stop=(d == DT - 1))
                        mm.then_inc(lg_done, 1)

                chunks(pe, body)


EXPERTS = 8
CAP = -(-TOKENS * 5 // (4 * EXPERTS))
SLOTS = EXPERTS * CAP
HF = 4 * D
HFT = HF // P
QUARTERS = 4
SPLIT = [(0, P), (P, P), (2 * P, CAP - 2 * P)]


def experts(nc, A, W, dram, out):
    with ExitStack() as ctx:
        def sb(name, shape, dt=F32):
            return ctx.enter_context(nc.sbuf_tensor(name, shape, dt))

        def sem(name):
            return ctx.enter_context(nc.semaphore(name))

        def bank(name):
            return ctx.enter_context(nc.psum_tensor(name, [P, 512], F32))

        x2, h, logits = W["x2"], W["h"], W["logits"]
        tri = sb("tri", [P, P])
        ones = sb("ones", [P, P])
        e_iota = sb("e_iota", [P, EXPERTS])
        e_int = sb("e_int", [P, EXPERTS], mybir.dt.int32)
        tok = sb("tok", [P, TT])
        tok_int = sb("tok_int", [P, TT], mybir.dt.int32)
        zeros = sb("zeros16", [P, TT])
        m, total, rec, top, idx, pos, keep, slot, far, tw = (
            sb("gt_" + n, [P, TT]) for n in ("m", "total", "rec", "top", "idx", "pos", "keep", "slot", "far", "tw"))
        prob, eq, hot, tot, run, pre = (sb("gt_" + n, [P, TT, EXPERTS]) for n in ("prob", "eq", "hot", "tot", "run", "pre"))
        scatter_to = sb("scatter_to", [P, TT], U32)
        gather_from = sb("gather_from", [P, TT], U32)

        raw1 = [sb(f"raw1_{i}", [P, DT * HF]) for i in range(2)]
        raw2 = [sb(f"raw2_{i}", [P, HFT * D]) for i in range(2)]
        w1_hi, w1_lo = ([sb(f"w1_{p}{i}", [P, DT, HF], F32R) for i in range(2)] for p in ("hi", "lo"))
        w2_hi, w2_lo = ([sb(f"w2_{p}{i}", [P, HFT, D], F32R) for i in range(2)] for p in ("hi", "lo"))
        b1 = sb("b1", [P, EXPERTS, HFT])
        b2 = sb("b2", [P, EXPERTS, D])
        rows = [sb(f"rows{i}", [P, 3, D]) for i in range(2)]
        rT_hi = sb("rT_hi", [P, DT, CAP], F32R)
        rT_lo = sb("rT_lo", [P, DT, CAP], F32R)
        hid = [sb(f"hid{i}", [P, CAP]) for i in range(2)]
        hid_hi = sb("hid_hi", [P, HFT, CAP], F32R)
        hid_lo = sb("hid_lo", [P, HFT, CAP], F32R)
        eo = [sb(f"eo{i}", [P, 3, D]) for i in range(2)]

        ps_t = [bank("ps_et0"), bank("ps_et1")]
        ps_h = [bank(f"ps_h{i}") for i in range(3)]
        ps_y = [bank("ps_ey0"), bank("ps_ey1")]
        ps_c = bank("ps_count")

        masks = sem("masks")
        consts = sem("consts")
        b_in = sem("b_in")
        g_step = sem("gate_step")
        g_exp = sem("gate_exp")
        counted = sem("counted")
        slots_ready = sem("slots_ready")
        scattered = sem("scattered")
        w_in = [sem("ew_in0"), sem("ew_in1")]
        w_hi_done, w_lo_done = sem("ew_hi"), sem("ew_lo")
        rows_in = [sem("rows_in0"), sem("rows_in1")]
        t_done, t_hi, t_lo = sem("et_done"), sem("et_hi"), sem("et_lo")
        h_done, h_relu, h_hi, h_lo = sem("eh_done"), sem("eh_relu"), sem("eh_hi"), sem("eh_lo")
        y_done, y_copied = sem("ey_done"), sem("ey_copied")
        eo_stored = [sem("eo_stored0"), sem("eo_stored1")]
        gathered = [sem(f"gathered{q}") for q in range(QUARTERS)]
        summed = sem("summed")
        stored = sem("out_stored")

        PAIRS = EXPERTS // 2
        QT = TT // QUARTERS

        def pairs(eng, body):
            body(0)
            with eng.Fori(1, PAIRS - 1) as j:
                body(j)
            body(PAIRS - 1)

        def exists(j, n):
            return not (isinstance(j, int) and 2 * j + n >= EXPERTS)

        def flat(ap):
            return ap.rearrange("p a b -> p (a b)")

        with nc.Block() as block:
            @block.sync
            def _(sp):
                sp.dma_start(b1[:, :, :], A["b1"]).then_inc(b_in, 16)
                sp.dma_start(flat(b2[:, :, :]), A["b2"].to_broadcast([P, EXPERTS * D])).then_inc(b_in, 16)

                def load_weights(e, i):
                    sp.dma_start(raw1[i][:, :].rearrange("p (t n) -> p t n", t=DT),
                                 A["w1"].rearrange("e (t p) n -> e p t n", p=P)[e]).then_inc(w_in[i], 16)
                    sp.dma_start(raw2[i][:, :].rearrange("p (t n) -> p t n", t=HFT),
                                 A["w2"].rearrange("e (t p) n -> e p t n", p=P)[e]).then_inc(w_in[i], 16)

                def load_rows(e, i):
                    slots = dram["slots"][0:SLOTS, :].rearrange("(e s) d -> e s d", s=CAP)[e]
                    sp.dma_start(rows[i][:, 0:2, :], slots[0:2 * P, :].rearrange("(k p) d -> p k d", p=P)).then_inc(rows_in[i], 16)
                    sp.dma_start(rows[i][0:CAP - 2 * P, 2, :], slots[2 * P:CAP, :]).then_inc(rows_in[i], 16)

                def body(j):
                    for i in range(2):
                        if exists(j, i + 1):
                            wait(sp, t_done, j, 4, 2 * i)
                            load_rows(2 * j + i + 1, (i + 1) % 2)
                        if exists(j, i + 2):
                            wait(sp, w_lo_done, j, 4, 2 * i + 2)
                            load_weights(2 * j + i + 2, i)

                load_weights(0, 0)
                load_weights(1, 1)
                sp.wait_ge(scattered, 16 * TT)
                load_rows(0, 0)
                pairs(sp, body)

            @block.gpsimd
            def _(pool):
                pool.memset(ones[:, :], 1.0).then_inc(masks, 1)
                pool.memset(zeros[:, :], 0.0).then_inc(masks, 1)
                pool.iota(e_int[:, :], [[1, EXPERTS]], base=0, channel_multiplier=0).then_inc(masks, 1)
                pool.iota(tok_int[:, :], [[P, TT]], base=0, channel_multiplier=1).then_inc(masks, 1)
                pool.wait_ge(masks, 4)
                pool.affine_select(out=tri[:, :], in_=ones[:, :], compare_op=ALU.is_ge, fill=0.0, base=0,
                                   pattern=[[1, P]], channel_multiplier=-1).then_inc(masks, 1)
                pool.tensor_copy(e_iota[:, :], e_int[:, :]).then_inc(consts, 1)
                pool.tensor_copy(tok[:, :], tok_int[:, :]).then_inc(consts, 1)
                pool.wait_ge(slots_ready, 2)
                for t in range(TT):
                    pool.indirect_dma_start(out=dram["slots"], out_offset=bass.IndirectOffsetOnAxis(scatter_to[:, t:t + 1], 0),
                                            in_=h[:, t, :], in_offset=None).then_inc(scattered, 16)

                def body(j):
                    for i in range(2):
                        if exists(j, i + 1):
                            n = (i + 1) % 2
                            for k, (raw, hi, lo) in enumerate(((raw1, w1_hi, w1_lo), (raw2, w2_hi, w2_lo))):
                                wait(pool, w_hi_done, j, 4, 2 * i + k + 3)
                                pool.tensor_tensor(flat(lo[n][:, :, :]), raw[n][:, :], f(flat(hi[n][:, :, :])),
                                                   ALU.subtract).then_inc(w_lo_done, 1)

                pool.wait_ge(w_lo_done, 2)
                pairs(pool, body)
                for i in range(2):
                    pool.wait_ge(eo_stored[i], 32 * PAIRS)
                for t in range(TT):
                    pool.indirect_dma_start(out=h[:, t, :], out_offset=None, in_=dram["results"],
                                            in_offset=bass.IndirectOffsetOnAxis(gather_from[:, t:t + 1], 0)).then_inc(gathered[t // QT], 16)

            @block.vector
            def _(dve):
                done = 0

                def step(op):
                    nonlocal done
                    op.then_inc(g_step, 1)
                    done += 1
                    dve.wait_ge(g_step, done)

                def over(v):
                    return v[:, :].unsqueeze(2).to_broadcast([P, TT, EXPERTS])

                iota = e_iota[:, :].unsqueeze(1).to_broadcast([P, TT, EXPERTS])
                dve.wait_ge(consts, 2)
                step(dve.tensor_reduce(m[:, :], logits[:, :, :], AX_X, ALU.max))
                step(dve.tensor_tensor(prob[:, :, :], logits[:, :, :], over(m), ALU.subtract))
                dve.wait_ge(g_exp, 1)
                step(dve.tensor_reduce(total[:, :], prob[:, :, :], AX_X, ALU.add))
                step(dve.reciprocal(rec[:, :], total[:, :]))
                step(dve.tensor_tensor(prob[:, :, :], prob[:, :, :], over(rec), ALU.mult))
                step(dve.tensor_reduce(top[:, :], prob[:, :, :], AX_X, ALU.max))
                step(dve.tensor_tensor(eq[:, :, :], prob[:, :, :], over(top), ALU.is_equal))
                step(dve.tensor_scalar(eq[:, :, :], eq[:, :, :], -float(EXPERTS), float(EXPERTS), ALU.mult, ALU.add))
                step(dve.tensor_tensor(eq[:, :, :], eq[:, :, :], iota, ALU.add))
                step(dve.tensor_reduce(idx[:, :], eq[:, :, :], AX_X, ALU.min))
                step(dve.tensor_tensor(hot[:, :, :], iota, over(idx), ALU.is_equal))
                dve.wait_ge(counted, 2)
                step(dve.tensor_copy(tot[:, :, :], ps_c[:, P:2 * P].rearrange("p (t e) -> p t e", e=EXPERTS)))
                for e in range(EXPERTS):
                    dve.tensor_tensor_scan(run[:, :, e], tot[:, :, e], zeros[:, :], 0.0, ALU.add, ALU.add).then_inc(g_step, 1)
                done += EXPERTS
                dve.wait_ge(g_step, done)
                step(dve.tensor_tensor(run[:, :, :], run[:, :, :], tot[:, :, :], ALU.subtract))
                step(dve.tensor_tensor(pre[:, :, :], run[:, :, :], ps_c[:, 0:P].rearrange("p (t e) -> p t e", e=EXPERTS), ALU.add))
                step(dve.tensor_tensor(pre[:, :, :], pre[:, :, :], hot[:, :, :], ALU.mult))
                step(dve.tensor_reduce(pos[:, :], pre[:, :, :], AX_X, ALU.add))
                step(dve.tensor_scalar(pos[:, :], pos[:, :], 1.0, None, ALU.subtract))
                step(dve.tensor_scalar(keep[:, :], pos[:, :], float(CAP), None, ALU.is_lt))
                step(dve.tensor_tensor(tw[:, :], top[:, :], keep[:, :], ALU.mult))
                step(dve.tensor_tensor(pos[:, :], pos[:, :], keep[:, :], ALU.mult))
                step(dve.tensor_scalar(slot[:, :], idx[:, :], float(CAP), None, ALU.mult))
                step(dve.tensor_tensor(slot[:, :], slot[:, :], pos[:, :], ALU.add))
                dve.tensor_copy(gather_from[:, :], slot[:, :]).then_inc(slots_ready, 1)
                step(dve.tensor_scalar(far[:, :], tok[:, :], float(SLOTS), None, ALU.add))
                step(dve.tensor_tensor(slot[:, :], slot[:, :], far[:, :], ALU.subtract))
                step(dve.tensor_tensor(slot[:, :], slot[:, :], keep[:, :], ALU.mult))
                step(dve.tensor_tensor(slot[:, :], slot[:, :], far[:, :], ALU.add))
                dve.tensor_copy(scatter_to[:, :], slot[:, :]).then_inc(slots_ready, 1)

                for k, (raw, hi, lo) in enumerate(((raw1, w1_hi, w1_lo), (raw2, w2_hi, w2_lo))):
                    dve.wait_ge(w_hi_done, k + 1)
                    dve.tensor_tensor(flat(lo[0][:, :, :]), raw[0][:, :], f(flat(hi[0][:, :, :])), ALU.subtract).then_inc(w_lo_done, 1)

                def rest_of_rows(j, n):
                    for d in range(DT):
                        wait(dve, t_hi, j, 4, 2 * n + d + 1)
                        dve.tensor_tensor(rT_lo[:, d, :], ps_t[d][:, 0:CAP], f(rT_hi[:, d, :]), ALU.subtract).then_inc(t_lo, 1)

                def body(j):
                    for i in range(2):
                        for k in range(HFT):
                            wait(dve, h_relu, j, 2 * HFT, HFT * i + k + 1)
                            dve.tensor_copy(hid_hi[:, k, :], hid[k % 2][:, :]).then_inc(h_hi, 1)
                            wait(dve, h_hi, j, 2 * HFT, HFT * i + k + 1)
                            dve.tensor_tensor(hid_lo[:, k, :], hid[k % 2][:, :], f(hid_hi[:, k, :]), ALU.subtract).then_inc(h_lo, 1)
                        if exists(j, i + 1):
                            rest_of_rows(j, i + 1)
                        wait(dve, eo_stored[i], j, 32, 0)
                        bias = b2[:, bass.ds(2 * j + i, 1), :].rearrange("p a d -> p (a d)")
                        for k in range(3):
                            wait(dve, y_done, j, 6, 3 * i + (2, 2, 3)[k])
                            r = slice(0, P) if k < 2 else slice(3 * P - CAP, P)
                            dve.tensor_tensor(eo[i][r, k, :], ps_y[k // 2][r, (k % 2) * D:(k % 2 + 1) * D], bias[r, :],
                                              ALU.add).then_inc(y_copied, 1)

                dve.wait_ge(b_in, 32)
                rest_of_rows(0, 0)
                pairs(dve, body)
                for t in range(TT):
                    dve.wait_ge(gathered[t // QT], 16 * QT)
                    dve.scalar_tensor_tensor(x2[:, t, :], h[:, t, :], tw[:, t:t + 1], x2[:, t, :], ALU.mult, ALU.add).then_inc(summed, 1)

            @block.scalar
            def _(act):
                act.wait_ge(g_step, 2)
                act.activation(prob[:, :, :], prob[:, :, :], ACT.Exp).then_inc(g_exp, 1)
                act.wait_ge(b_in, 32)

                def round_weights(j, n, k):
                    i = n % 2
                    if k == 0:
                        wait(act, w_in[i], j, 32, 32 * (n // 2 + 1))
                    wait(act, y_done, j, 6, 3 * (n - 1))
                    raw, hi = ((raw1, w1_hi), (raw2, w2_hi))[k]
                    act.activation(flat(hi[i][:, :, :]), raw[i][:, :], ACT.Copy).then_inc(w_hi_done, 1)

                def round_rows(j, n):
                    for d in range(DT):
                        wait(act, t_done, j, 4, 2 * n + d + 1)
                        act.activation(rT_hi[:, d, :], ps_t[d][:, 0:CAP], ACT.Copy).then_inc(t_hi, 1)

                def body(j):
                    for i in range(2):
                        for k in range(HFT):
                            wait(act, h_done, j, 2 * HFT, HFT * i + k + 1)
                            if k >= 2:
                                wait(act, h_lo, j, 2 * HFT, HFT * i + k - 1)
                            act.activation(hid[k % 2][:, :], ps_h[k % 3][:, 0:CAP], ACT.Relu,
                                           bias=b1[:, bass.ds(2 * j + i, 1), k]).then_inc(h_relu, 1)
                        if exists(j, i + 1):
                            round_weights(j, i + 1, 0)
                            round_rows(j, i + 1)
                            round_weights(j, i + 1, 1)
                        e = 2 * j + i
                        wait(act, y_copied, j, 6, 3 * i + 3)
                        slots = dram["results"].rearrange("(e s) d -> e s d", s=CAP)[e]
                        act.dma_start(slots[0:2 * P, :].rearrange("(k p) d -> p k d", p=P), eo[i][:, 0:2, :]).then_inc(eo_stored[i], 16)
                        act.dma_start(slots[2 * P:CAP, :], eo[i][3 * P - CAP:P, 2, :]).then_inc(eo_stored[i], 16)

                round_weights(0, 0, 0)
                round_weights(0, 0, 1)
                round_rows(0, 0)
                pairs(act, body)
                for q in range(QUARTERS):
                    act.wait_ge(summed, QT * (q + 1))
                    act.dma_start(out.rearrange("(t p) d -> p t d", p=P)[:, q * QT:(q + 1) * QT, :],
                                  x2[:, q * QT:(q + 1) * QT, :]).then_inc(stored, 16)
                act.wait_ge(stored, 16 * QUARTERS)

            @block.tensor
            def _(pe):
                pe.wait_ge(masks, 5)
                pe.wait_ge(g_step, 11)
                hot_flat = flat(hot[:, :, :])
                pe.matmul(ps_c[:, 0:P], tri[:, :], hot_flat, start=True, stop=True).then_inc(counted, 1)
                pe.matmul(ps_c[:, P:2 * P], ones[:, :], hot_flat, start=True, stop=True).then_inc(counted, 1)

                def transpose_rows(j, n):
                    i = n % 2
                    wait(pe, rows_in[i], j, 32, 32 * (n // 2 + 1))
                    wait(pe, t_lo, j, 4, 2 * n)
                    for d in range(DT):
                        for k, (at, size) in enumerate(SPLIT):
                            mm = pe.transpose(ps_t[d][:, at:at + size], rows[i][0:size, k, d * P:(d + 1) * P], W["ident"][0:size, 0:size])
                        mm.then_inc(t_done, 1)

                def body(j):
                    for i in range(2):
                        wait(pe, w_lo_done, j, 4, 2 * i + 1)
                        wait(pe, t_lo, j, 4, 2 * i + 2)
                        for k in range(HFT):
                            if k >= 3:
                                wait(pe, h_relu, j, 2 * HFT, HFT * i + k - 2)
                            for d in range(DT):
                                cols = slice(k * P, (k + 1) * P)
                                mm = three_pass(pe, ps_h[k % 3][:, 0:CAP], w1_hi[i][:, d, cols], w1_lo[i][:, d, cols],
                                                rT_hi[:, d, :], rT_lo[:, d, :], d == 0, d == DT - 1)
                            mm.then_inc(h_done, 1)
                        if exists(j, i + 1):
                            transpose_rows(j, i + 1)
                        wait(pe, w_lo_done, j, 4, 2 * i + 2)
                        wait(pe, y_copied, j, 6, 3 * i)
                        for k, at in enumerate((0, P, CAP - P)):
                            for t in range(HFT):
                                if k == 0:
                                    wait(pe, h_lo, j, 2 * HFT, HFT * i + t + 1)
                                mm = three_pass(pe, ps_y[k // 2][:, (k % 2) * D:(k % 2 + 1) * D], hid_hi[:, t, at:at + P],
                                                hid_lo[:, t, at:at + P], w2_hi[i][:, t, :], w2_lo[i][:, t, :], t == 0, t == HFT - 1)
                            mm.then_inc(y_done, 1)

                transpose_rows(0, 0)
                pairs(pe, body)


def perceiver_layer(nc, A, out):
    dram = {n: nc.dram_tensor(n + "_scratch", [GROUPS, P, DT * GTOK], F32, kind="Internal").ap()
            for n in ("xT_hi", "xT_lo")}
    dram["y"] = nc.dram_tensor("y_scratch", [GROUPS, P, 2 * D], F32, kind="Internal").ap()
    dram["slots"] = nc.dram_tensor("slots_scratch", [SLOTS + TOKENS, D], F32, kind="Internal").ap()
    dram["results"] = nc.dram_tensor("results_scratch", [SLOTS, D], F32, kind="Internal").ap()
    with ExitStack() as ctx:
        def sb(name, shape, dt=F32):
            return ctx.enter_context(nc.sbuf_tensor(name, shape, dt))

        W = {"ident": sb("ident", [P, P])}
        with ExitStack() as inner:
            for part in ("hi", "lo"):
                for n, shape in (("wq", [P, DT, E]), ("wk", [P, ET, D]), ("wv", [P, DT, ET, 3 * DK]), ("wo", [P, ET, D])):
                    W[f"{n}_{part}"] = inner.enter_context(nc.sbuf_tensor(f"{n}_{part}", shape, F32R))
            for n, cols in (("bq", ET), ("bv", ET), ("cmap", TT * 4 * HT)):
                W[n] = inner.enter_context(nc.sbuf_tensor(n + "_col", [P, cols], F32))
            prepare(nc, A, W, dram)
            attention(nc, A, W, dram)
        W["x2"] = sb("x2", [P, TT, D])
        W["h"] = sb("h", [P, TT, D])
        W["logits"] = sb("logits", [P, TT, 8])
        recurrence(nc, A, W, dram)
        experts(nc, A, W, dram, out)


def columns(v):
    return v.reshape(-1, P).T


def layouts(i):
    import numpy as np
    c = i["ctx_1024"]
    full = c[:, :KC * P, :].reshape(BATCH, KC, P, D)
    return {k: np.ascontiguousarray(v) for k, v in {
        "x": i["x"].reshape(TOKENS, D),
        "wq_nat": i["L0_xattn_Wq"],
        "wqT": i["L0_xattn_Wq"].T,
        "wk": i["L0_xattn_Wk"],
        "wvT": i["L0_xattn_Wv"].T,
        "woT": i["L0_xattn_Wo"].T,
        "bq": columns(i["L0_xattn_bq"]), "bk": columns(i["L0_xattn_bk"]), "bv": columns(i["L0_xattn_bv"]),
        "ctxT": c.reshape(BATCH, KEYS, DT, P).transpose(0, 3, 2, 1),
        "ctxN": full.transpose(0, 2, 1, 3),
        "ctxL": c[:, KC * P:, :],
        "rr": i["L0_attn_Wr"].T, "rk": i["L0_attn_Wk"].T, "rv": i["L0_attn_Wv"].T, "ro": i["L0_attn_Wo"].T,
        "rg": i["L0_attn_Wfr"].T, "fk": i["L0_attn_Wfk"].T, "fv": i["L0_attn_Wfv"].T,
        "ln_cols": np.concatenate([columns(i["L0_attn_" + n]) for n in ("ln1_w", "ln1_b", "ln2_w", "ln2_b")], 1),
        "decay_u": np.concatenate([columns(i["L0_attn_decay"]), columns(i["L0_attn_u"])], 1),
        "w1": i["L0_ffn_w1"], "w2": i["L0_ffn_w2"],
        "b1": i["L0_ffn_b1"].reshape(EXPERTS, HFT, P).transpose(2, 0, 1),
        "b2": i["L0_ffn_b2"].reshape(1, -1),
        "gateT": i["L0_ffn_gate_w"].T, "gate_b": i["L0_ffn_gate_b"][None],
    }.items()}


def kernel(**inputs):
    import numpy as np
    import concourse.bacc as bacc
    from concourse.bass_utils import run_bass_kernel_spmd

    arrays = layouts({k: np.asarray(v) for k, v in inputs.items()})
    nc = bacc.Bacc("TRN2", target_bir_lowering=False, num_devices=1, dynamic_dma_scratch_size=4096)
    A = {k: nc.dram_tensor("in_" + k, v.shape, mybir.dt.from_np(v.dtype), kind="ExternalInput").ap() for k, v in arrays.items()}
    out = nc.dram_tensor("out", (TOKENS, D), F32, kind="ExternalOutput").ap()
    perceiver_layer(nc, A, out)
    r = run_bass_kernel_spmd(nc, [{"in_" + k: v for k, v in arrays.items()}], core_ids=[0])
    return r.results[0]["out"].reshape(BATCH, QLEN, D)
```
